# Optimizing a Trainium2 kernel written in Bass

```python
import numpy as np
import jax
import jax.numpy as jnp

def _softmax(x, axis=-1):
    return jax.nn.softmax(x, axis=axis)

def _gelu(x):
    return jax.nn.gelu(x, approximate=True)

def _silu(x):
    return jax.nn.silu(x)

def _sigmoid(x):
    return jax.nn.sigmoid(x)

def _layernorm(x, axis=-1, eps=1e-05):
    m = jnp.mean(x, axis=axis, keepdims=True)
    v = jnp.var(x, axis=axis, keepdims=True)
    return (x - m) / jnp.sqrt(v + eps)

def _scatter_add(tgt, idx, src, axis=0):
    return tgt.at[idx].add(src)

def _segment_sum(src, seg, n):
    return jax.ops.segment_sum(src, seg, n)
kernel_name = 'mk_xattn_seq_d2_seqx_r4_90d7a9'

def setup_inputs(seed: int=0):
    np.random.seed(seed)
    _w = jnp.asarray

    def _rec_inputs():
        import jax
        import jax.numpy as jnp
        _rk = jax.random.key(seed)
        x = -0.0002928 + 1 * jax.random.normal(jax.random.fold_in(_rk, 1), (4, 512, 256), jnp.float32)
        _lenS = 512 - jax.random.randint(jax.random.fold_in(_rk, 7), (4,), 0, max(1, 512 // 4) + 1, jnp.int32)
        _lenS2 = 64 - jax.random.randint(jax.random.fold_in(_rk, 8), (4,), 0, max(1, 64 // 4) + 1, jnp.int32)
        _ctx_768P = jax.random.normal(jax.random.fold_in(_rk, 11), (4, 16, 192), jnp.float32)
        _ctx_768c = jax.random.dirichlet(jax.random.fold_in(_rk, 511), 0.3 * jnp.ones((16,), jnp.float32), (4, 64))
        _ctx_768t = jnp.einsum('bsk,bkd->bsd', _ctx_768c, _ctx_768P)
        _ctx_768t = _ctx_768t * jax.lax.rsqrt(jnp.mean(jnp.square(_ctx_768t)) + 1e-12) * 0.953939
        ctx_768 = 2.09791e-05 + 1.00001 * (_ctx_768t + 0.3 * jax.random.normal(jax.random.fold_in(_rk, 611), (4, 64, 192), jnp.float32))
        return (x, ctx_768)
    x, ctx_768 = _rec_inputs()

    def _L0_xattn_setup():
        import jax, jax.numpy as jnp
        import numpy as np
        DIM1, DIM2, H = (256, 192, 16)
        HID = 4 * DIM1
        EPS = 1e-05

        def layernorm(x, w, b):
            mu = jnp.mean(x, axis=-1, keepdims=True)
            var = jnp.mean((x - mu) ** 2, axis=-1, keepdims=True)
            return (x - mu) * jax.lax.rsqrt(var + EPS) * w + b
        key = jax.random.key(seed)
        ks = jax.random.split(key, 12)
        s1 = 1.0 / np.sqrt(DIM1)
        s2 = 1.0 / np.sqrt(DIM2)
        sh = 1.0 / np.sqrt(HID)
        return {'x': jax.random.normal(ks[0], (4, 256, DIM1), jnp.float32), 'y': jax.random.normal(ks[1], (4, 256, DIM2), jnp.float32), 'ln1_w': jnp.ones((DIM1,), jnp.float32), 'ln1_b': jnp.zeros((DIM1,), jnp.float32), 'ln2_w': jnp.ones((DIM2,), jnp.float32), 'ln2_b': jnp.zeros((DIM2,), jnp.float32), 'ln3_w': jnp.ones((DIM1,), jnp.float32), 'ln3_b': jnp.zeros((DIM1,), jnp.float32), 'Wq': jax.random.uniform(ks[2], (DIM1, DIM1), jnp.float32, -s1, s1), 'Wkv': jax.random.uniform(ks[3], (DIM2, 2 * DIM1), jnp.float32, -s2, s2), 'Wproj': jax.random.uniform(ks[4], (DIM1, DIM1), jnp.float32, -s1, s1), 'bproj': jnp.zeros((DIM1,), jnp.float32), 'W1': jax.random.uniform(ks[5], (DIM1, HID), jnp.float32, -s1, s1), 'b1': jnp.zeros((HID,), jnp.float32), 'W2': jax.random.uniform(ks[6], (HID, DIM1), jnp.float32, -sh, sh), 'b2': jnp.zeros((DIM1,), jnp.float32)}
    _L0_xattn_all = _L0_xattn_setup()
    _L0_xattn_in = {k: v for k, v in _L0_xattn_all.items() if k in ('ln1_w', 'ln1_b', 'ln2_w', 'ln2_b', 'ln3_w', 'ln3_b', 'Wq', 'Wkv', 'Wproj', 'bproj', 'W1', 'b1', 'W2', 'b2')}
    del _L0_xattn_all

    def _L1_xattn_setup():
        import jax, jax.numpy as jnp
        import numpy as np
        B, N, D, H, M, CD = (2, 512, 256, 16, 77, 192)
        DH = D // H
        FF = 4 * D
        NBITS = 8
        EPS = 1e-05

        def fake_quant_w(w, n_bits=NBITS):
            levels = 2 ** n_bits - 1
            mn = jnp.min(w)
            mx = jnp.max(w)
            delta = (mx - mn) / levels
            zp = jnp.round(-mn / delta)
            wq = jnp.clip(jnp.round(w / delta) + zp, 0, levels)
            wdq = (wq - zp) * delta
            return w + jax.lax.stop_gradient(wdq - w)

        def layernorm(x, g, b):
            mu = jnp.mean(x, axis=-1, keepdims=True)
            var = jnp.mean((x - mu) ** 2, axis=-1, keepdims=True)
            return (x - mu) * jax.lax.rsqrt(var + EPS) * g + b

        def linear(x, w, b=None):
            y = x @ fake_quant_w(w).T
            return y if b is None else y + b

        def cross_attn(x, ctx, qw, kw, vw, ow, ob):
            Bq, Nq, _ = x.shape
            Nk = ctx.shape[1]
            q = linear(x, qw).reshape(Bq, Nq, H, DH)
            k = linear(ctx, kw).reshape(Bq, Nk, H, DH)
            v = linear(ctx, vw).reshape(Bq, Nk, H, DH)
            scale = DH ** (-0.5)
            sim = jnp.einsum('bihd,bjhd->bhij', q, k) * scale
            attn = jax.nn.softmax(sim, axis=-1)
            out = jnp.einsum('bhij,bjhd->bihd', attn, v).reshape(Bq, Nq, D)
            return linear(out, ow, ob)

        def geglu_ff(x, w1, b1, w2, b2):
            h = linear(x, w1, b1)
            hidden, gate = jnp.split(h, 2, axis=-1)
            return linear(hidden * jax.nn.gelu(gate), w2, b2)
        key = jax.random.key(seed)
        ks = jax.random.split(key, 24)
        W = lambda k, o, i: jax.random.normal(k, (o, i), jnp.float32) * 0.02
        return {'x': jax.random.normal(ks[0], (B, N, D), jnp.float32), 'context': jax.random.normal(ks[1], (B, M, CD), jnp.float32), 'ln1_g': 1.0 + 0.1 * jax.random.normal(ks[2], (D,), jnp.float32), 'ln1_b': 0.1 * jax.random.normal(ks[3], (D,), jnp.float32), 'ln2_g': 1.0 + 0.1 * jax.random.normal(ks[4], (D,), jnp.float32), 'ln2_b': 0.1 * jax.random.normal(ks[5], (D,), jnp.float32), 'ln3_g': 1.0 + 0.1 * jax.random.normal(ks[6], (D,), jnp.float32), 'ln3_b': 0.1 * jax.random.normal(ks[7], (D,), jnp.float32), 'q1_w': W(ks[8], D, D), 'k1_w': W(ks[9], D, D), 'v1_w': W(ks[10], D, D), 'o1_w': W(ks[11], D, D), 'o1_b': jnp.zeros((D,), jnp.float32), 'q2_w': W(ks[12], D, D), 'k2_w': W(ks[13], D, CD), 'v2_w': W(ks[14], D, CD), 'o2_w': W(ks[15], D, D), 'o2_b': jnp.zeros((D,), jnp.float32), 'ff1_w': W(ks[16], 2 * FF, D), 'ff1_b': jnp.zeros((2 * FF,), jnp.float32), 'ff2_w': W(ks[17], D, FF), 'ff2_b': jnp.zeros((D,), jnp.float32)}
    _L1_xattn_all = _L1_xattn_setup()
    _L1_xattn_in = {k: v for k, v in _L1_xattn_all.items() if k in ('ln1_g', 'ln1_b', 'ln2_g', 'ln2_b', 'ln3_g', 'ln3_b', 'q1_w', 'k1_w', 'v1_w', 'o1_w', 'o1_b', 'q2_w', 'k2_w', 'v2_w', 'o2_w', 'o2_b', 'ff1_w', 'ff1_b', 'ff2_w', 'ff2_b')}
    del _L1_xattn_all
    return {'x': x, 'ctx_768': ctx_768, 'L0_xattn_ln1_w': _L0_xattn_in['ln1_w'], 'L0_xattn_ln1_b': _L0_xattn_in['ln1_b'], 'L0_xattn_ln2_w': _L0_xattn_in['ln2_w'], 'L0_xattn_ln2_b': _L0_xattn_in['ln2_b'], 'L0_xattn_ln3_w': _L0_xattn_in['ln3_w'], 'L0_xattn_ln3_b': _L0_xattn_in['ln3_b'], 'L0_xattn_Wq': _L0_xattn_in['Wq'], 'L0_xattn_Wkv': _L0_xattn_in['Wkv'], 'L0_xattn_Wproj': _L0_xattn_in['Wproj'], 'L0_xattn_bproj': _L0_xattn_in['bproj'], 'L0_xattn_W1': _L0_xattn_in['W1'], 'L0_xattn_b1': _L0_xattn_in['b1'], 'L0_xattn_W2': _L0_xattn_in['W2'], 'L0_xattn_b2': _L0_xattn_in['b2'], 'L1_xattn_ln1_g': _L1_xattn_in['ln1_g'], 'L1_xattn_ln1_b': _L1_xattn_in['ln1_b'], 'L1_xattn_ln2_g': _L1_xattn_in['ln2_g'], 'L1_xattn_ln2_b': _L1_xattn_in['ln2_b'], 'L1_xattn_ln3_g': _L1_xattn_in['ln3_g'], 'L1_xattn_ln3_b': _L1_xattn_in['ln3_b'], 'L1_xattn_q1_w': _L1_xattn_in['q1_w'], 'L1_xattn_k1_w': _L1_xattn_in['k1_w'], 'L1_xattn_v1_w': _L1_xattn_in['v1_w'], 'L1_xattn_o1_w': _L1_xattn_in['o1_w'], 'L1_xattn_o1_b': _L1_xattn_in['o1_b'], 'L1_xattn_q2_w': _L1_xattn_in['q2_w'], 'L1_xattn_k2_w': _L1_xattn_in['k2_w'], 'L1_xattn_v2_w': _L1_xattn_in['v2_w'], 'L1_xattn_o2_w': _L1_xattn_in['o2_w'], 'L1_xattn_o2_b': _L1_xattn_in['o2_b'], 'L1_xattn_ff1_w': _L1_xattn_in['ff1_w'], 'L1_xattn_ff1_b': _L1_xattn_in['ff1_b'], 'L1_xattn_ff2_w': _L1_xattn_in['ff2_w'], 'L1_xattn_ff2_b': _L1_xattn_in['ff2_b']}

def reference(x, ctx_768, L0_xattn_ln1_w, L0_xattn_ln1_b, L0_xattn_ln2_w, L0_xattn_ln2_b, L0_xattn_ln3_w, L0_xattn_ln3_b, L0_xattn_Wq, L0_xattn_Wkv, L0_xattn_Wproj, L0_xattn_bproj, L0_xattn_W1, L0_xattn_b1, L0_xattn_W2, L0_xattn_b2, L1_xattn_ln1_g, L1_xattn_ln1_b, L1_xattn_ln2_g, L1_xattn_ln2_b, L1_xattn_ln3_g, L1_xattn_ln3_b, L1_xattn_q1_w, L1_xattn_k1_w, L1_xattn_v1_w, L1_xattn_o1_w, L1_xattn_o1_b, L1_xattn_q2_w, L1_xattn_k2_w, L1_xattn_v2_w, L1_xattn_o2_w, L1_xattn_o2_b, L1_xattn_ff1_w, L1_xattn_ff1_b, L1_xattn_ff2_w, L1_xattn_ff2_b):
    import jax
    import jax.numpy as jnp

    def _L0_xattn_ref(x, y, ln1_w, ln1_b, ln2_w, ln2_b, ln3_w, ln3_b, Wq, Wkv, Wproj, bproj, W1, b1, W2, b2):
        import jax, jax.numpy as jnp
        import numpy as np
        DIM1, DIM2, H = (256, 192, 16)
        HID = 4 * DIM1
        EPS = 1e-05

        def layernorm(x, w, b):
            mu = jnp.mean(x, axis=-1, keepdims=True)
            var = jnp.mean((x - mu) ** 2, axis=-1, keepdims=True)
            return (x - mu) * jax.lax.rsqrt(var + EPS) * w + b
        B, N1, C1 = x.shape
        hd = C1 // H
        scale = hd ** (-0.5)
        xn = layernorm(x, ln1_w, ln1_b)
        yn = layernorm(y, ln2_w, ln2_b)
        q = (xn @ Wq).reshape(B, N1, H, hd).transpose(0, 2, 1, 3)
        kv = (yn @ Wkv).reshape(B, y.shape[1], 2, H, hd)
        k = kv[:, :, 0].transpose(0, 2, 1, 3)
        v = kv[:, :, 1].transpose(0, 2, 1, 3)
        attn = jax.nn.softmax(jnp.einsum('bhqd,bhkd->bhqk', q, k) * scale, axis=-1)
        o = jnp.einsum('bhqk,bhkd->bhqd', attn, v).transpose(0, 2, 1, 3).reshape(B, N1, C1)
        x = x + (o @ Wproj + bproj)
        h = jax.nn.gelu(layernorm(x, ln3_w, ln3_b) @ W1 + b1, approximate=False)
        x = x + (h @ W2 + b2)
        return x

    def _L1_xattn_ref(x, context, ln1_g, ln1_b, ln2_g, ln2_b, ln3_g, ln3_b, q1_w, k1_w, v1_w, o1_w, o1_b, q2_w, k2_w, v2_w, o2_w, o2_b, ff1_w, ff1_b, ff2_w, ff2_b):
        import jax, jax.numpy as jnp
        import numpy as np
        B, N, D, H, M, CD = (2, 512, 256, 16, 77, 192)
        DH = D // H
        FF = 4 * D
        NBITS = 8
        EPS = 1e-05

        def fake_quant_w(w, n_bits=NBITS):
            levels = 2 ** n_bits - 1
            mn = jnp.min(w)
            mx = jnp.max(w)
            delta = (mx - mn) / levels
            zp = jnp.round(-mn / delta)
            wq = jnp.clip(jnp.round(w / delta) + zp, 0, levels)
            wdq = (wq - zp) * delta
            return w + jax.lax.stop_gradient(wdq - w)

        def layernorm(x, g, b):
            mu = jnp.mean(x, axis=-1, keepdims=True)
            var = jnp.mean((x - mu) ** 2, axis=-1, keepdims=True)
            return (x - mu) * jax.lax.rsqrt(var + EPS) * g + b

        def linear(x, w, b=None):
            y = x @ fake_quant_w(w).T
            return y if b is None else y + b

        def cross_attn(x, ctx, qw, kw, vw, ow, ob):
            Bq, Nq, _ = x.shape
            Nk = ctx.shape[1]
            q = linear(x, qw).reshape(Bq, Nq, H, DH)
            k = linear(ctx, kw).reshape(Bq, Nk, H, DH)
            v = linear(ctx, vw).reshape(Bq, Nk, H, DH)
            scale = DH ** (-0.5)
            sim = jnp.einsum('bihd,bjhd->bhij', q, k) * scale
            attn = jax.nn.softmax(sim, axis=-1)
            out = jnp.einsum('bhij,bjhd->bihd', attn, v).reshape(Bq, Nq, D)
            return linear(out, ow, ob)

        def geglu_ff(x, w1, b1, w2, b2):
            h = linear(x, w1, b1)
            hidden, gate = jnp.split(h, 2, axis=-1)
            return linear(hidden * jax.nn.gelu(gate), w2, b2)
        x = cross_attn(layernorm(x, ln1_g, ln1_b), layernorm(x, ln1_g, ln1_b), q1_w, k1_w, v1_w, o1_w, o1_b) + x
        x = cross_attn(layernorm(x, ln2_g, ln2_b), context, q2_w, k2_w, v2_w, o2_w, o2_b) + x
        x = geglu_ff(layernorm(x, ln3_g, ln3_b), ff1_w, ff1_b, ff2_w, ff2_b) + x
        return x
    x = _L0_xattn_ref(x, ctx_768, L0_xattn_ln1_w, L0_xattn_ln1_b, L0_xattn_ln2_w, L0_xattn_ln2_b, L0_xattn_ln3_w, L0_xattn_ln3_b, L0_xattn_Wq, L0_xattn_Wkv, L0_xattn_Wproj, L0_xattn_bproj, L0_xattn_W1, L0_xattn_b1, L0_xattn_W2, L0_xattn_b2)
    x = _L1_xattn_ref(x, ctx_768, L1_xattn_ln1_g, L1_xattn_ln1_b, L1_xattn_ln2_g, L1_xattn_ln2_b, L1_xattn_ln3_g, L1_xattn_ln3_b, L1_xattn_q1_w, L1_xattn_k1_w, L1_xattn_v1_w, L1_xattn_o1_w, L1_xattn_o1_b, L1_xattn_q2_w, L1_xattn_k2_w, L1_xattn_v2_w, L1_xattn_o2_w, L1_xattn_o2_b, L1_xattn_ff1_w, L1_xattn_ff1_b, L1_xattn_ff2_w, L1_xattn_ff2_b)
    return x

_drawn_inputs = setup_inputs


def setup_inputs(seed=0):
    import zlib

    import numpy as np

    out = dict(_drawn_inputs(seed))
    spreads = {'L0_xattn_ln1_w': (1.0, 0.6),
     'L0_xattn_ln1_b': (0.0, 0.8),
     'L0_xattn_ln2_w': (1.0, 0.563),
     'L0_xattn_ln2_b': (0.0, 0.1),
     'L0_xattn_ln3_w': (1.0, 0.2),
     'L0_xattn_ln3_b': (0.0, 0.371),
     'L0_xattn_bproj': (0.0, 0.1),
     'L0_xattn_b1': (0.0, 0.1),
     'L0_xattn_b2': (0.0, 0.1),
     'L1_xattn_o1_b': (0.0, 0.1),
     'L1_xattn_o2_b': (0.0, 0.1),
     'L1_xattn_ff1_b': (0.0, 0.524),
     'L1_xattn_ff2_b': (0.0, 0.1)}
    factors = {'L1_xattn_ln1_g': 8.0,
     'L1_xattn_ln1_b': 6.419,
     'L1_xattn_ln2_g': 8.0,
     'L1_xattn_ln2_b': 8.0,
     'L1_xattn_ln3_g': 8.0,
     'L1_xattn_ln3_b': 8.0,
     'L1_xattn_q1_w': 8.0,
     'L1_xattn_k1_w': 8.0,
     'L1_xattn_q2_w': 8.0,
     'L1_xattn_k2_w': 8.0}
    for name, (base, spread) in spreads.items():
        noise = np.random.default_rng([zlib.crc32(name.encode()), seed]).standard_normal(out[name].shape)
        drawn = base * np.exp(spread * noise) if base else spread * noise
        out[name] = jnp.asarray(drawn.astype(out[name].dtype))
    for name, factor in factors.items():
        out[name] = (out[name] * factor).astype(out[name].dtype)
    return out
```

```python
from contextlib import ExitStack

import concourse.bass as bass
from concourse import mybir

F32 = mybir.dt.float32
F32R = mybir.dt.float32r
ACT = mybir.ActivationFunctionType
ALU = mybir.AluOpType
AX = mybir.AxisListType

B, R, D, C, NK = 4, 512, 256, 192, 64
H, HD = 16, 16
T, F = R // 128, D // 128
CK = C // 2
HID = 4 * D
M = HID // 128
EPS = 1e-5
SCALE = float(HD) ** -0.5
LEVELS = 255.0
MAGIC = 1.5 * 2.0 ** 23
VW = 32
VS = HD + 1
VN = H * VS + VW - VS

W0 = {"kv": (2, 2 * D), "q": (2, D), "proj": (2, D), "w1": (2, HID), "w2": (M, D)}
W1 = {"q1": (2, D), "k1": (2, D), "v1": (2, D), "o1": (2, D), "k2": (2, D), "v2": (2, D), "q2": (2, D),
      "o2": (2, D), "ff1": (2, 2 * HID), "ff2": (M, D)}
QN = list(W1)


def offsets(widths):
    at, out = 0, {}
    for name, (tiles, n) in widths.items():
        out[name] = at
        at += tiles * n
    return out, at


OFF0, N0 = offsets(W0)
OFF1, N1 = offsets(W1)
VEC = {"a1_g": 2, "a1_b": 2, "a2_g": 2, "a2_b": 2, "a3_g": 2, "a3_b": 2, "b1_g": 2, "b1_b": 2, "b2_g": 2,
       "b2_b": 2, "b3_g": 2, "b3_b": 2, "mlp0_b": M, "ff1_b": 2 * M}
OFFV, NV = {}, 0
for _name, _n in VEC.items():
    OFFV[_name] = NV
    NV += _n
ROWS = ["bproj", "b2", "o1_b", "o2_b", "ff2_b"]
ROW_SLOT = {"bproj": 0, "b2": 1, "o1_b": 2, "o2_b": 0, "ff2_b": 1}
BIAS_AFTER = {"a1": "bproj", "a3": "b2", "b1": "o1_b", "b2": "o2_b", "b3": "ff2_b"}
LN_OF = {"xa": "a1", "sa": "b1", "xb": "b2"}
PROJ = {"xa": "proj", "sa": "o1", "xb": "o2"}


def order():
    first = [("load", 0, 0), ("load", 0, 1)]
    layer0 = ["ctx", "ln:a1", "q:xa", "max:xa:0", "neg:xa:0", "exp:xa+out1:xa", "out2:xa", "out3:xa", "ln:a3",
              "mlp0"]
    layer1 = ["ctx1", "ln:b1", "q:sa", "k:sa", "v:sa", "max:sa:0", "neg:sa:0", "max:sa:1", "neg:sa:1",
              "exp:sa+out1:sa", "out2:sa", "out3:sa", "ln:b2", "q:xb", "max:xb:0", "neg:xb:0", "exp:xb+out1:xb",
              "out2:xb", "out3:xb", "ln:b3", "mlp1"]
    out = list(first)
    quant = [("stats", i) for i in range(len(QN))] + [("scalars", 0)] + [("round", i) for i in range(len(QN))]
    for ph, layer in enumerate((layer0, layer1)):
        if ph == 1:
            out += quant + [("integers", 0), ("load", 1, 0), ("load", 1, 1)]
        for a in (0, 2):
            for st in layer:
                for b in (a, a + 1):
                    for one in st.split("+"):
                        out.append((one, b))
                if ph == 0:
                    if st == "q:xa" and a == 0:
                        out.append(("raw", 0))
                    if st in ("exp:xa+out1:xa", "out3:xa", "ln:a3", "mlp0", "q:xa", "max:xa:0") and \
                            (a or st not in ("q:xa", "max:xa:0")):
                        n = 2
                        out += quant[:n]
                        quant = quant[n:]
            out += [(f"store{ph}", b) for b in (a, a + 1)]
            if a == 0:
                out += [("load", ph, b) for b in (2, 3)]
    return out


ORDER = order()


def heads(group, size):
    pairs = size // 2
    return [(hp, par) for hp in range(group * pairs, group * pairs + pairs) for par in range(2)]


def bank_uses():
    plan, count, turn = {}, [0] * 8, {"long": 0, "short": 0}

    def use(key, kind="short"):
        first, n = (0, 2) if kind == "long" else (2, 6)
        k = first + turn[kind] % n
        turn[kind] += 1
        plan[key] = (k, count[k])
        count[k] += 1

    for st, *args in ORDER:
        b = args[-1]
        name, *rest = st.split(":")
        if name in ("ctx", "ctx1"):
            for x in ("T", "K", "V"):
                use((st, b, x))
        elif name in ("ln", "q", "k", "out2"):
            for f in range(2):
                use((st, b, f))
        elif name in ("v", "out3"):
            for t2 in range(T // 2):
                use((st, b, t2))
        elif name == "max":
            if rest[0] == "sa":
                for hp, par in heads(int(rest[1]), 8):
                    for t in range(T):
                        use((st, b, hp, par, t))
            else:
                for t in range(T):
                    for par in range(2):
                        use((st, b, t, par))
        elif name == "neg":
            use((st, b))
        elif name == "exp":
            for qd in range(4):
                for kt in range(T if rest[0] == "sa" else 1):
                    for j in range(4 if rest[0] == "sa" else 2):
                        use((st, b, qd, kt, j))
                use((st, b, qd, "pv"), "long")
        elif name == "out1":
            for t in range(T):
                use((st, b, t))
        elif name in ("mlp0", "mlp1"):
            for m in range(M):
                use((st, b, m, "h"))
                if name == "mlp1":
                    use((st, b, m, "g"))
            for t2 in range(T // 2):
                use((st, b, t2, "acc"), "long")
    return plan


def prob_units():
    units, at = {}, 0
    for st, *args in ORDER:
        if st.startswith("exp"):
            b = args[-1]
            self_ = st.endswith("sa")
            for qd in range(4):
                for kt in range(T if self_ else 1):
                    n = 4 if self_ else 2
                    last = kt == (T if self_ else 1) - 1
                    units[(st, b, qd, kt)] = (at, n, last)
                    at += n
    return units


def program(nc, x, ctx_in, w0_in, w1_in, vec_in, rows_in, out):
    plan = bank_uses()
    units = prob_units()
    NP = 8
    tile_unit, quad_used, used = {}, {}, 0
    for u, (first, n, last) in units.items():
        for k in range(n):
            tile_unit[first + k] = u
        if not last:
            used += 1
        quad_used[u] = used

    top = [(nc.sbuf_base + 63) // 64 * 64]

    def sb(name, shape, dt, at=None):
        size = 4
        for n in shape[1:]:
            size *= n
        size = (size + 31) // 32 * 32
        if at is None:
            at = top[0]
            top[0] += size
        return nc.alloc_sbuf_tensor_at(name, shape, dt, offset=at), at + size

    def new(name, shape, dt=F32):
        return sb(name, shape, dt)[0]

    xs = [new(f"x{i}", [128, T, D]) for i in range(2)]
    rowz = [new(f"rowz{i}", [128, T, D]) for i in range(2)]
    hiT = [new(f"hiT{i}", [128, F, R], F32R) for i in range(2)]
    loT = [new(f"loT{i}", [128, F, R], F32R) for i in range(2)]
    qk_at = top[0]
    qk_parts = new("qk_parts", [128, 2, 2, R], F32R)
    ctx_z, c_at = sb("ctx_z", [128, C], F32, qk_at)
    ctx_full, c_at = sb("ctx_full", [CK, 2, 128], F32, c_at)
    ctx_hi, c_at = sb("ctx_hi", [CK, 2, 128], F32R, c_at)
    ctx_lo, c_at = sb("ctx_lo", [CK, 2, 128], F32R, c_at)
    q_stack = [new(f"q_stack{i}", [128, H // 2, R], F32R) for i in range(2)]
    o_at = top[0]
    o_raw = new("o_raw", [128, 4, R])
    full_t, _ = sb("full_t", [128, F, R], F32, o_at)
    kc_stack = [new(f"kc_stack{i}", [128, H // 2, 2 * NK], F32R) for i in range(2)]
    vc = [new(f"vc{i}", [128, VN]) for i in range(2)]
    neg_parts = new("neg_parts", [16, 2, R], F32R)
    rows = new("rows", [128, 3, D])
    vec = new("vec", [128, NV])
    ident = new("ident", [128, 128])
    ctx_rows = [new(f"ctx_rows{i}", [128, C]) for i in range(2)]
    kc_parts = new("kc_parts", [128, 2, 2 * NK], F32R)
    six = [new(f"six{i}", [128, T, 6]) for i in range(2)]
    meanvar = [new(f"meanvar{i}", [128, T, 2]) for i in range(2)]
    vareps = new("vareps", [128, T])
    rstd = [new(f"rstd{i}", [128, T]) for i in range(2)]
    half = new("half", [128, T])
    negmax = [new(f"negmax{i}", [128, T, H]) for i in range(2)]
    rsum = new("rsum", [128, H])
    NQ = len(QN)
    ext = new("ext", [128, 2 * NQ])
    allext = new("allext", [128, 2 * NQ])
    qs = new("qs", [128, 8, NQ])
    qhi = new("qhi", [128, NQ], F32R)
    prods = new("prods", [128, 4])
    ffb = new("ffb", [128, M])
    arena = top[0]
    probs, end = sb("probs", [128, NP, R], F32)
    top[0] = end
    hid_parts, at = sb("hid_parts", [128, 2, 2, R], F32R, arena)
    hid, at = sb("hid", [128, 2, R], F32, at)
    gate, at = sb("gate", [128, 2, R], F32, at)
    region = top[0]
    wh, at = sb("wh", [128, N0], F32R, region)
    wl, at = sb("wl", [128, N0], F32R, at)
    raw_at = at
    raw1, _ = sb("raw1", [128, N1], F32, raw_at)
    wn, at1 = sb("wn", [128, N1], F32R, region)
    k_stack, vx = [], []
    for i in range(2):
        t_, at1 = sb(f"k_stack{i}", [128, H // 2, R], F32R, at1)
        k_stack.append(t_)
    for i in range(2):
        t_, at1 = sb(f"vx{i}", [128, T, VN], F32, at1)
        vx.append(t_)
    raw0a, _ = sb("raw0", [128, N0], F32, raw_at)

    scr = {}
    for inst in ("xa", "sa", "xb"):
        for b in range(B):
            scr["q", inst, b] = nc.dram_tensor(f"q_{inst}{b}", (D, 2, R), F32, kind="Internal").ap()
            scr["n", inst, b] = nc.dram_tensor(f"n_{inst}{b}", (H, 2, R), F32, kind="Internal").ap()
            if inst == "sa":
                scr["k", inst, b] = nc.dram_tensor(f"k_{inst}{b}", (D, 2, R), F32, kind="Internal").ap()
            else:
                scr["k", inst, b] = nc.dram_tensor(f"k_{inst}{b}", (D, 2, NK), F32, kind="Internal").ap()
    mid = nc.dram_tensor("mid", (B, R, D), F32, kind="Internal").ap()

    with ExitStack() as stack:
        psum = stack.enter_context(nc.psum_tensor("banks", [128, 8, 512], F32))
        sems = {}

        def S(name):
            if name not in sems:
                sems[name] = stack.enter_context(nc.semaphore(name.replace(":", "_")))
            return sems[name]

        full = [S(f"bank_full{k}") for k in range(8)]
        free = [S(f"bank_free{k}") for k in range(8)]

        def bank(key):
            return psum[:, plan[key][0], :]

        def claim(pe, key):
            k, before = plan[key]
            if before:
                pe.wait_ge(free[k], before)
            return psum[:, k, :]

        def filled(eng, key):
            k, before = plan[key]
            eng.wait_ge(full[k], before + 1)
            return psum[:, k, :]

        def drained(eng, key):
            k, before = plan[key]
            eng.wait_ge(free[k], before + 1)

        def done(key):
            return full[plan[key][0]]

        def release(key):
            return free[plan[key][0]]

        def nth(b, per, j=0):
            return b * per + j + 1

        def weights(name, kt, a, n, rows_=128):
            if name in W0:
                o = OFF0[name] + kt * W0[name][1] + a
                return (wh[0:rows_, o:o + n], wl[0:rows_, o:o + n])
            o = OFF1[name] + kt * W1[name][1] + a
            return (wn[0:rows_, o:o + n],)

        def passes(xp, wp):
            return [(xp[0], wp[0]), (xp[1], wp[0])] + ([(xp[0], wp[1])] if len(wp) == 2 else [])

        def delta(name, parts=128):
            i = QN.index(name)
            return qs[0:parts, 0, i:i + 1]

        def col(name, i, parts=128):
            o = OFFV[name] + i
            return vec[0:parts, o:o + 1]

        def stack_of(inst, b):
            return k_stack[b % 2] if inst == "sa" else kc_stack[b % 2]

        def dma_count(b):
            return b // 2 + 1

        qk_list = [s_ for s_ in ORDER if s_[0][:2] in ("q:", "k:")]
        qk_index = {s_: i for i, s_ in enumerate(qk_list)}
        q_prev, q_seen, neg_index, neg_total, parity = {}, {}, {}, {}, [0, 0]
        for par_ in range(2):
            of_parity = [s_ for s_ in qk_list if s_[0][:2] == "q:" and s_[1] % 2 == par_]
            for i, s_ in enumerate(of_parity):
                q_prev[s_] = of_parity[i - 1] if i else None
                q_seen[s_] = i + 1
        for i, s_ in enumerate([s_ for s_ in ORDER if s_[0].startswith("neg")]):
            neg_index[s_] = i
            parity[s_[1] % 2] += 32
            neg_total[(s_[0].split(":")[1], s_[1])] = parity[s_[1] % 2]
        ln_list = [s_ for s_ in ORDER if s_[0].startswith("ln:")]
        ln_index = {s_: i for i, s_ in enumerate(ln_list)}
        out_index = {s_: i for i, s_ in enumerate(s_ for s_ in ORDER if s_[0].startswith("out1"))}
        q_scaled = {"q:sa": 0, "q:xb": 1}

        def kc_user(n):
            return ("exp:xa", n) if n < B else ("exp:xb", n - B)

        block = stack.enter_context(nc.Block())

        @block.sync
        def _(sp):
            def loaded(dst, src, sem):
                sp.dma_start(dst, src).then_inc(S(sem), 16)

            loaded(vec[:], vec_in, "vectors_loaded")
            n0 = OFF0["q"]
            loaded(raw0a[:, 0:n0], w0_in[:, 0:n0], "raw0_kv_loaded")
            loaded(ctx_rows[0][0:NK, :], ctx_in[0], "ctx_loaded0")
            loaded(ctx_rows[0][NK:128, :], ctx_in[0], "ctx_loaded0")
            loaded(ctx_rows[1][0:NK, :], ctx_in[1], "ctx_loaded1")
            loaded(ctx_rows[1][NK:128, :], ctx_in[1], "ctx_loaded1")

            def load_ctx(b, ph):
                n = ph * B + b - 2
                filled(sp, ("ctx", n, "T") if n < B else ("ctx1", n - B, "T"))
                for half_ in range(2):
                    loaded(ctx_rows[b % 2][half_ * NK:half_ * NK + NK, :], ctx_in[b], f"ctx_loaded{b % 2}")

            def restack(src, dst_rows, sem):
                for par in range(2):
                    for g, part in enumerate(dst_rows[1]):
                        r = 64 * par + HD * g
                        sp.dma_start(dst_rows[0](par, r).bitcast(F32), src[par, part]).then_inc(S(sem), 16)

            q_order = (0, 0, 1)
            k_order = (0, 1, 0)

            for st, *args in ORDER:
                b = args[-1]
                name, *rest = st.split(":")
                if name == "load":
                    ph = args[0]
                    n = ph * B + b
                    if n >= 2:
                        sp.wait_ge(S(f"stored{b % 2}"), 16 * (ph * 2 + b // 2))
                        load_ctx(b, ph)
                    loaded(xs[b % 2][:], (x if ph == 0 else mid)[b].rearrange("(t p) d -> p t d", p=128),
                           f"x_loaded{b % 2}")
                    if n == B:
                        sp.wait_ge(S("a3_biased"), B * T)
                        for i in (3, 4):
                            loaded(rows[:, ROW_SLOT[ROWS[i]], :], rows_in[i:i + 1, :].broadcast_to([128, D]),
                                   "rows_loaded")
                    if n == 1:
                        for w in ("q", "proj", "w1", "w2"):
                            o, m_ = OFF0[w], W0[w][0] * W0[w][1]
                            loaded(raw0a[:, o:o + m_], w0_in[:, o:o + m_], f"raw0_{w}_loaded")
                        for i in (0, 1, 2):
                            loaded(rows[:, i, :], rows_in[i:i + 1, :].broadcast_to([128, D]), "rows_loaded")
                elif name == "raw":
                    sp.wait_ge(S("w0_split"), len(W0))
                    for w in QN:
                        o, m_ = OFF1[w], W1[w][0] * W1[w][1]
                        loaded(raw1[:, o:o + m_], w1_in[:, o:o + m_], f"raw1_{w}_loaded")
                elif name in ("ctx", "ctx1"):
                    inst = "xa" if name == "ctx" else "xb"
                    d = scr["k", inst, b]
                    n = (0 if name == "ctx" else B) + b
                    drained(sp, (st, b, "K"))
                    sp.dma_start(d.rearrange("(m p) q n -> p q m n", p=128),
                                 kc_parts[:].bitcast(F32).rearrange("p q (m n) -> p q m n", m=2)).then_inc(S("kc_sent"), 16)
                    sp.wait_ge(S("kc_sent"), 16 * (n + 1))
                    if n >= 2:
                        filled(sp, (*kc_user(n - 2), 3, "pv"))
                    else:
                        sp.wait_ge(S("kc_set"), 4)
                    src = d.rearrange("(hp par d) q n -> par q d hp n", par=2, d=HD)
                    restack(src, (lambda par, r: kc_stack[b % 2][r:r + HD, :, par * NK:par * NK + NK], k_order),
                            f"kc_stacked{b % 2}")
                elif name in ("q", "k"):
                    inst = rest[0]
                    d = scr[name, inst, b]
                    for m in range(2):
                        drained(sp, (st, b, m))
                        sp.dma_start(d[m * 128:m * 128 + 128], qk_parts[:, m, :, :].bitcast(F32)).then_inc(S(f"qk_sent{m}"), 16)
                    i = qk_index[(st, b)]
                    for m in range(2):
                        sp.wait_ge(S(f"qk_sent{m}"), 16 * (i + 1))
                    src = d.rearrange("(hp par d) q n -> par q d hp n", par=2, d=HD)
                    if name == "q":
                        before = q_prev[(st, b)]
                        if before:
                            filled(sp, (before[0].replace("q:", "exp:"), before[1], 3, "pv"))
                        else:
                            sp.wait_ge(S("pool_set"), 4)
                        restack(src, (lambda par, r: q_stack[b % 2][r:r + HD, :, :], q_order), f"q_stacked{b % 2}")
                    else:
                        if b >= 2:
                            filled(sp, ("exp:sa", b - 2, 3, "pv"))
                        else:
                            sp.wait_ge(S("ones_set"), 4)
                        restack(src, (lambda par, r: k_stack[b % 2][r:r + HD, :, :], k_order), f"k_stacked{b % 2}")
                elif name == "neg":
                    inst, g = rest[0], int(rest[1])
                    n = 8 if inst == "sa" else 16
                    drained(sp, (st, b))
                    d = scr["n", inst, b][g * 8:g * 8 + n]
                    sp.dma_start(d, neg_parts[0:n, :, :].bitcast(F32)).then_inc(S("neg_sent"), 16)
                    sp.wait_ge(S("neg_sent"), 16 * (neg_index[(st, b)] + 1))
                    src = d.rearrange("(par hp) q n -> par q hp n", par=2)
                    for par in range(2):
                        r = 64 * par + 3 * HD
                        sp.dma_start(q_stack[b % 2][r:r + 2, g * 4:g * 4 + n // 2, :].bitcast(F32),
                                     src[par]).then_inc(S(f"neg_stacked{b % 2}"), 16)
                elif name == "store0":
                    for t2 in range(T // 2):
                        drained(sp, ("mlp0", b, t2, "acc"))
                    sp.dma_start(mid[b].rearrange("(t p) d -> p t d", p=128), xs[b % 2][:]).then_inc(
                        S(f"stored{b % 2}"), 16)
                elif name == "store1":
                    for t2 in range(T // 2):
                        drained(sp, ("mlp1", b, t2, "acc"))
                    sp.dma_start(out[b].rearrange("(t p) d -> p t d", p=128), xs[b % 2][:]).then_inc(
                        S(f"stored{b % 2}"), 16)
            for i in range(2):
                sp.wait_ge(S(f"stored{i}"), 16 * 4)

        @block.gpsimd
        def _(pool):
            nc.gpsimd.memset(ident[:], 0.0).then_inc(S("ident_zero"), 1)
            nc.gpsimd.memset(half[:], -0.5).then_inc(S("ident_zero"), 1)
            pool.wait_ge(S("ident_zero"), 2)
            nc.gpsimd.affine_select(out=ident[:], in_=ident[:], compare_op=ALU.not_equal, fill=1.0, base=0,
                                    pattern=[[-1, 128]], channel_multiplier=1).then_inc(S("ident_ready"), 1)
            for i in range(2):
                nc.gpsimd.memset(vc[i][:], 1.0).then_inc(S("pool_set"), 1)
            for i in range(2):
                nc.gpsimd.memset(q_stack[i][:].bitcast(F32), 0.0).then_inc(S("pool_set"), 1)

            def power(b, ready, n, var, out_, t):
                pool.wait_ge(ready, n)
                nc.gpsimd.tensor_scalar(vareps[:, 0:t], var, EPS, 1.0, ALU.add, ALU.mult).then_inc(S("vareps"), 1)
                power.n += 1
                pool.wait_ge(S("vareps"), power.n)
                return nc.gpsimd.tensor_tensor(out_, vareps[:, 0:t], half[:, 0:t], ALU.pow)

            power.n = 0
            for st, *args in ORDER:
                b = args[-1]
                name, *rest = st.split(":")
                if name == "ctx":
                    power(b, S("ctx_mean"), nth(b, 1), meanvar[b % 2][:, 0:1, 1], rstd[b % 2][:, 0:1], 1).then_inc(
                        S("ctx_rstd"), 1)
                elif name == "ln":
                    inst = rest[0]
                    power(b, S(f"{inst}_mean"), nth(b, T, T - 1), meanvar[b % 2][:, :, 1], rstd[b % 2][:],
                          T).then_inc(S(f"{inst}_rstd"), 1)
                    if b == 0 and inst in ("a1", "b1"):
                        pool.wait_ge(S("rows_loaded"), 16 * (3 if inst == "a1" else 5))
                    pool.wait_ge(S(f"{inst}_rowz"), nth(b, T, T - 1))
                    r = ROW_SLOT[BIAS_AFTER[inst]]
                    for t in range(T):
                        nc.gpsimd.tensor_tensor(xs[b % 2][:, t, :], xs[b % 2][:, t, :], rows[:, r, :],
                                                ALU.add).then_inc(S(f"{inst}_biased"), 1)
                elif name == "scalars":
                    pool.wait_ge(S("extremes"), 2 * NQ)
                    nc.gpsimd.partition_all_reduce(allext[:], ext[:], 128,
                                                   bass.bass_isa.ReduceOp.max).then_inc(S("extremes_all"), 1)

        @block.tensor
        def _(pe):
            def product(out_, pairs, lhs_is_w):
                for i, (xp, wp) in enumerate(pairs):
                    lhs, rhs = (wp, xp) if lhs_is_w else (xp, wp)
                    last = nc.tensor.matmul(out_, lhs, rhs, start=(i == 0), stop=(i == len(pairs) - 1))
                return last

            def parts(b, kt, a, n):
                return (hiT[b % 2][:, kt, a:a + n], loT[b % 2][:, kt, a:a + n])

            def wait_weights(name):
                if name in W0:
                    pe.wait_ge(S("w0_split"), list(W0).index(name) + 1)
                else:
                    pe.wait_ge(S("integers"), QN.index(name) + 1)

            pending = []

            def values(unit):
                st, b, qd, kt = unit
                first, n, last = units[unit]
                inst = st.split(":")[1]
                o = bank((st, b, qd, "pv"))
                if kt == 0:
                    claim(pe, (st, b, qd, "pv"))
                drained(pe, (st, b, qd, kt, n - 1))
                for j in range(4):
                    h = 4 * qd + j
                    if inst == "sa":
                        lhs = vx[b % 2][:, kt, h * VS:h * VS + VW]
                        rhs = probs[:, (first + j) % NP, :]
                    else:
                        r = NK * (j % 2)
                        lhs = vc[b % 2][r:r + NK, h * VS:h * VS + VW]
                        rhs = probs[r:r + NK, (first + j // 2) % NP, :]
                    mm = nc.tensor.matmul(o[VW * j:VW * j + VW, :], lhs, rhs, start=(kt == 0), stop=last,
                                          tile_position=(0 if inst == "sa" else r, VW * j))
                mm.then_inc(done((st, b, qd, "pv")) if last else S("probs_used"), 1)

            pe.wait_ge(S("ident_ready"), 1)
            for st, *args in ORDER:
                b = args[-1]
                name, *rest = st.split(":")
                if name in ("ctx", "ctx1"):
                    wk, wv = ("kv", "kv") if name == "ctx" else ("k2", "v2")
                    va = D if name == "ctx" else 0
                    o = claim(pe, (st, b, "T"))
                    if name == "ctx":
                        pe.wait_ge(S("ctx_z"), nth(b, 1))
                        src = ctx_z
                    else:
                        pe.wait_ge(S(f"ctx_loaded{b % 2}"), 32 * (2 + b // 2 + 1))
                        src = ctx_rows[b % 2]
                    for kt in range(2):
                        mm = nc.tensor.transpose(o[0:CK, kt * 128:kt * 128 + 128], src[:, kt * CK:kt * CK + CK],
                                                 ident[:])
                    mm.then_inc(done((st, b, "T")), 1)
                    o = claim(pe, (st, b, "K"))
                    pe.wait_ge(S("ctx_lo"), nth((0 if name == "ctx" else B) + b, 1))
                    wait_weights(wk)
                    for m in range(2):
                        pairs = []
                        for kt in range(2):
                            xp = (ctx_hi[:, kt, 0:NK], ctx_lo[:, kt, 0:NK])
                            pairs += passes(xp, weights(wk, kt, m * 128, 128, CK))
                        mm = product(o[:, m * NK:m * NK + NK], pairs, True)
                    mm.then_inc(done((st, b, "K")), 1)
                    o = claim(pe, (st, b, "V"))
                    wait_weights(wv)
                    pairs = []
                    for kt in range(2):
                        pairs += passes((ctx_hi[:, kt, :], ctx_lo[:, kt, :]), weights(wv, kt, va, D, CK))
                    product(o[:, 0:D], pairs, False).then_inc(done((st, b, "V")), 1)
                elif name == "ln":
                    inst = rest[0]
                    for f in range(F):
                        o = claim(pe, (st, b, f))
                        pe.wait_ge(S(f"{inst}_rowz"), nth(b, T, T - 1))
                        for t in range(T):
                            mm = nc.tensor.transpose(o[:, t * 128:t * 128 + 128],
                                                     rowz[b % 2][:, t, f * 128:f * 128 + 128], ident[:])
                        mm.then_inc(done((st, b, f)), 1)
                elif name in ("q", "k"):
                    w = {"q:xa": "q", "q:sa": "q1", "k:sa": "k1", "q:xb": "q2"}[st]
                    wait_weights(w)
                    pe.wait_ge(S(f"{LN_OF[rest[0]]}_loT"), nth(b, F, F - 1))
                    for m in range(2):
                        o = claim(pe, (st, b, m))
                        pairs = []
                        for kt in range(F):
                            pairs += passes(parts(b, kt, 0, R), weights(w, kt, m * 128, 128))
                        product(o, pairs, True).then_inc(done((st, b, m)), 1)
                elif name == "v":
                    wait_weights("v1")
                    for t2 in range(T // 2):
                        o = claim(pe, (st, b, t2))
                        for i in range(2):
                            pairs = []
                            for kt in range(F):
                                pairs += passes(parts(b, kt, (2 * t2 + i) * 128, 128), weights("v1", kt, 0, D))
                            mm = product(o[:, i * D:i * D + D], pairs, False)
                        mm.then_inc(done((st, b, t2)), 1)
                elif name == "max":
                    inst, g = rest[0], int(rest[1])
                    pe.wait_ge(S(f"q_stacked{b % 2}"), 16 * 6 * q_seen[(f"q:{inst}", b)])
                    ks = stack_of(inst, b)
                    if inst == "sa":
                        pe.wait_ge(S(f"k_stacked{b % 2}"), 16 * 6 * (b // 2 + 1))
                        for hp, par in heads(g, 8):
                            r = 64 * par
                            for t in range(T):
                                key = (st, b, hp, par, t)
                                o = claim(pe, key)
                                nc.tensor.matmul(o, q_stack[b % 2][r:r + 3 * HD, hp, t * 128:t * 128 + 128],
                                                 ks[r:r + 3 * HD, hp, :], start=True, stop=True,
                                                 tile_position=(r, 0)).then_inc(done(key), 1)
                    else:
                        n = (0 if inst == "xa" else 2) + b // 2 + 1
                        pe.wait_ge(S(f"kc_stacked{b % 2}"), 16 * 6 * n)
                        for t in range(T):
                            for par in range(2):
                                r = 64 * par
                                o = claim(pe, (st, b, t, par))
                                for hp in range(H // 2):
                                    mm = nc.tensor.matmul(o[:, hp * NK:hp * NK + NK],
                                                          q_stack[b % 2][r:r + 3 * HD, hp, t * 128:t * 128 + 128],
                                                          ks[r:r + 3 * HD, hp, par * NK:par * NK + NK],
                                                          start=True, stop=True, tile_position=(r, 0))
                                mm.then_inc(done((st, b, t, par)), 1)
                elif name == "neg":
                    inst, g = rest[0], int(rest[1])
                    n = 8 if inst == "sa" else 16
                    o = claim(pe, (st, b))
                    last_max = (*heads(g, 8)[-1], T - 1) if inst == "sa" else (T - 1, 1)
                    drained(pe, (st.replace("neg", "max"), b, *last_max))
                    for t in range(T):
                        mm = nc.tensor.transpose(o[0:n, t * 128:t * 128 + 128], negmax[b % 2][:, t, g * 8:g * 8 + n],
                                                 ident[:])
                    mm.then_inc(done((st, b)), 1)
                elif name == "exp":
                    inst = rest[0]
                    ks = stack_of(inst, b)
                    pe.wait_ge(S(f"neg_stacked{b % 2}"), neg_total[(inst, b)])
                    if inst == "sa":
                        filled_v = [("v:sa", b, t2) for t2 in range(T // 2)]
                    else:
                        filled_v = [("ctx" if inst == "xa" else "ctx1", b, "V")]
                    if b < 2:
                        pe.wait_ge(S("pool_set"), 4)
                    if inst == "sa" and b < 2:
                        pe.wait_ge(S("ones_set"), 4)
                    for key in filled_v:
                        drained(pe, key)
                    for qd in range(4):
                        for kt in range(T if inst == "sa" else 1):
                            if inst == "sa":
                                for j in range(4):
                                    hp, r = 2 * qd + j // 2, 64 * (j % 2)
                                    key = (st, b, qd, kt, j)
                                    o = claim(pe, key)
                                    nc.tensor.matmul(o, ks[r:r + 3 * HD + 2, hp, kt * 128:kt * 128 + 128],
                                                     q_stack[b % 2][r:r + 3 * HD + 2, hp, :], start=True, stop=True,
                                                     tile_position=(r, 0)).then_inc(done(key), 1)
                            else:
                                for j in range(2):
                                    key = (st, b, qd, kt, j)
                                    o = claim(pe, key)
                                    nc.tensor.matmul(o, ks[:, 2 * qd + j, :], q_stack[b % 2][:, 2 * qd + j, :],
                                                     start=True, stop=True).then_inc(done(key), 1)
                            if pending:
                                values(pending.pop())
                            pending.append((st, b, qd, kt))
                    values(pending.pop())
                elif name == "out1":
                    inst = rest[0]
                    for t in range(T):
                        o = claim(pe, (st, b, t))
                        for qd in range(4):
                            drained(pe, (f"exp:{inst}", b, qd, "pv"))
                            mm = nc.tensor.transpose(o[:, qd * 128:qd * 128 + 128],
                                                     o_raw[:, qd, t * 128:t * 128 + 128], ident[:])
                        mm.then_inc(done((st, b, t)), 1)
                elif name == "out2":
                    inst = rest[0]
                    for f in range(F):
                        o = claim(pe, (st, b, f))
                        for t in range(T):
                            drained(pe, (f"out1:{inst}", b, t))
                            mm = nc.tensor.transpose(o[:, t * 128:t * 128 + 128],
                                                     rowz[b % 2][:, t, f * 128:f * 128 + 128], ident[:])
                        mm.then_inc(done((st, b, f)), 1)
                elif name == "out3":
                    inst = rest[0]
                    w = PROJ[inst]
                    wait_weights(w)
                    for t2 in range(T // 2):
                        o = claim(pe, (st, b, t2))
                        for f in range(F):
                            drained(pe, (f"out2:{inst}", b, f))
                        for i in range(2):
                            pairs = []
                            for kt in range(F):
                                pairs += passes(parts(b, kt, (2 * t2 + i) * 128, 128), weights(w, kt, 0, D))
                            mm = product(o[:, i * D:i * D + D], pairs, False)
                        mm.then_inc(done((st, b, t2)), 1)
                elif name in ("mlp0", "mlp1"):
                    first = name == "mlp0"
                    wu, wd = ("w1", "w2") if first else ("ff1", "ff2")
                    wait_weights(wu)
                    pe.wait_ge(S(f"{'a3' if first else 'b3'}_loT"), nth(b, F, F - 1))

                    def up(m, kind):
                        a = m * 128 + (HID if kind == "g" else 0)
                        o = claim(pe, (st, b, m, kind))
                        pairs = []
                        for kt in range(F):
                            pairs += passes(parts(b, kt, 0, R), weights(wu, kt, a, 128))
                        product(o, pairs, True).then_inc(done((st, b, m, kind)), 1)

                    def down(m):
                        if m == 0:
                            for t2 in range(T // 2):
                                claim(pe, (st, b, t2, "acc"))
                            wait_weights(wd)
                        pe.wait_ge(S(f"{name}_lo"), nth(b, M, m))
                        hp_ = (hid_parts[:, m % 2, 0, :], hid_parts[:, m % 2, 1, :])
                        for t in range(T):
                            o = bank((st, b, t // 2, "acc"))[:, (t % 2) * D:(t % 2) * D + D]
                            xp = tuple(p_[:, t * 128:t * 128 + 128] for p_ in hp_)
                            ps_ = passes(xp, weights(wd, m, 0, D))
                            for i, (a_, w_) in enumerate(ps_):
                                mm = nc.tensor.matmul(o, a_, w_, start=(m == 0 and i == 0 and t % 2 == 0),
                                                      stop=(m == M - 1 and i == len(ps_) - 1), skip_group_check=True)
                            if m == M - 1 and t % 2 == 1:
                                mm.then_inc(done((st, b, t // 2, "acc")), 1)

                    for m in range(M):
                        up(m, "h")
                        if not first:
                            up(m, "g")
                        if m:
                            down(m - 1)
                    down(M - 1)

        @block.scalar
        def _(act):
            def split0(i):
                w = list(W0)[i]
                o, m_ = OFF0[w], W0[w][0] * W0[w][1]
                act.wait_ge(S(f"raw0_{w}_loaded"), 16)
                nc.scalar.copy(wh[:, o:o + m_], raw0a[:, o:o + m_]).then_inc(S("w0_hi"), 1)

            def o_copy(st, b, qd):
                o = filled(act, (st, b, qd, "pv"))
                nc.scalar.copy(o_raw[:, qd, :], o).then_inc(release((st, b, qd, "pv")), 1)

            split0(0)
            act.wait_ge(S("vectors_loaded"), 16)
            neg_n, tile = 0, 0
            for st, *args in ORDER:
                b = args[-1]
                name, *rest = st.split(":")
                if name in ("ctx", "ctx1"):
                    n = (0 if name == "ctx" else B) + b
                    o = filled(act, (st, b, "T"))
                    if n:
                        act.wait_ge(S("ctx_lo"), n)
                    for kt in range(2):
                        src = o[0:CK, kt * 128:kt * 128 + 128]
                        if name == "ctx":
                            ins = nc.scalar.activation(ctx_full[:, kt, :], src, ACT.Identity,
                                                       bias=col("a2_b", kt, CK), scale=col("a2_g", kt, CK))
                        else:
                            ins = nc.scalar.copy(ctx_full[:, kt, :], src)
                    ins.then_inc(release((st, b, "T")), 1)
                    drained(act, (st, b, "T"))
                    if n:
                        pst, pb = ("ctx", n - 1) if n <= B else ("ctx1", n - 1 - B)
                        filled(act, (pst, pb, "V"))
                    nc.scalar.copy(ctx_hi[:], ctx_full[:]).then_inc(S("ctx_hi"), 1)
                    o = filled(act, (st, b, "K"))
                    if n:
                        act.wait_ge(S("kc_sent"), 16 * n)
                    nc.scalar.copy(kc_parts[:, 0, :], o[:, 0:2 * NK]).then_inc(S("kc_hi"), 1)
                    o = filled(act, (st, b, "V"))
                    if n < 2:
                        act.wait_ge(S("pool_set"), 2)
                    else:
                        filled(act, (*kc_user(n - 2), 3, "pv"))
                    v_ = vc[b % 2][:, 0:H * VS].rearrange("p (h e) -> p h e", e=VS)[:, :, 0:HD]
                    src = o[:, 0:D].rearrange("p (h d) -> p h d", d=HD)
                    if name == "ctx":
                        nc.scalar.copy(v_, src).then_inc(release((st, b, "V")), 1)
                    else:
                        nc.scalar.mul(v_, src, delta("v2")).then_inc(release((st, b, "V")), 1)
                    if st == "ctx" and b < 2:
                        for i in ((1, 2), (3, 4))[b]:
                            split0(i)
                elif name == "ln":
                    inst = rest[0]
                    i = ln_index[(st, b)]
                    for f in range(F):
                        o = filled(act, (st, b, f))
                        if i:
                            pst, pb = ln_list[i - 1]
                            act.wait_ge(S(f"{pst.split(':')[1]}_loT"), nth(pb, F, f))
                        nc.scalar.activation(full_t[:, f, :], o, ACT.Identity, bias=col(f"{inst}_b", f),
                                             scale=col(f"{inst}_g", f)).then_inc(release((st, b, f)), 1)
                        drained(act, (st, b, f))
                        nc.scalar.copy(hiT[b % 2][:, f, :], full_t[:, f, :]).then_inc(S(f"{inst}_hiT"), 1)
                elif name in ("q", "k"):
                    i = qk_index[(st, b)]
                    for m in range(2):
                        o = filled(act, (st, b, m))
                        if i:
                            act.wait_ge(S(f"qk_sent{m}"), 16 * i)
                        if st in q_scaled:
                            nc.scalar.mul(qk_parts[:, m, 0, :], o, prods[:, q_scaled[st]:q_scaled[st] + 1]).then_inc(
                                S("qk_hi"), 1)
                        else:
                            nc.scalar.copy(qk_parts[:, m, 0, :], o).then_inc(S("qk_hi"), 1)
                elif name == "v":
                    for t2 in range(T // 2):
                        o = filled(act, (st, b, t2))
                        if b >= 2:
                            filled(act, ("exp:sa", b - 2, 3, "pv"))
                        elif t2 == 0:
                            act.wait_ge(S("ones_set"), 4)
                        nc.scalar.mul(vx[b % 2][:, 2 * t2:2 * t2 + 2, 0:H * VS].rearrange(
                                          "p t (h e) -> p t h e", e=VS)[:, :, :, 0:HD],
                                      o.rearrange("p (t h d) -> p t h d", t=2, d=HD),
                                      delta("v1")).then_inc(release((st, b, t2)), 1)
                elif name == "neg":
                    n = 8 if rest[0] == "sa" else 16
                    o = filled(act, (st, b))
                    if neg_n:
                        act.wait_ge(S("neg_sent"), 16 * neg_n)
                    nc.scalar.copy(neg_parts[0:n, 0, :], o[0:n, :]).then_inc(S("neg_hi"), 1)
                    neg_n += 1
                elif name == "exp":
                    inst = rest[0]
                    for qd in range(4):
                        for kt in range(T if inst == "sa" else 1):
                            for j in range(4 if inst == "sa" else 2):
                                o = filled(act, (st, b, qd, kt, j))
                                if tile >= NP:
                                    u = tile_unit[tile - NP]
                                    if units[u][2]:
                                        filled(act, (u[0], u[1], u[2], "pv"))
                                    else:
                                        act.wait_ge(S("probs_used"), quad_used[u])
                                nc.scalar.activation(probs[:, tile % NP, :], o, ACT.Exp, scale=SCALE).then_inc(
                                    release((st, b, qd, kt, j)), 1)
                                tile += 1
                        if qd:
                            o_copy(st, b, qd - 1)
                    o_copy(st, b, 3)
                elif name == "out2":
                    for f in range(F):
                        o = filled(act, (st, b, f))
                        nc.scalar.copy(hiT[b % 2][:, f, :], o).then_inc(S("o_hiT"), 1)
                elif name in ("mlp0", "mlp1"):
                    first = name == "mlp0"
                    for m in range(M):
                        n = b * M + m
                        s_ = m % 2
                        if first:
                            o = filled(act, (st, b, m, "h"))
                            if n >= 2:
                                act.wait_ge(S("mlp0_lo"), n - 1)
                            nc.scalar.activation(hid[:, s_, :], o, ACT.Gelu, bias=col("mlp0_b", m)).then_inc(
                                release((st, b, m, "h")), 1)
                            drained(act, (st, b, m, "h"))
                        else:
                            o = filled(act, (st, b, m, "g"))
                            if n >= 2:
                                drained(act, (st, *divmod(n - 2, M), "h"))
                            nc.scalar.activation(gate[:, s_, :], o, ACT.Gelu_apprx_tanh,
                                                 bias=col("ff1_b", M + m), scale=delta("ff1")).then_inc(
                                release((st, b, m, "g")), 1)
                            drained(act, (st, b, m, "h"))
                        nc.scalar.copy(hid_parts[:, s_, 0, :], hid[:, s_, :]).then_inc(S(f"{name}_hi"), 1)

        @block.vector
        def _(dve):
            def split0(i):
                w = list(W0)[i]
                o, m_ = OFF0[w], W0[w][0] * W0[w][1]
                dve.wait_ge(S("w0_hi"), i + 1)
                nc.vector.tensor_tensor(wl[:, o:o + m_], raw0a[:, o:o + m_], wh[:, o:o + m_],
                                        ALU.subtract).then_inc(S("w0_split"), 1)

            for i in range(2):
                nc.vector.memset(kc_stack[i][:].bitcast(F32), 0.0).then_inc(S("kc_zero"), 1)
                dve.wait_ge(S("kc_zero"), i + 1)
                for par in range(2):
                    nc.vector.memset(kc_stack[i][64 * par + 32:64 * par + 64, :, par * NK:par * NK + NK].bitcast(F32),
                                     1.0).then_inc(S("kc_set"), 1)
            nc.vector.memset(ext[:], -3.0e38).then_inc(S("ext_set"), 1)
            split0(0)
            for st, *args in ORDER:
                b = args[-1]
                name, *rest = st.split(":")
                if name in ("ctx", "ctx1"):
                    n = (0 if name == "ctx" else B) + b
                    if name == "ctx":
                        cr = ctx_rows[b % 2]
                        dve.wait_ge(S(f"ctx_loaded{b % 2}"), 32 * (b // 2 + 1))
                        nc.vector.bn_stats(six[b % 2][:, 0, :], cr[:]).then_inc(S("ctx_six"), 1)
                        dve.wait_ge(S("ctx_six"), nth(b, 1))
                        nc.vector.bn_aggr(meanvar[b % 2][:, 0, :], six[b % 2][:, 0, :]).then_inc(S("ctx_mean"), 1)
                        dve.wait_ge(S("ctx_rstd"), nth(b, 1))
                        if b:
                            filled(dve, (st, b - 1, "T"))
                        nc.vector.tensor_scalar(ctx_z[:], cr[:], meanvar[b % 2][:, 0, 0:1], rstd[b % 2][:, 0:1],
                                                ALU.subtract, ALU.mult).then_inc(S("ctx_z"), 1)
                    dve.wait_ge(S("ctx_hi"), n + 1)
                    nc.vector.tensor_tensor(ctx_lo[:], ctx_full[:], ctx_hi[:], ALU.subtract).then_inc(S("ctx_lo"), 1)
                    dve.wait_ge(S("kc_hi"), n + 1)
                    o = filled(dve, (st, b, "K"))
                    nc.vector.tensor_tensor(kc_parts[:, 1, :], o[:, 0:2 * NK], kc_parts[:, 0, :],
                                            ALU.subtract).then_inc(release((st, b, "K")), 1)
                    if st == "ctx" and b < 2:
                        for i in ((1, 2), (3, 4))[b]:
                            split0(i)
                elif name == "ln":
                    inst = rest[0]
                    xb = xs[b % 2]
                    if inst in ("a1", "b1"):
                        dve.wait_ge(S(f"x_loaded{b % 2}"), 16 * ((0 if inst == "a1" else 2) + b // 2 + 1))
                    else:
                        att = {"a3": "xa", "b2": "sa", "b3": "xb"}[inst]
                        for t2 in range(T // 2):
                            drained(dve, (f"out3:{att}", b, t2))
                    for t in range(T):
                        nc.vector.bn_stats(six[b % 2][:, t, :], xb[:, t, :]).then_inc(S(f"{inst}_six"), 1)
                    for t in range(T):
                        dve.wait_ge(S(f"{inst}_six"), nth(b, T, t))
                        nc.vector.bn_aggr(meanvar[b % 2][:, t, :], six[b % 2][:, t, :]).then_inc(
                            S(f"{inst}_mean"), 1)
                    dve.wait_ge(S(f"{inst}_rstd"), nth(b, 1))
                    for t in range(T):
                        nc.vector.tensor_scalar(rowz[b % 2][:, t, :], xb[:, t, :], meanvar[b % 2][:, t, 0:1],
                                                rstd[b % 2][:, t:t + 1], ALU.subtract, ALU.mult).then_inc(
                            S(f"{inst}_rowz"), 1)
                    for f in range(F):
                        dve.wait_ge(S(f"{inst}_hiT"), nth(b, F, f))
                        nc.vector.tensor_tensor(loT[b % 2][:, f, :], full_t[:, f, :], hiT[b % 2][:, f, :], ALU.subtract).then_inc(
                            S(f"{inst}_loT"), 1)
                elif name in ("q", "k"):
                    i = qk_index[(st, b)]
                    for m in range(2):
                        dve.wait_ge(S("qk_hi"), 2 * i + m + 1)
                        o = filled(dve, (st, b, m))
                        hi_ = qk_parts[:, m, 0, :]
                        if st in q_scaled:
                            ins = nc.vector.scalar_tensor_tensor(
                                out=qk_parts[:, m, 1, :], in0=o, scalar=prods[:, q_scaled[st]:q_scaled[st] + 1],
                                in1=hi_, op0=ALU.mult, op1=ALU.subtract)
                        else:
                            ins = nc.vector.tensor_tensor(qk_parts[:, m, 1, :], o, hi_, ALU.subtract)
                        ins.then_inc(release((st, b, m)), 1)
                elif name == "max":
                    inst, g = rest[0], int(rest[1])
                    nm = negmax[b % 2]
                    if inst == "sa":
                        for hp, par in heads(g, 8):
                            c = g * 8 + par * 4 + hp % 4
                            for t in range(T):
                                o = filled(dve, (st, b, hp, par, t))
                                nc.vector.tensor_reduce(nm[:, t, c:c + 1], o, AX.X, ALU.max, negate=True).then_inc(
                                    release((st, b, hp, par, t)), 1)
                        key = (st, b, *heads(g, 8)[-1], T - 1)
                    else:
                        for t in range(T):
                            for par in range(2):
                                o = filled(dve, (st, b, t, par))
                                nc.vector.tensor_reduce(nm[:, t, par * 8:par * 8 + 8],
                                                        o.rearrange("p (h k) -> p h k", k=NK), AX.X, ALU.max,
                                                        negate=True).then_inc(release((st, b, t, par)), 1)
                elif name == "neg":
                    i = neg_index[(st, b)]
                    n = 8 if rest[0] == "sa" else 16
                    dve.wait_ge(S("neg_hi"), i + 1)
                    o = filled(dve, (st, b))
                    nc.vector.tensor_tensor(neg_parts[0:n, 1, :], o[0:n, :], neg_parts[0:n, 0, :],
                                            ALU.subtract).then_inc(release((st, b)), 1)
                elif name == "out1":
                    for t in range(T):
                        o = filled(dve, (st, b, t)).rearrange("p (h e) -> p h e", e=VW)
                        n = out_index[(st, b)] * T + t
                        nc.vector.reciprocal(rsum[:], o[:, :, HD]).then_inc(S("rsum"), 1)
                        dve.wait_ge(S("rsum"), n + 1)
                        nc.vector.tensor_tensor(rowz[b % 2][:, t, :].rearrange("p (h d) -> p h d", d=HD),
                                                o[:, :, 0:HD], rsum[:].unsqueeze(2).broadcast_to([128, H, HD]),
                                                ALU.mult).then_inc(release((st, b, t)), 1)
                        drained(dve, (st, b, t))
                elif name == "out2":
                    n = out_index[(st.replace("out2", "out1"), b)]
                    for f in range(F):
                        dve.wait_ge(S("o_hiT"), 2 * n + f + 1)
                        o = filled(dve, (st, b, f))
                        nc.vector.tensor_tensor(loT[b % 2][:, f, :], o, hiT[b % 2][:, f, :], ALU.subtract).then_inc(
                            release((st, b, f)), 1)
                elif name == "out3":
                    inst = rest[0]
                    dve.wait_ge(S(f"{LN_OF[inst]}_biased"), nth(b, T, T - 1))
                    for t2 in range(T // 2):
                        o = filled(dve, (st, b, t2)).rearrange("p (t d) -> p t d", t=2)
                        x2 = xs[b % 2][:, 2 * t2:2 * t2 + 2, :]
                        if inst == "xa":
                            ins = nc.vector.tensor_tensor(x2, o, x2, ALU.add)
                        else:
                            ins = nc.vector.scalar_tensor_tensor(out=x2, in0=o, scalar=delta(PROJ[inst]), in1=x2,
                                                                 op0=ALU.mult, op1=ALU.add)
                        ins.then_inc(release((st, b, t2)), 1)
                elif name in ("mlp0", "mlp1"):
                    first = name == "mlp0"
                    for m in range(M):
                        n = b * M + m
                        s_ = m % 2
                        if not first:
                            o = filled(dve, (st, b, m, "h"))
                            drained(dve, (st, b, m, "g"))
                            if n >= 2:
                                dve.wait_ge(S("mlp1_lo"), n - 1)
                            nc.vector.scalar_tensor_tensor(out=hid[:, s_, :], in0=o, scalar=ffb[:, m:m + 1],
                                                           in1=gate[:, s_, :], op0=ALU.add, op1=ALU.mult).then_inc(
                                release((st, b, m, "h")), 1)
                        dve.wait_ge(S(f"{name}_hi"), n + 1)
                        ins = nc.vector.tensor_tensor(hid_parts[:, s_, 1, :], hid[:, s_, :], hid_parts[:, s_, 0, :],
                                                      ALU.subtract)
                        ins.then_inc(S(f"{name}_lo"), 1)
                    dve.wait_ge(S(f"{'a3' if first else 'b3'}_biased"), nth(b, T, T - 1))
                    for t2 in range(T // 2):
                        o = filled(dve, (st, b, t2, "acc")).rearrange("p (t d) -> p t d", t=2)
                        x2 = xs[b % 2][:, 2 * t2:2 * t2 + 2, :]
                        if first:
                            ins = nc.vector.tensor_tensor(x2, o, x2, ALU.add)
                        else:
                            ins = nc.vector.scalar_tensor_tensor(out=x2, in0=o, scalar=prods[:, 2:3], in1=x2,
                                                                 op0=ALU.mult, op1=ALU.add)
                        ins.then_inc(release((st, b, t2, "acc")), 1)
                elif name == "stats":
                    w = QN[b]
                    o, m_ = OFF1[w], W1[w][0] * W1[w][1]
                    p_ = CK if w in ("k2", "v2") else 128
                    dve.wait_ge(S(f"raw1_{w}_loaded"), 16)
                    nc.vector.tensor_reduce(ext[0:p_, b:b + 1], raw1[0:p_, o:o + m_], AX.X, ALU.max).then_inc(
                        S("extremes"), 1)
                    nc.vector.tensor_reduce(ext[0:p_, NQ + b:NQ + b + 1], raw1[0:p_, o:o + m_], AX.X, ALU.min,
                                            negate=True).then_inc(S("extremes"), 1)
                elif name == "scalars":
                    dve.wait_ge(S("extremes_all"), 1)
                    steps = [0]

                    def step(ins):
                        ins.then_inc(S("scalar_step"), 1)
                        steps[0] += 1
                        dve.wait_ge(S("scalar_step"), steps[0])

                    mx, nmn = allext[:, 0:NQ], allext[:, NQ:2 * NQ]
                    dl, inv, span, low, high, t0, t1, zp = (qs[:, i, :] for i in range(8))
                    step(nc.vector.tensor_tensor(span, mx, nmn, ALU.add))
                    step(nc.vector.tensor_scalar(t0, span, 1.0 / LEVELS, None, ALU.mult))
                    step(nc.vector.tensor_copy(qhi[:], t0))
                    step(nc.vector.tensor_tensor(t1, t0, qhi[:], ALU.subtract))
                    step(nc.vector.scalar_tensor_tensor(out=zp, in0=qhi[:], scalar=-LEVELS, in1=span, op0=ALU.mult,
                                                        op1=ALU.add))
                    step(nc.vector.scalar_tensor_tensor(out=low, in0=t1, scalar=-LEVELS, in1=zp, op0=ALU.mult,
                                                        op1=ALU.add))
                    step(nc.vector.scalar_tensor_tensor(out=dl, in0=low, scalar=1.0 / LEVELS, in1=t0, op0=ALU.mult,
                                                        op1=ALU.add))
                    step(nc.vector.reciprocal(inv, dl))
                    step(nc.vector.tensor_tensor(t0, nmn, inv, ALU.mult))
                    step(nc.vector.tensor_scalar(t1, t0, MAGIC, None, ALU.add))
                    step(nc.vector.tensor_scalar(zp, t1, -MAGIC, None, ALU.add))
                    step(nc.vector.tensor_scalar(low, zp, -1.0, MAGIC, ALU.mult, ALU.add))
                    step(nc.vector.tensor_scalar(high, low, LEVELS, None, ALU.add))
                    for i, (a_, c_) in enumerate((("q1", "k1"), ("q2", "k2"), ("ff1", "ff2"))):
                        step(nc.vector.tensor_tensor(prods[:, i:i + 1], delta(a_), delta(c_), ALU.mult))
                    dve.wait_ge(S("vectors_loaded"), 16)
                    i = QN.index("ff1")
                    nc.vector.tensor_scalar(ffb[:], vec[:, OFFV["ff1_b"]:OFFV["ff1_b"] + M], qs[:, 1, i:i + 1], None,
                                            ALU.mult).then_inc(S("quant_scalars"), 1)
                elif name == "round":
                    o, m_ = OFF1[QN[b]], W1[QN[b]][0] * W1[QN[b]][1]
                    v = raw1[:, o:o + m_]
                    nc.vector.tensor_scalar(v, v, qs[:, 1, b:b + 1], MAGIC, ALU.mult, ALU.add).then_inc(
                        S("rounded"), 1)
                    dve.wait_ge(S("rounded"), b + 1)
                    nc.vector.tensor_scalar(v, v, qs[:, 3, b:b + 1], qs[:, 4, b:b + 1], ALU.max, ALU.min).then_inc(
                        S("clipped"), 1)
                elif name == "integers":
                    for t2 in range(T // 2):
                        filled(dve, ("mlp0", B - 1, t2, "acc"))
                    for i, w in enumerate(QN):
                        o, m_ = OFF1[w], W1[w][0] * W1[w][1]
                        dve.wait_ge(S("clipped"), i + 1)
                        nc.vector.tensor_scalar(wn[:, o:o + m_], raw1[:, o:o + m_], -MAGIC, None,
                                                ALU.add).then_inc(S("integers"), 1)
                    dve.wait_ge(S("integers"), NQ)
                    for i in range(2):
                        nc.vector.memset(k_stack[i][:].bitcast(F32), 1.0).then_inc(S("ones_set"), 1)
                        nc.vector.memset(vx[i][:], 1.0).then_inc(S("ones_set"), 1)


_VECTORS = {"a1_g": "L0_xattn_ln1_w", "a1_b": "L0_xattn_ln1_b", "a2_g": "L0_xattn_ln2_w", "a2_b": "L0_xattn_ln2_b",
            "a3_g": "L0_xattn_ln3_w", "a3_b": "L0_xattn_ln3_b", "b1_g": "L1_xattn_ln1_g", "b1_b": "L1_xattn_ln1_b",
            "b2_g": "L1_xattn_ln2_g", "b2_b": "L1_xattn_ln2_b", "b3_g": "L1_xattn_ln3_g", "b3_b": "L1_xattn_ln3_b",
            "mlp0_b": "L0_xattn_b1", "ff1_b": "L1_xattn_ff1_b"}


def kernel(**inputs):
    import numpy as _np
    import concourse.bacc as _bacc
    from concourse import mybir as _mybir
    from concourse.bass_utils import run_bass_kernel_spmd as _run

    a = {k: _np.asarray(v) for k, v in inputs.items()}

    def pack(weights, widths):
        cols = []
        for name, w in weights.items():
            tiles, n = widths[name]
            rows_ = w.shape[0] // tiles
            tile = _np.zeros((128, tiles, n), w.dtype)
            tile[:rows_] = w.reshape(tiles, rows_, n).transpose(1, 0, 2)
            cols.append(tile.reshape(128, tiles * n))
        return _np.ascontiguousarray(_np.concatenate(cols, axis=1))

    w0 = pack({"kv": a["L0_xattn_Wkv"], "q": a["L0_xattn_Wq"], "proj": a["L0_xattn_Wproj"], "w1": a["L0_xattn_W1"],
               "w2": a["L0_xattn_W2"]}, W0)
    w1 = pack({n: a[f"L1_xattn_{n}_w"].T for n in W1}, W1)
    vec = _np.zeros((128, NV), w0.dtype)
    for name, n in VEC.items():
        v = a[_VECTORS[name]].reshape(n, -1).T
        vec[:v.shape[0], OFFV[name]:OFFV[name] + n] = v
    rows = _np.stack([a["L0_xattn_bproj"], a["L0_xattn_b2"], a["L1_xattn_o1_b"], a["L1_xattn_o2_b"],
                      a["L1_xattn_ff2_b"]])
    arrays = {"x": a["x"], "ctx": a["ctx_768"], "w0": w0, "w1": w1, "vec": vec, "rows": rows}
    arrays = {f"in_{k}_dram": _np.ascontiguousarray(v) for k, v in arrays.items()}

    nc = _bacc.Bacc("TRN2", target_bir_lowering=False, num_devices=1)
    args = [nc.dram_tensor(k, v.shape, _mybir.dt.from_np(v.dtype), kind="ExternalInput").ap()
            for k, v in arrays.items()]
    o = nc.dram_tensor("out_0_dram", (B, R, D), _mybir.dt.float32, kind="ExternalOutput").ap()
    program(nc, *args, o)
    r = _run(nc, [arrays], core_ids=[0])
    return r.results[0]["out_0_dram"]
```

```python
from contextlib import ExitStack

import concourse.bass as bass
from concourse import mybir

F32 = mybir.dt.float32
F32R = mybir.dt.float32r
ACT = mybir.ActivationFunctionType
ALU = mybir.AluOpType
AX = mybir.AxisListType

B, R, D, C, NK = 4, 512, 256, 192, 64
H, HD = 16, 16
T, F = R // 128, D // 128
CK = C // 2
HID = 4 * D
M = HID // 128
EPS = 1e-5
SCALE = float(HD) ** -0.5
LEVELS = 255.0
MAGIC = 1.5 * 2.0 ** 23
VW = 32
VS = HD + 1
VN = H * VS + VW - VS

W0 = {"kv": (2, 2 * D), "q": (2, D), "proj": (2, D), "w1": (2, HID), "w2": (M, D)}
W1 = {"q1": (2, D), "k1": (2, D), "v1": (2, D), "o1": (2, D), "k2": (2, D), "v2": (2, D), "q2": (2, D),
      "o2": (2, D), "ff1": (2, 2 * HID), "ff2": (M, D)}
QN = list(W1)


def offsets(widths):
    at, out = 0, {}
    for name, (tiles, n) in widths.items():
        out[name] = at
        at += tiles * n
    return out, at


OFF0, N0 = offsets(W0)
OFF1, N1 = offsets(W1)
SPLIT0, SPLIT1 = OFF0["w1"], OFF1["ff1"]
VEC = {"a1_g": 2, "a1_b": 2, "a2_g": 2, "a2_b": 2, "a3_g": 2, "a3_b": 2, "b1_g": 2, "b1_b": 2, "b2_g": 2,
       "b2_b": 2, "b3_g": 2, "b3_b": 2, "mlp0_b": M, "ff1_b": 2 * M}
OFFV, NV = {}, 0
for _name, _n in VEC.items():
    OFFV[_name] = NV
    NV += _n
ROWS = ["bproj", "b2", "o1_b", "o2_b", "ff2_b"]
BIAS_AFTER = {"a1": "bproj", "a3": "b2", "b1": "o1_b", "b2": "o2_b", "b3": "ff2_b"}
LN_OF = {"xa": "a1", "sa": "b1", "xb": "b2"}
PROJ = {"xa": "proj", "sa": "o1", "xb": "o2"}



COST = {"load": (0, 0, 0, 4), "ctxz": (0, 1.2, 0, 3), "ctx": (0.3, 0.5, 1.4, 2.5), "ctxk": (2.0, 0.4, 0.6, 2.5),
        "ctxr": (0, 0, 0, 2), "ln": (0, 2.9, 0, 5.0), "lt": (0.9, 1.2, 2.4, 3.5), "q": (1.7, 1.3, 1.1, 2.8),
        "k": (1.7, 1.2, 1.0, 2.8), "v": (1.7, 0, 1.1, 1.8), "qr": (0, 0, 0, 5), "kr": (0, 0, 0, 5),
        "max:sa": (0.86, 2.45, 0, 0), "max:x": (1.7, 1.2, 0, 0), "neg": (0.45, 0.6, 0.5, 2.0),
        "negr": (0, 0, 0, 5.5), "exp:sa": (0.86, 0, 1.95, 0), "exp:x": (0.43, 0, 0.95, 0),
        "val:sa": (0.94, 0, 0, 0), "val:x": (0.94, 0, 0, 0), "out1": (1.8, 2.1, 0, 3.2), "out2": (0.9, 1.2, 1.0, 2.6),
        "out3": (1.7, 1.3, 0, 2.6), "mlp0": (1.3, 0.6, 1.0, 0), "down0": (1.3, 0, 0, 0), "mlp1": (1.7, 1.2, 1.0, 0),
        "down1": (0.9, 0, 0, 0), "store0": (0, 0, 0, 4), "store1": (0, 0, 0, 4), "stats": (0, 1.2, 0, 3),
        "statsff": (0, 8, 0, 9), "scalars": (0, 2, 0, 8), "round": (0, 0, 0, 6), "raw": (0, 0, 0, 6), "ones": (0, 0, 0, 2)}
SLACK = 2.0


def cost(st):
    name, *rest = st.split(":")
    if name in ("max", "exp", "val"):
        name += ":sa" if rest[0] == "sa" else ":x"
    return COST[name]


def attention_steps(inst):
    if inst == "sa":
        units = [f"{qd}:{kt}" for qd in range(4) for kt in range(T)]
        out = [f"max:sa:{h}" for h in range(8)] + ["neg:sa:0", "max:sa:8", "negr:sa:0"]
        out += [f"max:sa:{h}" for h in range(9, 12)]
        maxima = [f"max:sa:{h}" for h in range(12, H)]
        lead = 4
    else:
        units = [f"{qd}:0" for qd in range(4)]
        out = [f"max:{inst}:{t}" for t in range(T)] + [f"neg:{inst}:0", f"negr:{inst}:0"]
        maxima, lead = [], 0
    for i, u in enumerate(units):
        out.append(f"exp:{inst}:{u}")
        if i:
            out.append(f"val:{inst}:{units[i - 1]}")
        if i < lead:
            out.append(maxima[i])
        if lead and i == lead - 1:
            out.append("neg:sa:1")
        if lead and i == lead:
            out.append("negr:sa:1")
    return out + [f"val:{inst}:{units[-1]}"]


def thread(par):
    out = []
    turns = [(0, par), (0, par + 2), (1, par), (1, par + 2)]
    for n, (layer, b) in enumerate(turns):
        att = ["xa"] if layer == 0 else ["sa", "xb"]
        steps = [f"load:{layer}"]
        if n == 0:
            steps += ["ctxz", "ctx:xa", "ctxk:xa", "ctxr:xa"]
        for inst in att:
            a = LN_OF[inst]
            steps += [f"ln:{a}", f"lt:{a}"]
            if inst == "sa":
                steps += ["q:sa", "k:sa", "qr:sa", "v:sa", "kr:sa"]
            else:
                steps += [f"q:{inst}", f"qr:{inst}"]
            steps += attention_steps(inst) + [f"out1:{inst}", f"out2:{inst}", f"out3:{inst}"]
        a = "a3" if layer == 0 else "b3"
        steps += [f"ln:{a}", f"lt:{a}"]
        ahead = {}
        if n < 3:
            nl, nb = turns[n + 1]
            x_ = "xa" if nl == 0 else "xb"
            ahead = {0: ("ctxz", nb), 2: (f"ctx:{x_}", nb), 3: (f"ctxk:{x_}", nb), 5: (f"ctxr:{x_}", nb)}
            if nl:
                del ahead[0]
        steps = [(st, b) for st in steps]
        for m in range(M):
            steps.append((f"mlp{layer}:{m}", b))
            if m:
                steps.append((f"down{layer}:{m - 1}", b))
            if m in ahead:
                steps.append(ahead[m])
        steps += [(f"down{layer}:{M - 1}", b), (f"store{layer}", b)]
        out += steps
        if (layer, b) == (0, 3):
            i = out.index(("out3:xa", 3))
            out.insert(i + 1, ("ones", 0))
    return out


QSMALL = 8


def order():
    quant = [("raw", 0)] + [("stats", i) for i in range(QSMALL)] + [("scalars", 0)]
    quant += [("round", i) for i in range(QSMALL)]
    quant += [("raw", 1), ("stats", 8), ("stats", 9), ("scalars", 1), ("round", 8), ("round", 9)]
    threads = [thread(0), thread(1), quant]
    needs = {("kr:sa", 0): ("ones", 0), ("raw", 1): (f"down0:{M - 1}", 3), ("q:sa", 0): ("round", QSMALL - 1),
             ("ctxk:xb", 0): ("round", QSMALL - 1), ("mlp1:0", 0): ("round", 9), ("ctxz", 2): ("ctxz", 1),
             ("raw", 0): ("ctxk:xa", 1)}
    def lock(st):
        take, give = [], []
        if st in ("exp:xa:0:0", "exp:sa:0:0", "exp:xb:0:0", "mlp0:0", "mlp1:0"):
            take.append("act")
        if st in ("out1:xa", "out1:sa", "out1:xb", f"down0:{M - 1}", f"down1:{M - 1}"):
            give.append("act")
        if st == "v:sa":
            take.append("sa")
        if st == f"val:sa:3:{T - 1}":
            give.append("sa")
        return take, give

    at, ready, held, done_, out = [0, 0, 0], [0.0, 6.0, 20.0], {}, set(), []
    pe = dve = act = 0.0
    while any(at[i] < len(threads[i]) for i in range(3)):
        best = None
        for i in range(3):
            if at[i] == len(threads[i]):
                continue
            st = threads[i][at[i]]
            if needs.get(st, st) not in done_ and st in needs:
                continue
            if any(held.get(x_, i) != i for x_ in lock(st[0])[0]):
                continue
            c = cost(st[0])
            start = max(ready[i], pe) if c[0] else ready[i]
            if best is None or start < best[0]:
                best = (start, i, st, c)
        start, i, st, c = best
        at[i] += 1
        out.append(st)
        done_.add(st)
        take, give = lock(st[0])
        for x_ in take:
            held[x_] = i
        for x_ in give:
            del held[x_]
        if c[0]:
            pe = start + c[0]
        if c[1]:
            dve = max(dve, start) + c[1]
        if c[2]:
            act = max(act, start) + c[2]
        ready[i] = start + max(c[0], c[3])
        slack = 0 if c[3] else SLACK
        if c[1]:
            ready[i] = max(ready[i], dve - slack)
        if c[2]:
            ready[i] = max(ready[i], act - slack)
    return out


ORDER = order()


def heads(h):
    return h // 8 * 4 + h % 8 // 2, h % 2


def bank_uses():
    plan, count, turn = {}, [0] * 8, {"long": 0, "short": 0}

    def use(key, kind="short"):
        first, n = (0, 2) if kind == "long" else (2, 6)
        k = first + turn[kind] % n
        turn[kind] += 1
        plan[key] = (k, count[k])
        count[k] += 1

    for st, b in ORDER:
        name, *rest = st.split(":")
        if name == "ctx":
            use((st, b))
        elif name == "ctxk":
            use((st, b, "K"))
            use((st, b, "V"))
        elif name in ("lt", "q", "k", "out2"):
            for f in range(F):
                use((st, b, f))
        elif name in ("v", "out3"):
            for t2 in range(T // 2):
                use((st, b, t2))
        elif name == "max":
            for i in range(T if rest[0] == "sa" else 2):
                use((st, b, i))
        elif name == "neg":
            use((st, b))
        elif name == "exp":
            inst, qd, kt = rest
            if kt == "0":
                use(("pv", inst, b, int(qd)), "long")
            for j in range(4 if inst == "sa" else 2):
                use((st, b, j))
        elif name == "out1":
            for t in range(T):
                use((st, b, t))
        elif name in ("mlp0", "mlp1"):
            if rest[0] == "0":
                for t2 in range(T // 2):
                    use((name, "acc", b, t2), "long")
            if name == "mlp1":
                use((st, b, "g"))
            use((st, b, "h"))
    return plan


def prob_units():
    units, at = {}, 0
    for st, b in ORDER:
        if st.startswith("exp"):
            _, inst, qd, kt = st.split(":")
            n = 4 if inst == "sa" else 2
            units[(st, b)] = (at, n, inst != "sa" or int(kt) == T - 1)
            at += n
    return units


def program(nc, x, ctx_in, w0_in, w1_in, vec_in, rows_in, out):
    plan = bank_uses()
    units = prob_units()
    NP = 12
    tile_unit, quad_used, used = {}, {}, 0
    for u, (first, n, last) in units.items():
        for k in range(n):
            tile_unit[first + k] = u
        if not last:
            used += 1
        quad_used[u] = used

    top = [(nc.sbuf_base + 63) // 64 * 64]

    def sb(name, shape, dt, at=None):
        size = 4
        for n in shape[1:]:
            size *= n
        size = (size + 31) // 32 * 32
        if at is None:
            at = top[0]
            top[0] += size
        return nc.alloc_sbuf_tensor_at(name, shape, dt, offset=at), at + size

    def new(name, shape, dt=F32):
        return sb(name, shape, dt)[0]

    xs = [new(f"x{i}", [128, T, D]) for i in range(2)]
    rowz = [new(f"rowz{i}", [128, T, D]) for i in range(2)]
    hiT = [new(f"hiT{i}", [128, F, R], F32R) for i in range(2)]
    full_at = top[0]
    loT = [new(f"loT{i}", [128, F, R], F32R) for i in range(2)]
    full_t = [sb(f"full_t{i}", [128, F, R], F32, full_at + i * F * R * 4)[0] for i in range(2)]
    qk_parts = new("qk_parts", [128, 2, 2, R], F32R)
    ctx_z = new("ctx_z", [128, C])
    ctx_hi = new("ctx_hi", [CK, 2, 128], F32R)
    lo_at = top[0]
    ctx_lo = new("ctx_lo", [CK, 2, 128], F32R)
    ctx_full, _ = sb("ctx_full", [CK, 2, 128], F32, lo_at)
    q_stack = [new(f"q_stack{i}", [128, H // 2, R], F32R) for i in range(2)]
    o_raw = new("o_raw", [128, 4, R])
    kc_stack = [new(f"kc_stack{i}", [128, H // 2, 2 * NK], F32R) for i in range(2)]
    vc = [new(f"vc{i}", [128, VN]) for i in range(2)]
    neg_parts = new("neg_parts", [16, 2, R], F32R)
    rows = new("rows", [128, len(ROWS), D])
    vec = new("vec", [128, NV])
    ident = new("ident", [128, 128])
    ctx_rows = [new(f"ctx_rows{i}", [128, C]) for i in range(B)]
    kc_parts = new("kc_parts", [128, 2, 2 * NK], F32R)
    six = [new(f"six{i}", [128, T, 6]) for i in range(2)]
    meanvar = [new(f"meanvar{i}", [128, T, 2]) for i in range(2)]
    vareps = new("vareps", [128, T])
    rstd = [new(f"rstd{i}", [128, T]) for i in range(2)]
    half = new("half", [128, T])
    negmax = [new(f"negmax{i}", [128, T, H]) for i in range(2)]
    rsum = new("rsum", [128, H])
    NQ = len(QN)
    ext = new("ext", [128, 2 * NQ])
    allext = new("allext", [128, 2 * NQ])
    qs = new("qs", [128, 8, NQ])
    qhi = new("qhi", [128, NQ], F32R)
    prods = new("prods", [128, 4])
    ffb = new("ffb", [128, M])
    arena = top[0]
    probs, end = sb("probs", [128, NP, R], F32)
    top[0] = end
    hid_hi, at = sb("hid_hi", [128, 2, R], F32R, arena)
    hid_lo, _ = sb("hid_lo", [128, 2, R], F32R, at)
    hid, at = sb("hid", [128, 2, R], F32, at)
    gate, at = sb("gate", [128, 2, R], F32, at)
    raw_at = top[0]
    raw1a = new("raw1a", [128, SPLIT1])
    wn_a, _ = sb("wn_a", [128, SPLIT1], F32R, raw_at)
    vx = new("vx", [128, T, VN])
    k_stack, _ = sb("k_stack", [128, H // 2, R], F32R, top[0])
    whl = {"att": [new(f"w_att_{p_}", [128, SPLIT0], F32R) for p_ in ("hi", "lo")]}
    raw1b, _ = sb("raw1b", [128, N1 - SPLIT1], F32, top[0])
    wn_b, _ = sb("wn_b", [128, N1 - SPLIT1], F32R, top[0])
    raw0_at = top[0]
    whl["mlp"] = [new(f"w_mlp_{p_}", [128, N0 - SPLIT0], F32R) for p_ in ("hi", "lo")]
    raw0, _ = sb("raw0", [128, N0], F32, arena)

    scr = {}
    for inst in ("xa", "sa", "xb"):
        for b in range(B):
            scr["q", inst, b] = nc.dram_tensor(f"q_{inst}{b}", (D, 3, R), F32, kind="Internal").ap()
            scr["k", inst, b] = nc.dram_tensor(f"k_{inst}{b}", (D, 3, R if inst == "sa" else NK), F32,
                                               kind="Internal").ap()
            scr["n", inst, b] = nc.dram_tensor(f"n_{inst}{b}", (H, 2, R), F32, kind="Internal").ap()
    mid = nc.dram_tensor("mid", (B, R, D), F32, kind="Internal").ap()

    with ExitStack() as stack:
        psum = stack.enter_context(nc.psum_tensor("banks", [128, 8, 512], F32))
        sems = {}

        def S(name):
            if name not in sems:
                sems[name] = stack.enter_context(nc.semaphore(name.replace(":", "_")))
            return sems[name]

        full = [S(f"bank_full{k}") for k in range(8)]
        free = [S(f"bank_free{k}") for k in range(8)]

        def bank(key):
            return psum[:, plan[key][0], :]

        def claim(pe, key):
            k, before = plan[key]
            if before:
                pe.wait_ge(free[k], before)
            return psum[:, k, :]

        def filled(eng, key):
            k, before = plan[key]
            eng.wait_ge(full[k], before + 1)
            return psum[:, k, :]

        def drained(eng, key):
            k, before = plan[key]
            eng.wait_ge(free[k], before + 1)

        def done(key):
            return full[plan[key][0]]

        def release(key):
            return free[plan[key][0]]

        def nth(b, per, j=0):
            return b * per + j + 1

        def weights(name, kt, a, n, rows_=128):
            if name in W0:
                o = OFF0[name] + kt * W0[name][1] + a
                pair, o = (whl["att"], o) if o < SPLIT0 else (whl["mlp"], o - SPLIT0)
                return tuple(p_[0:rows_, o:o + n] for p_ in pair)
            o = OFF1[name] + kt * W1[name][1] + a
            t_, o = (wn_a, o) if o < SPLIT1 else (wn_b, o - SPLIT1)
            return (t_[0:rows_, o:o + n],)

        def split_to(name, part):
            o, m_ = OFF0[name], W0[name][0] * W0[name][1]
            pair, o = (whl["att"], o) if o < SPLIT0 else (whl["mlp"], o - SPLIT0)
            return pair[part][:, o:o + m_]

        def raw1_of(i):
            o, m_ = OFF1[QN[i]], W1[QN[i]][0] * W1[QN[i]][1]
            if o < SPLIT1:
                return raw1a[:, o:o + m_], wn_a[:, o:o + m_]
            return raw1b[:, o - SPLIT1:o - SPLIT1 + m_], wn_b[:, o - SPLIT1:o - SPLIT1 + m_]

        def passes(xp, wp):
            return [(xp[0], wp[0]), (xp[1], wp[0])] + ([(xp[0], wp[1])] if len(wp) == 2 else [])

        def delta(name, parts=128):
            i = QN.index(name)
            return qs[0:parts, 0, i:i + 1]

        def col(name, i, parts=128):
            o = OFFV[name] + i
            return vec[0:parts, o:o + 1]

        def stack_of(inst, b):
            return k_stack if inst == "sa" else kc_stack[b % 2]

        def index_of(*names):
            found = [s_ for s_ in ORDER if s_[0] in names or s_[0].split(":")[0] in names]
            return found, {s_: i for i, s_ in enumerate(found)}

        qk_list, qk_index = index_of("q", "k")
        ctx_list, ctx_index = index_of("ctx")
        z_list, z_index = index_of("ctxz")
        mlp_list, mlp_index = index_of("mlp0", "mlp1")
        neg_list, neg_index = index_of("neg")
        out_list, out_index = index_of("out1")
        sa_list, sa_index = index_of("v")
        ln_index = {}
        for inst in ("a1", "a3", "b1", "b2", "b3"):
            for i, s_ in enumerate(index_of(f"ln:{inst}")[0]):
                ln_index[inst, s_[1]] = i
        q_seen, q_prev, neg_total = {}, {}, {}
        for par_ in range(2):
            qs_ = [s_ for s_ in qk_list if s_[0][:2] == "q:" and s_[1] % 2 == par_]
            for i, (st, b) in enumerate(qs_):
                inst = st.split(":")[1]
                q_seen[inst, b] = i + 1
                q_prev[inst, b] = (qs_[i - 1][0].split(":")[1], qs_[i - 1][1]) if i else None
            for i, (st, b) in enumerate(s_ for s_ in neg_list if s_[1] % 2 == par_):
                neg_total[st.split(":")[1], b] = 16 * 2 * (i + 1)
        q_scaled = {"q:sa": 0, "q:xb": 1}

        def last_use(eng, inst, b):
            filled(eng, ("pv", inst, b, 3))

        def kc_user(b, inst):
            turns = [("xa", b % 2), ("xa", b % 2 + 2), ("xb", b % 2), ("xb", b % 2 + 2)]
            i = turns.index((inst, b))
            return turns[i - 1] if i else None

        def kc_count(inst, b):
            return (0 if inst == "xa" else 2) + b // 2 + 1

        block = stack.enter_context(nc.Block())

        @block.sync
        def _(sp):
            def loaded(dst, src, sem):
                sp.dma_start(dst, src).then_inc(S(sem), 16)

            loaded(raw0[:, 0:OFF0["q"]], w0_in[:, 0:OFF0["q"]], "raw0_kv_loaded")
            for b in range(B):
                for half_ in range(2):
                    loaded(ctx_rows[b][half_ * NK:half_ * NK + NK, :], ctx_in[b], f"ctx_loaded{b}")
                if b == 0:
                    loaded(vec[:], vec_in, "vectors_loaded")
                if b == 1:
                    for i in range(2):
                        loaded(xs[i][:], x[i].rearrange("(t p) d -> p t d", p=128), f"x_loaded{i}")
                    for w in ("q", "proj", "w1", "w2"):
                        o, m_ = OFF0[w], W0[w][0] * W0[w][1]
                        loaded(raw0[:, o:o + m_], w0_in[:, o:o + m_], f"raw0_{w}_loaded")
            for i in range(len(ROWS)):
                loaded(rows[:, i, :], rows_in[i:i + 1, :].broadcast_to([128, D]), "rows_loaded")

            def send(d, parts_of, kind, sem):
                hi_, lo_ = parts_of(0), parts_of(1)
                for slot, part in enumerate((hi_, lo_, hi_) if kind == "q" else (hi_, hi_, lo_)):
                    sp.dma_start(d[:, slot], part).then_inc(S(sem), 16)

            for st, b in ORDER:
                name, *rest = st.split(":")
                if name == "load":
                    layer = int(rest[0])
                    if (layer, b) in ((0, 0), (0, 1)):
                        continue
                    sp.wait_ge(S(f"stored{b % 2}"), 16 * (layer * 2 + b // 2))
                    loaded(xs[b % 2][:], (x if layer == 0 else mid)[b].rearrange("(t p) d -> p t d", p=128),
                           f"x_loaded{b % 2}")
                elif name == "raw":
                    if b == 0:
                        for i in range(QSMALL):
                            loaded(raw1_of(i)[0], w1_in[:, OFF1[QN[i]]:OFF1[QN[i]] + raw1_of(i)[0].shape[1]],
                                   f"raw1_{QN[i]}_loaded")
                    else:
                        filled(sp, ("mlp0", "acc", B - 1, 1))
                        for i in range(QSMALL, NQ):
                            loaded(raw1_of(i)[0], w1_in[:, OFF1[QN[i]]:OFF1[QN[i]] + raw1_of(i)[0].shape[1]],
                                   f"raw1_{QN[i]}_loaded")
                elif name == "ctxk":
                    inst = rest[0]
                    drained(sp, (st, b, "K"))
                    send(scr["k", inst, b].rearrange("(m p) s n -> p s m n", p=128),
                         lambda part: kc_parts[:, part, :].bitcast(F32).rearrange("p (m n) -> p m n", m=2), "k",
                         "kc_sent")
                elif name == "ctxr":
                    inst = rest[0]
                    sp.wait_ge(S("kc_sent"), 48 * (ctx_index[(f"ctx:{inst}", b)] + 1))
                    before = kc_user(b, inst)
                    if before:
                        last_use(sp, *before)
                    else:
                        sp.wait_ge(S("kc_set"), 4)
                    src = scr["k", inst, b].rearrange("(hp par d) s n -> par (d s) hp n", par=2, d=HD)
                    for par in range(2):
                        r = 64 * par
                        sp.dma_start(kc_stack[b % 2][r:r + 3 * HD, :, par * NK:par * NK + NK].bitcast(F32),
                                     src[par]).then_inc(S(f"kc_stacked{b % 2}"), 16)
                elif name in ("q", "k"):
                    for m in range(F):
                        drained(sp, (st, b, m))
                    send(scr[name, rest[0], b].rearrange("(m p) s n -> p s m n", p=128),
                         lambda part: qk_parts[:, :, part, :].bitcast(F32), name, "qk_sent")
                elif name in ("qr", "kr"):
                    inst = rest[0]
                    sp.wait_ge(S("qk_sent"), 48 * (qk_index[(st[0] + st[2:], b)] + 1))
                    src = scr[name[0], inst, b].rearrange("(hp par d) s n -> par (d s) hp n", par=2, d=HD)
                    if name == "qr":
                        if q_prev[inst, b]:
                            last_use(sp, *q_prev[inst, b])
                        else:
                            sp.wait_ge(S("pool_set"), 4)
                        dst, sem = q_stack[b % 2], f"q_stacked{b % 2}"
                    else:
                        i = sa_index[("v:sa", b)]
                        if i:
                            last_use(sp, "sa", sa_list[i - 1][1])
                        sp.wait_ge(S("ones_set"), 3)
                        dst, sem = k_stack, "k_stacked"
                    for par in range(2):
                        r = 64 * par
                        sp.dma_start(dst[r:r + 3 * HD, :, :].bitcast(F32), src[par]).then_inc(S(sem), 16)
                elif name == "neg":
                    inst, g = rest[0], int(rest[1])
                    n = 8 if inst == "sa" else 16
                    drained(sp, (st, b))
                    sp.dma_start(scr["n", inst, b][g * 8:g * 8 + n],
                                 neg_parts[0:n, :, :].bitcast(F32)).then_inc(S("neg_sent"), 16)
                elif name == "negr":
                    inst, g = rest[0], int(rest[1])
                    n = 8 if inst == "sa" else 16
                    sp.wait_ge(S("neg_sent"), 16 * (neg_index[(f"neg:{inst}:{g}", b)] + 1))
                    src = scr["n", inst, b][g * 8:g * 8 + n].rearrange("(par hp) q n -> par q hp n", par=2)
                    for par in range(2):
                        r = 64 * par + 3 * HD
                        sp.dma_start(q_stack[b % 2][r:r + 2, g * 4:g * 4 + n // 2, :].bitcast(F32),
                                     src[par]).then_inc(S(f"neg_stacked{b % 2}"), 16)
                elif name in ("store0", "store1"):
                    for t2 in range(T // 2):
                        drained(sp, (f"mlp{name[-1]}", "acc", b, t2))
                    sp.dma_start((mid if name == "store0" else out)[b].rearrange("(t p) d -> p t d", p=128),
                                 xs[b % 2][:]).then_inc(S(f"stored{b % 2}"), 16)
            for i in range(2):
                sp.wait_ge(S(f"stored{i}"), 16 * 4)

        @block.gpsimd
        def _(pool):
            nc.gpsimd.memset(ident[:], 0.0).then_inc(S("ident_zero"), 1)
            nc.gpsimd.memset(half[:], -0.5).then_inc(S("ident_zero"), 1)
            pool.wait_ge(S("ident_zero"), 2)
            nc.gpsimd.affine_select(out=ident[:], in_=ident[:], compare_op=ALU.not_equal, fill=1.0, base=0,
                                    pattern=[[-1, 128]], channel_multiplier=1).then_inc(S("ident_ready"), 1)
            for i in range(2):
                nc.gpsimd.memset(vc[i][:], 1.0).then_inc(S("pool_set"), 1)
            nc.gpsimd.memset(vx[:], 1.0).then_inc(S("ones_set"), 1)
            for i in range(2):
                nc.gpsimd.memset(q_stack[i][:].bitcast(F32), 0.0).then_inc(S("pool_set"), 1)

            def power(b, ready, n, var, out_, t):
                pool.wait_ge(ready, n)
                nc.gpsimd.tensor_scalar(vareps[:, 0:t], var, EPS, 1.0, ALU.add, ALU.mult).then_inc(S("vareps"), 1)
                power.n += 1
                pool.wait_ge(S("vareps"), power.n)
                return nc.gpsimd.tensor_tensor(out_, vareps[:, 0:t], half[:, 0:t], ALU.pow)

            power.n = 0
            step_n = chunks = 0
            for st, b in ORDER:
                name, *rest = st.split(":")
                if name == "ctxz":
                    i = z_index[(st, b)]
                    power(b, S("ctx_mean"), i + 1, meanvar[b % 2][:, 0:1, 1], rstd[b % 2][:, 0:1], 1).then_inc(
                        S("ctx_rstd"), 1)
                elif name == "ln":
                    inst = rest[0]
                    i = ln_index[inst, b]
                    power(b, S(f"{inst}_mean"), T * (i + 1), meanvar[b % 2][:, :, 1], rstd[b % 2][:],
                          T).then_inc(S(f"{inst}_rstd"), 1)
                    if i == 0 and inst == "a1":
                        pool.wait_ge(S("rows_loaded"), 16 * len(ROWS))
                    pool.wait_ge(S(f"{inst}_rowz"), T * (i + 1))
                    r = ROWS.index(BIAS_AFTER[inst])
                    for t in range(T):
                        nc.gpsimd.tensor_tensor(xs[b % 2][:, t, :], xs[b % 2][:, t, :], rows[:, r, :],
                                                ALU.add).then_inc(S(f"{inst}_biased"), 1)
                    last_biased = (inst, i)
                elif name == "scalars":
                    pool.wait_ge(S("extremes"), 2 * (QSMALL if b == 0 else NQ))
                    if b:
                        pool.wait_ge(S("quant_scalars"), 1)
                    nc.gpsimd.partition_all_reduce(allext[:], ext[:], 128,
                                                   bass.bass_isa.ReduceOp.max).then_inc(S("extremes_all"), 1)
                elif name == "round":
                    raw, ints = raw1_of(b)
                    pool.wait_ge(S("quant_scalars"), 1 if b < QSMALL else 2)
                    for a in range(0, raw.shape[1], 2 * R):
                        n = min(2 * R, raw.shape[1] - a)
                        v = raw[:, a:a + n]
                        nc.gpsimd.tensor_scalar(v, v, qs[:, 1, b:b + 1], MAGIC, ALU.mult, ALU.add).then_inc(
                            S("round_step"), 1)
                        pool.wait_ge(S("round_step"), step_n + 1)
                        nc.gpsimd.tensor_scalar(v, v, qs[:, 3, b:b + 1], qs[:, 4, b:b + 1], ALU.max,
                                                ALU.min).then_inc(S("round_step"), 1)
                        step_n += 2
                        chunks += 1
                        pool.wait_ge(S("round_step"), step_n)
                        nc.gpsimd.tensor_scalar(ints[:, a:a + n], v, -MAGIC, None, ALU.add).then_inc(
                            S("integers"), 1)
                elif name == "ones":
                    filled(pool, ("out3:xa", B - 1, 1))
                    pool.wait_ge(S(f"{last_biased[0]}_biased"), T * (last_biased[1] + 1))
                    pool.wait_ge(S("integers"), chunks)
                    for par in range(2):
                        nc.gpsimd.memset(k_stack[64 * par + 32:64 * par + 64, :, :].bitcast(F32), 1.0).then_inc(
                            S("ones_set"), 1)
                        pool.wait_ge(S("ones_set"), 2 + par)

        @block.tensor
        def _(pe):
            def product(out_, pairs, lhs_is_w):
                for i, (xp, wp) in enumerate(pairs):
                    lhs, rhs = (wp, xp) if lhs_is_w else (xp, wp)
                    last = nc.tensor.matmul(out_, lhs, rhs, start=(i == 0), stop=(i == len(pairs) - 1))
                return last

            def parts(b, kt, a, n):
                return (hiT[b % 2][:, kt, a:a + n], loT[b % 2][:, kt, a:a + n])

            def wait_weights(name):
                if name in W0:
                    pe.wait_ge(S("w0_split"), list(W0).index(name) + 1)
                else:
                    pe.wait_ge(S("integers"), sum(-(-W1[w][0] * W1[w][1] // (2 * R))
                                                  for w in QN[:QN.index(name) + 1]))

            pe.wait_ge(S("ident_ready"), 1)
            for st, b in ORDER:
                name, *rest = st.split(":")
                if name == "ctx":
                    o = claim(pe, (st, b))
                    if rest[0] == "xa":
                        pe.wait_ge(S("ctx_z"), z_index[("ctxz", b)] + 1)
                        src = ctx_z
                    else:
                        pe.wait_ge(S(f"ctx_loaded{b}"), 32)
                        src = ctx_rows[b]
                    for kt in range(2):
                        mm = nc.tensor.transpose(o[0:CK, kt * 128:kt * 128 + 128], src[:, kt * CK:kt * CK + CK],
                                                 ident[:])
                    mm.then_inc(done((st, b)), 1)
                elif name == "ctxk":
                    wk, wv, va = ("kv", "kv", D) if rest[0] == "xa" else ("k2", "v2", 0)
                    o = claim(pe, (st, b, "K"))
                    pe.wait_ge(S("ctx_lo"), ctx_index[(f"ctx:{rest[0]}", b)] + 1)
                    wait_weights(wk)
                    for m in range(2):
                        pairs = []
                        for kt in range(2):
                            xp = (ctx_hi[:, kt, 0:NK], ctx_lo[:, kt, 0:NK])
                            pairs += passes(xp, weights(wk, kt, m * 128, 128, CK))
                        mm = product(o[:, m * NK:m * NK + NK], pairs, True)
                    mm.then_inc(done((st, b, "K")), 1)
                    o = claim(pe, (st, b, "V"))
                    wait_weights(wv)
                    pairs = []
                    for kt in range(2):
                        pairs += passes((ctx_hi[:, kt, :], ctx_lo[:, kt, :]), weights(wv, kt, va, D, CK))
                    product(o[:, 0:D], pairs, False).then_inc(done((st, b, "V")), 1)
                elif name == "lt":
                    inst = rest[0]
                    pe.wait_ge(S(f"{inst}_rowz"), T * (ln_index[inst, b] + 1))
                    for f in range(F):
                        o = claim(pe, (st, b, f))
                        for t in range(T):
                            mm = nc.tensor.transpose(o[:, t * 128:t * 128 + 128],
                                                     rowz[b % 2][:, t, f * 128:f * 128 + 128], ident[:])
                        mm.then_inc(done((st, b, f)), 1)
                elif name in ("q", "k"):
                    w = {"q:xa": "q", "q:sa": "q1", "k:sa": "k1", "q:xb": "q2"}[st]
                    wait_weights(w)
                    inst = LN_OF[rest[0]]
                    pe.wait_ge(S(f"{inst}_loT"), F * (ln_index[inst, b] + 1))
                    for m in range(F):
                        o = claim(pe, (st, b, m))
                        pairs = []
                        for kt in range(F):
                            pairs += passes(parts(b, kt, 0, R), weights(w, kt, m * 128, 128))
                        product(o, pairs, True).then_inc(done((st, b, m)), 1)
                elif name == "v":
                    wait_weights("v1")
                    for t2 in range(T // 2):
                        o = claim(pe, (st, b, t2))
                        for i in range(2):
                            pairs = []
                            for kt in range(F):
                                pairs += passes(parts(b, kt, (2 * t2 + i) * 128, 128), weights("v1", kt, 0, D))
                            mm = product(o[:, i * D:i * D + D], pairs, False)
                        mm.then_inc(done((st, b, t2)), 1)
                elif name == "max":
                    inst, i = rest[0], int(rest[1])
                    pe.wait_ge(S(f"q_stacked{b % 2}"), 32 * q_seen[inst, b])
                    ks = stack_of(inst, b)
                    if inst == "sa":
                        pe.wait_ge(S("k_stacked"), 32 * (sa_index[("v:sa", b)] + 1))
                        hp, par = heads(i)
                        r = 64 * par
                        for t in range(T):
                            o = claim(pe, (st, b, t))
                            nc.tensor.matmul(o, q_stack[b % 2][r:r + 3 * HD, hp, t * 128:t * 128 + 128],
                                             ks[r:r + 3 * HD, hp, :], start=True, stop=True,
                                             tile_position=(r, 0)).then_inc(done((st, b, t)), 1)
                    else:
                        pe.wait_ge(S(f"kc_stacked{b % 2}"), 32 * kc_count(inst, b))
                        for par in range(2):
                            r = 64 * par
                            o = claim(pe, (st, b, par))
                            for hp in range(H // 2):
                                mm = nc.tensor.matmul(o[:, hp * NK:hp * NK + NK],
                                                      q_stack[b % 2][r:r + 3 * HD, hp, i * 128:i * 128 + 128],
                                                      ks[r:r + 3 * HD, hp, par * NK:par * NK + NK],
                                                      start=True, stop=True, tile_position=(r, 0))
                            mm.then_inc(done((st, b, par)), 1)
                elif name == "neg":
                    inst, g = rest[0], int(rest[1])
                    n = 8 if inst == "sa" else 16
                    o = claim(pe, (st, b))
                    drained(pe, (f"max:sa:{g * 8 + 7}", b, T - 1) if inst == "sa" else (f"max:{inst}:{T - 1}", b, 1))
                    for t in range(T):
                        mm = nc.tensor.transpose(o[0:n, t * 128:t * 128 + 128], negmax[b % 2][:, t, g * 8:g * 8 + n],
                                                 ident[:])
                    mm.then_inc(done((st, b)), 1)
                elif name == "exp":
                    inst, qd, kt = rest[0], int(rest[1]), int(rest[2])
                    ks = stack_of(inst, b)
                    behind = 32 if inst == "sa" and qd < 2 else 0
                    pe.wait_ge(S(f"neg_stacked{b % 2}"), neg_total[inst, b] - behind)
                    for j in range(4 if inst == "sa" else 2):
                        o = claim(pe, (st, b, j))
                        if inst == "sa":
                            hp, r = 2 * qd + j // 2, 64 * (j % 2)
                            nc.tensor.matmul(o, ks[r:r + 3 * HD + 2, hp, kt * 128:kt * 128 + 128],
                                             q_stack[b % 2][r:r + 3 * HD + 2, hp, :], start=True, stop=True,
                                             tile_position=(r, 0)).then_inc(done((st, b, j)), 1)
                        else:
                            nc.tensor.matmul(o, ks[:, 2 * qd + j, :], q_stack[b % 2][:, 2 * qd + j, :],
                                             start=True, stop=True).then_inc(done((st, b, j)), 1)
                elif name == "val":
                    inst, qd, kt = rest[0], int(rest[1]), int(rest[2])
                    unit = (f"exp:{inst}:{qd}:{kt}", b)
                    first, n, last = units[unit]
                    pv = ("pv", inst, b, qd)
                    if kt == 0:
                        claim(pe, pv)
                        if qd == 0:
                            pe.wait_ge(S("pool_set"), 4)
                            pe.wait_ge(S("ones_set"), 1)
                            for key in ([("v:sa", b, t2) for t2 in range(T // 2)] if inst == "sa" else
                                        [(f"ctxk:{inst}", b, "V")]):
                                drained(pe, key)
                    drained(pe, (*unit, n - 1))
                    for j in range(4):
                        h = 4 * qd + j
                        if inst == "sa":
                            r, lhs, rhs = 0, vx[:, kt, h * VS:h * VS + VW], probs[:, (first + j) % NP, :]
                        else:
                            r = NK * (j % 2)
                            lhs = vc[b % 2][r:r + NK, h * VS:h * VS + VW]
                            rhs = probs[r:r + NK, (first + j // 2) % NP, :]
                        mm = nc.tensor.matmul(bank(pv)[VW * j:VW * j + VW, :], lhs, rhs, start=(kt == 0), stop=last,
                                              tile_position=(r, VW * j))
                    mm.then_inc(done(pv) if last else S("probs_used"), 1)
                elif name == "out1":
                    inst = rest[0]
                    for t in range(T):
                        o = claim(pe, (st, b, t))
                        for qd in range(4):
                            drained(pe, ("pv", inst, b, qd))
                            mm = nc.tensor.transpose(o[:, qd * 128:qd * 128 + 128],
                                                     o_raw[:, qd, t * 128:t * 128 + 128], ident[:])
                        mm.then_inc(done((st, b, t)), 1)
                elif name == "out2":
                    inst = rest[0]
                    for t in range(T):
                        drained(pe, (f"out1:{inst}", b, t))
                    for f in range(F):
                        o = claim(pe, (st, b, f))
                        for t in range(T):
                            mm = nc.tensor.transpose(o[:, t * 128:t * 128 + 128],
                                                     rowz[b % 2][:, t, f * 128:f * 128 + 128], ident[:])
                        mm.then_inc(done((st, b, f)), 1)
                elif name == "out3":
                    inst = rest[0]
                    w = PROJ[inst]
                    wait_weights(w)
                    for f in range(F):
                        drained(pe, (f"out2:{inst}", b, f))
                    for t2 in range(T // 2):
                        o = claim(pe, (st, b, t2))
                        for i in range(2):
                            pairs = []
                            for kt in range(F):
                                pairs += passes(parts(b, kt, (2 * t2 + i) * 128, 128), weights(w, kt, 0, D))
                            mm = product(o[:, i * D:i * D + D], pairs, False)
                        mm.then_inc(done((st, b, t2)), 1)
                elif name in ("mlp0", "mlp1"):
                    m = int(rest[0])
                    wu, ln = ("w1", "a3") if name == "mlp0" else ("ff1", "b3")
                    wait_weights(wu)
                    pe.wait_ge(S(f"{ln}_loT"), F * (ln_index[ln, b] + 1))
                    for kind in ("h",) if name == "mlp0" else ("g", "h"):
                        a = m * 128 + (HID if kind == "g" else 0)
                        o = claim(pe, (st, b, kind))
                        pairs = []
                        for kt in range(F):
                            pairs += passes(parts(b, kt, 0, R), weights(wu, kt, a, 128))
                        product(o, pairs, True).then_inc(done((st, b, kind)), 1)
                elif name in ("down0", "down1"):
                    m = int(rest[0])
                    mlp, wd = (("mlp0", "w2"), ("mlp1", "ff2"))[int(name[-1])]
                    if m == 0:
                        for t2 in range(T // 2):
                            claim(pe, (mlp, "acc", b, t2))
                        wait_weights(wd)
                    u = mlp_index[(f"{mlp}:{m}", b)]
                    pe.wait_ge(S("hid_lo"), u + 1)
                    hp_ = (hid_hi[:, u % 2, :], hid_lo[:, u % 2, :])
                    for t in range(T):
                        o = bank((mlp, "acc", b, t // 2))[:, (t % 2) * D:(t % 2) * D + D]
                        ps_ = passes(tuple(p_[:, t * 128:t * 128 + 128] for p_ in hp_), weights(wd, m, 0, D))
                        for i, (a_, w_) in enumerate(ps_):
                            mm = nc.tensor.matmul(o, a_, w_, start=(m == 0 and i == 0 and t % 2 == 0),
                                                  stop=(m == M - 1 and i == len(ps_) - 1), skip_group_check=True)
                        if m == M - 1 and t % 2 == 1:
                            mm.then_inc(done((mlp, "acc", b, t // 2)), 1)

        @block.scalar
        def _(act):
            def split0(i):
                w = list(W0)[i]
                o, m_ = OFF0[w], W0[w][0] * W0[w][1]
                act.wait_ge(S(f"raw0_{w}_loaded"), 16)
                nc.scalar.copy(split_to(w, 0), raw0[:, o:o + m_]).then_inc(S("w0_hi"), 1)

            split0(0)
            act.wait_ge(S("vectors_loaded"), 16)
            for st, b in ORDER:
                name, *rest = st.split(":")
                if name == "ctx":
                    n = ctx_index[(st, b)]
                    o = filled(act, (st, b))
                    if n:
                        pst, pb = ctx_list[n - 1]
                        filled(act, (pst.replace("ctx", "ctxk"), pb, "V"))
                    for kt in range(2):
                        src = o[0:CK, kt * 128:kt * 128 + 128]
                        if rest[0] == "xa":
                            ins = nc.scalar.activation(ctx_full[:, kt, :], src, ACT.Identity,
                                                       bias=col("a2_b", kt, CK), scale=col("a2_g", kt, CK))
                        else:
                            ins = nc.scalar.copy(ctx_full[:, kt, :], src)
                    ins.then_inc(release((st, b)), 1)
                    drained(act, (st, b))
                    nc.scalar.copy(ctx_hi[:], ctx_full[:]).then_inc(S("ctx_hi"), 1)
                elif name == "ctxk":
                    inst = rest[0]
                    n = ctx_index[(f"ctx:{inst}", b)]
                    o = filled(act, (st, b, "K"))
                    if n:
                        act.wait_ge(S("kc_sent"), 48 * n)
                    nc.scalar.copy(kc_parts[:, 0, :], o[:, 0:2 * NK]).then_inc(S("kc_hi"), 1)
                    o = filled(act, (st, b, "V"))
                    before = kc_user(b, inst)
                    if before:
                        last_use(act, *before)
                    else:
                        act.wait_ge(S("pool_set"), 2)
                    v_ = vc[b % 2][:, 0:H * VS].rearrange("p (h e) -> p h e", e=VS)[:, :, 0:HD]
                    src = o[:, 0:D].rearrange("p (h d) -> p h d", d=HD)
                    if inst == "xa":
                        nc.scalar.copy(v_, src).then_inc(release((st, b, "V")), 1)
                    else:
                        nc.scalar.mul(v_, src, delta("v2")).then_inc(release((st, b, "V")), 1)
                    if (inst, b) in (("xa", 0), ("xa", 1)):
                        for i in ((1, 2), (3, 4))[b]:
                            split0(i)
                elif name == "lt":
                    inst = rest[0]
                    for f in range(F):
                        o = filled(act, (st, b, f))
                        nc.scalar.activation(full_t[b % 2][:, f, :], o, ACT.Identity, bias=col(f"{inst}_b", f),
                                             scale=col(f"{inst}_g", f)).then_inc(release((st, b, f)), 1)
                        drained(act, (st, b, f))
                        nc.scalar.copy(hiT[b % 2][:, f, :], full_t[b % 2][:, f, :]).then_inc(S(f"{inst}_hiT"), 1)
                elif name in ("q", "k"):
                    i = qk_index[(st, b)]
                    for m in range(F):
                        o = filled(act, (st, b, m))
                        if i and m == 0:
                            act.wait_ge(S("qk_sent"), 48 * i)
                        if st in q_scaled:
                            nc.scalar.mul(qk_parts[:, m, 0, :], o, prods[:, q_scaled[st]:q_scaled[st] + 1]).then_inc(
                                S("qk_hi"), 1)
                        else:
                            nc.scalar.copy(qk_parts[:, m, 0, :], o).then_inc(S("qk_hi"), 1)
                elif name == "v":
                    i = sa_index[(st, b)]
                    if i:
                        last_use(act, "sa", sa_list[i - 1][1])
                    else:
                        act.wait_ge(S("ones_set"), 1)
                    for t2 in range(T // 2):
                        o = filled(act, (st, b, t2))
                        nc.scalar.mul(vx[:, 2 * t2:2 * t2 + 2, 0:H * VS].rearrange(
                                          "p t (h e) -> p t h e", e=VS)[:, :, :, 0:HD],
                                      o.rearrange("p (t h d) -> p t h d", t=2, d=HD),
                                      delta("v1")).then_inc(release((st, b, t2)), 1)
                elif name == "neg":
                    n = 8 if rest[0] == "sa" else 16
                    i = neg_index[(st, b)]
                    o = filled(act, (st, b))
                    if i:
                        act.wait_ge(S("neg_sent"), 16 * i)
                    nc.scalar.copy(neg_parts[0:n, 0, :], o[0:n, :]).then_inc(S("neg_hi"), 1)
                elif name == "exp":
                    first, n, _last = units[(st, b)]
                    if first == 0:
                        act.wait_ge(S("w0_split"), len(W0))
                    for j in range(n):
                        tile = first + j
                        o = filled(act, (st, b, j))
                        if tile >= NP:
                            u = tile_unit[tile - NP]
                            if units[u][2]:
                                last_of = u[0].split(":")
                                filled(act, ("pv", last_of[1], u[1], int(last_of[2])))
                            else:
                                act.wait_ge(S("probs_used"), quad_used[u])
                        nc.scalar.activation(probs[:, tile % NP, :], o, ACT.Exp, scale=SCALE).then_inc(
                            release((st, b, j)), 1)
                elif name == "val":
                    inst, qd, kt = rest[0], int(rest[1]), int(rest[2])
                    if units[(f"exp:{inst}:{qd}:{kt}", b)][2]:
                        o = filled(act, ("pv", inst, b, qd))
                        nc.scalar.copy(o_raw[:, qd, :], o).then_inc(release(("pv", inst, b, qd)), 1)
                elif name == "out2":
                    for f in range(F):
                        o = filled(act, (st, b, f))
                        nc.scalar.copy(hiT[b % 2][:, f, :], o).then_inc(S("o_hiT"), 1)
                elif name in ("mlp0", "mlp1"):
                    m = int(rest[0])
                    u = mlp_index[(st, b)]
                    s_ = u % 2
                    if name == "mlp0":
                        o = filled(act, (st, b, "h"))
                        nc.scalar.activation(hid[:, s_, :], o, ACT.Gelu, bias=col("mlp0_b", m)).then_inc(
                            release((st, b, "h")), 1)
                    else:
                        o = filled(act, (st, b, "g"))
                        if m >= 2:
                            drained(act, (*mlp_list[u - 2], "h"))
                        nc.scalar.activation(gate[:, s_, :], o, ACT.Gelu_apprx_tanh,
                                             bias=col("ff1_b", M + m), scale=delta("ff1")).then_inc(
                            release((st, b, "g")), 1)
                    drained(act, (st, b, "h"))
                    nc.scalar.copy(hid_hi[:, s_, :], hid[:, s_, :]).then_inc(S("hid_hi"), 1)

        @block.vector
        def _(dve):
            def split0(i):
                w = list(W0)[i]
                o, m_ = OFF0[w], W0[w][0] * W0[w][1]
                dve.wait_ge(S("w0_hi"), i + 1)
                nc.vector.tensor_tensor(split_to(w, 1), raw0[:, o:o + m_], split_to(w, 0),
                                        ALU.subtract).then_inc(S("w0_split"), 1)

            for i in range(2):
                nc.vector.memset(kc_stack[i][:].bitcast(F32), 0.0).then_inc(S("kc_zero"), 1)
                dve.wait_ge(S("kc_zero"), i + 1)
                for par in range(2):
                    nc.vector.memset(kc_stack[i][64 * par + 32:64 * par + 64, :, par * NK:par * NK + NK].bitcast(F32),
                                     1.0).then_inc(S("kc_set"), 1)
            steps = [0]
            nc.vector.memset(ext[:], -3.0e38).then_inc(S("ext_set"), 1)
            split0(0)
            for st, b in ORDER:
                name, *rest = st.split(":")
                if name == "ctxz":
                    i = z_index[(st, b)]
                    cr = ctx_rows[b]
                    dve.wait_ge(S(f"ctx_loaded{b}"), 32)
                    nc.vector.bn_stats(six[b % 2][:, 0, :], cr[:]).then_inc(S("ctx_six"), 1)
                    dve.wait_ge(S("ctx_six"), i + 1)
                    nc.vector.bn_aggr(meanvar[b % 2][:, 0, :], six[b % 2][:, 0, :]).then_inc(S("ctx_mean"), 1)
                    dve.wait_ge(S("ctx_rstd"), i + 1)
                    if i:
                        filled(dve, ("ctx:xa", z_list[i - 1][1]))
                    nc.vector.tensor_scalar(ctx_z[:], cr[:], meanvar[b % 2][:, 0, 0:1], rstd[b % 2][:, 0:1],
                                            ALU.subtract, ALU.mult).then_inc(S("ctx_z"), 1)
                elif name == "ctx":
                    dve.wait_ge(S("ctx_hi"), ctx_index[(st, b)] + 1)
                    nc.vector.tensor_tensor(ctx_lo[:], ctx_full[:], ctx_hi[:], ALU.subtract).then_inc(S("ctx_lo"), 1)
                elif name == "ctxk":
                    dve.wait_ge(S("kc_hi"), ctx_index[(f"ctx:{rest[0]}", b)] + 1)
                    o = filled(dve, (st, b, "K"))
                    nc.vector.tensor_tensor(kc_parts[:, 1, :], o[:, 0:2 * NK], kc_parts[:, 0, :],
                                            ALU.subtract).then_inc(release((st, b, "K")), 1)
                    if (rest[0], b) in (("xa", 0), ("xa", 1)):
                        for i in ((1, 2), (3, 4))[b]:
                            split0(i)
                elif name == "ln":
                    inst = rest[0]
                    i = ln_index[inst, b]
                    xb = xs[b % 2]
                    if inst in ("a1", "b1"):
                        dve.wait_ge(S(f"x_loaded{b % 2}"), 16 * ((0 if inst == "a1" else 2) + b // 2 + 1))
                    else:
                        att = {"a3": "xa", "b2": "sa", "b3": "xb"}[inst]
                        for t2 in range(T // 2):
                            drained(dve, (f"out3:{att}", b, t2))
                    for t in range(T):
                        nc.vector.bn_stats(six[b % 2][:, t, :], xb[:, t, :]).then_inc(S(f"{inst}_six"), 1)
                    for t in range(T):
                        dve.wait_ge(S(f"{inst}_six"), T * i + t + 1)
                        nc.vector.bn_aggr(meanvar[b % 2][:, t, :], six[b % 2][:, t, :]).then_inc(
                            S(f"{inst}_mean"), 1)
                    dve.wait_ge(S(f"{inst}_rstd"), i + 1)
                    for t in range(T):
                        nc.vector.tensor_scalar(rowz[b % 2][:, t, :], xb[:, t, :], meanvar[b % 2][:, t, 0:1],
                                                rstd[b % 2][:, t:t + 1], ALU.subtract, ALU.mult).then_inc(
                            S(f"{inst}_rowz"), 1)
                elif name == "lt":
                    inst = rest[0]
                    for f in range(F):
                        dve.wait_ge(S(f"{inst}_hiT"), F * ln_index[inst, b] + f + 1)
                        nc.vector.tensor_tensor(loT[b % 2][:, f, :], full_t[b % 2][:, f, :], hiT[b % 2][:, f, :],
                                                ALU.subtract).then_inc(S(f"{inst}_loT"), 1)
                elif name in ("q", "k"):
                    i = qk_index[(st, b)]
                    for m in range(F):
                        dve.wait_ge(S("qk_hi"), F * i + m + 1)
                        o = filled(dve, (st, b, m))
                        hi_ = qk_parts[:, m, 0, :]
                        if st in q_scaled:
                            ins = nc.vector.scalar_tensor_tensor(
                                out=qk_parts[:, m, 1, :], in0=o, scalar=prods[:, q_scaled[st]:q_scaled[st] + 1],
                                in1=hi_, op0=ALU.mult, op1=ALU.subtract)
                        else:
                            ins = nc.vector.tensor_tensor(qk_parts[:, m, 1, :], o, hi_, ALU.subtract)
                        ins.then_inc(release((st, b, m)), 1)
                elif name == "max":
                    i = int(rest[1])
                    nm = negmax[b % 2]
                    if rest[0] == "sa":
                        hp, par = heads(i)
                        c = hp // 4 * 8 + par * 4 + hp % 4
                        for t in range(T):
                            o = filled(dve, (st, b, t))
                            nc.vector.tensor_reduce(nm[:, t, c:c + 1], o, AX.X, ALU.max, negate=True).then_inc(
                                release((st, b, t)), 1)
                    else:
                        for par in range(2):
                            o = filled(dve, (st, b, par))
                            nc.vector.tensor_reduce(nm[:, i, par * 8:par * 8 + 8],
                                                    o.rearrange("p (h k) -> p h k", k=NK), AX.X, ALU.max,
                                                    negate=True).then_inc(release((st, b, par)), 1)
                elif name == "neg":
                    n = 8 if rest[0] == "sa" else 16
                    dve.wait_ge(S("neg_hi"), neg_index[(st, b)] + 1)
                    o = filled(dve, (st, b))
                    nc.vector.tensor_tensor(neg_parts[0:n, 1, :], o[0:n, :], neg_parts[0:n, 0, :],
                                            ALU.subtract).then_inc(release((st, b)), 1)
                elif name == "out1":
                    for t in range(T):
                        o = filled(dve, (st, b, t)).rearrange("p (h e) -> p h e", e=VW)
                        n = out_index[(st, b)] * T + t
                        if n:
                            pst, pb = (st, b) if t else out_list[out_index[(st, b)] - 1]
                            drained(dve, (pst, pb, (t - 1) % T))
                        nc.vector.reciprocal(rsum[:], o[:, :, HD]).then_inc(S("rsum"), 1)
                        dve.wait_ge(S("rsum"), n + 1)
                        nc.vector.tensor_tensor(rowz[b % 2][:, t, :].rearrange("p (h d) -> p h d", d=HD),
                                                o[:, :, 0:HD], rsum[:].unsqueeze(2).broadcast_to([128, H, HD]),
                                                ALU.mult).then_inc(release((st, b, t)), 1)
                elif name == "out2":
                    n = out_index[(st.replace("out2", "out1"), b)]
                    for f in range(F):
                        dve.wait_ge(S("o_hiT"), F * n + f + 1)
                        o = filled(dve, (st, b, f))
                        nc.vector.tensor_tensor(loT[b % 2][:, f, :], o, hiT[b % 2][:, f, :], ALU.subtract).then_inc(
                            release((st, b, f)), 1)
                elif name == "out3":
                    inst = rest[0]
                    ln = LN_OF[inst]
                    dve.wait_ge(S(f"{ln}_biased"), T * (ln_index[ln, b] + 1))
                    for t2 in range(T // 2):
                        o = filled(dve, (st, b, t2)).rearrange("p (t d) -> p t d", t=2)
                        x2 = xs[b % 2][:, 2 * t2:2 * t2 + 2, :]
                        if inst == "xa":
                            ins = nc.vector.tensor_tensor(x2, o, x2, ALU.add)
                        else:
                            ins = nc.vector.scalar_tensor_tensor(out=x2, in0=o, scalar=delta(PROJ[inst]), in1=x2,
                                                                 op0=ALU.mult, op1=ALU.add)
                        ins.then_inc(release((st, b, t2)), 1)
                elif name in ("mlp0", "mlp1"):
                    m = int(rest[0])
                    u = mlp_index[(st, b)]
                    s_ = u % 2
                    if name == "mlp1":
                        o = filled(dve, (st, b, "h"))
                        drained(dve, (st, b, "g"))
                        nc.vector.scalar_tensor_tensor(out=hid[:, s_, :], in0=o, scalar=ffb[:, m:m + 1],
                                                       in1=gate[:, s_, :], op0=ALU.add, op1=ALU.mult).then_inc(
                            release((st, b, "h")), 1)
                    dve.wait_ge(S("hid_hi"), u + 1)
                    nc.vector.tensor_tensor(hid_lo[:, s_, :], hid[:, s_, :], hid_hi[:, s_, :],
                                            ALU.subtract).then_inc(S("hid_lo"), 1)
                elif name in ("down0", "down1") and int(rest[0]) == M - 1:
                    mlp, ln = (("mlp0", "a3"), ("mlp1", "b3"))[int(name[-1])]
                    dve.wait_ge(S(f"{ln}_biased"), T * (ln_index[ln, b] + 1))
                    for t2 in range(T // 2):
                        o = filled(dve, (mlp, "acc", b, t2)).rearrange("p (t d) -> p t d", t=2)
                        x2 = xs[b % 2][:, 2 * t2:2 * t2 + 2, :]
                        if mlp == "mlp0":
                            ins = nc.vector.tensor_tensor(x2, o, x2, ALU.add)
                        else:
                            ins = nc.vector.scalar_tensor_tensor(out=x2, in0=o, scalar=prods[:, 2:3], in1=x2,
                                                                 op0=ALU.mult, op1=ALU.add)
                        ins.then_inc(release((mlp, "acc", b, t2)), 1)
                elif name == "stats":
                    w = QN[b]
                    raw, _ints = raw1_of(b)
                    p_ = CK if w in ("k2", "v2") else 128
                    dve.wait_ge(S(f"raw1_{w}_loaded"), 16)
                    nc.vector.tensor_reduce(ext[0:p_, b:b + 1], raw[0:p_, :], AX.X, ALU.max).then_inc(
                        S("extremes"), 1)
                    nc.vector.tensor_reduce(ext[0:p_, NQ + b:NQ + b + 1], raw[0:p_, :], AX.X, ALU.min,
                                            negate=True).then_inc(S("extremes"), 1)
                elif name == "scalars":
                    dve.wait_ge(S("extremes_all"), b + 1)
                    lo_, hi_ = ((0, QSMALL), (QSMALL, NQ))[b]
                    def step(ins):
                        ins.then_inc(S("scalar_step"), 1)
                        steps[0] += 1
                        dve.wait_ge(S("scalar_step"), steps[0])

                    mx, nmn = allext[:, lo_:hi_], allext[:, NQ + lo_:NQ + hi_]
                    dl, inv, span, low, high, t0, t1, zp = (qs[:, i, lo_:hi_] for i in range(8))
                    qh = qhi[:, lo_:hi_]
                    step(nc.vector.tensor_tensor(span, mx, nmn, ALU.add))
                    step(nc.vector.tensor_scalar(t0, span, 1.0 / LEVELS, None, ALU.mult))
                    step(nc.vector.tensor_copy(qh, t0))
                    step(nc.vector.tensor_tensor(t1, t0, qh, ALU.subtract))
                    step(nc.vector.scalar_tensor_tensor(out=zp, in0=qh, scalar=-LEVELS, in1=span, op0=ALU.mult,
                                                        op1=ALU.add))
                    step(nc.vector.scalar_tensor_tensor(out=low, in0=t1, scalar=-LEVELS, in1=zp, op0=ALU.mult,
                                                        op1=ALU.add))
                    step(nc.vector.scalar_tensor_tensor(out=dl, in0=low, scalar=1.0 / LEVELS, in1=t0, op0=ALU.mult,
                                                        op1=ALU.add))
                    step(nc.vector.reciprocal(inv, dl))
                    step(nc.vector.tensor_tensor(t0, nmn, inv, ALU.mult))
                    step(nc.vector.tensor_scalar(t1, t0, MAGIC, None, ALU.add))
                    step(nc.vector.tensor_scalar(zp, t1, -MAGIC, None, ALU.add))
                    step(nc.vector.tensor_scalar(low, zp, -1.0, MAGIC, ALU.mult, ALU.add))
                    step(nc.vector.tensor_scalar(high, low, LEVELS, None, ALU.add))
                    for i, (a_, c_) in enumerate((("q1", "k1"), ("q2", "k2"), ("ff1", "ff2"))):
                        if (i == 2) == (b == 1):
                            step(nc.vector.tensor_tensor(prods[:, i:i + 1], delta(a_), delta(c_), ALU.mult))
                    if b == 0:
                        nc.vector.tensor_copy(ffb[:], vec[:, OFFV["ff1_b"]:OFFV["ff1_b"] + M]).then_inc(
                            S("quant_scalars"), 1)
                    else:
                        i = QN.index("ff1")
                        dve.wait_ge(S("quant_scalars"), 1)
                        nc.vector.tensor_scalar(ffb[:], vec[:, OFFV["ff1_b"]:OFFV["ff1_b"] + M], qs[:, 1, i:i + 1],
                                                None, ALU.mult).then_inc(S("quant_scalars"), 1)


_VECTORS = {"a1_g": "L0_xattn_ln1_w", "a1_b": "L0_xattn_ln1_b", "a2_g": "L0_xattn_ln2_w", "a2_b": "L0_xattn_ln2_b",
            "a3_g": "L0_xattn_ln3_w", "a3_b": "L0_xattn_ln3_b", "b1_g": "L1_xattn_ln1_g", "b1_b": "L1_xattn_ln1_b",
            "b2_g": "L1_xattn_ln2_g", "b2_b": "L1_xattn_ln2_b", "b3_g": "L1_xattn_ln3_g", "b3_b": "L1_xattn_ln3_b",
            "mlp0_b": "L0_xattn_b1", "ff1_b": "L1_xattn_ff1_b"}


def kernel(**inputs):
    import numpy as _np
    import concourse.bacc as _bacc
    from concourse import mybir as _mybir
    from concourse.bass_utils import run_bass_kernel_spmd as _run

    a = {k: _np.asarray(v) for k, v in inputs.items()}

    def pack(weights, widths):
        cols = []
        for name, w in weights.items():
            tiles, n = widths[name]
            rows_ = w.shape[0] // tiles
            tile = _np.zeros((128, tiles, n), w.dtype)
            tile[:rows_] = w.reshape(tiles, rows_, n).transpose(1, 0, 2)
            cols.append(tile.reshape(128, tiles * n))
        return _np.ascontiguousarray(_np.concatenate(cols, axis=1))

    w0 = pack({"kv": a["L0_xattn_Wkv"], "q": a["L0_xattn_Wq"], "proj": a["L0_xattn_Wproj"], "w1": a["L0_xattn_W1"],
               "w2": a["L0_xattn_W2"]}, W0)
    w1 = pack({n: a[f"L1_xattn_{n}_w"].T for n in W1}, W1)
    vec = _np.zeros((128, NV), w0.dtype)
    for name, n in VEC.items():
        v = a[_VECTORS[name]].reshape(n, -1).T
        vec[:v.shape[0], OFFV[name]:OFFV[name] + n] = v
    rows = _np.stack([a["L0_xattn_bproj"], a["L0_xattn_b2"], a["L1_xattn_o1_b"], a["L1_xattn_o2_b"],
                      a["L1_xattn_ff2_b"]])
    arrays = {"x": a["x"], "ctx": a["ctx_768"], "w0": w0, "w1": w1, "vec": vec, "rows": rows}
    arrays = {f"in_{k}_dram": _np.ascontiguousarray(v) for k, v in arrays.items()}

    nc = _bacc.Bacc("TRN2", target_bir_lowering=False, num_devices=1)
    args = [nc.dram_tensor(k, v.shape, _mybir.dt.from_np(v.dtype), kind="ExternalInput").ap()
            for k, v in arrays.items()]
    o = nc.dram_tensor("out_0_dram", (B, R, D), _mybir.dt.float32, kind="ExternalOutput").ap()
    program(nc, *args, o)
    r = _run(nc, [arrays], core_ids=[0])
    return r.results[0]["out_0_dram"]
```

```python
from contextlib import ExitStack

import concourse.bass as bass
from concourse import mybir

F32 = mybir.dt.float32
F32R = mybir.dt.float32r
ACT = mybir.ActivationFunctionType
ALU = mybir.AluOpType
AX = mybir.AxisListType

B, R, D, C, NK = 4, 512, 256, 192, 64
H, HD = 16, 16
T, F = R // 128, D // 128
CK = C // 2
HID = 4 * D
M = HID // 128
EPS = 1e-5
SCALE = float(HD) ** -0.5
LEVELS = 255.0
MAGIC = 1.5 * 2.0 ** 23
VW = 32
VS = HD + 1
VN = H * VS + VW - VS

W0 = {"kv": (2, 2 * D), "q": (2, D), "proj": (2, D), "w1": (2, HID), "w2": (M, D)}
W1 = {"q1": (2, D), "k1": (2, D), "v1": (2, D), "o1": (2, D), "k2": (2, D), "v2": (2, D), "q2": (2, D),
      "o2": (2, D), "ff1": (2, 2 * HID), "ff2": (M, D)}
QN = list(W1)


def offsets(widths):
    at, out = 0, {}
    for name, (tiles, n) in widths.items():
        out[name] = at
        at += tiles * n
    return out, at


OFF0, N0 = offsets(W0)
OFF1, N1 = offsets(W1)
SPLIT0, SPLIT1 = OFF0["w1"], OFF1["ff1"]
VEC = {"a1_g": 2, "a1_b": 2, "a2_g": 2, "a2_b": 2, "a3_g": 2, "a3_b": 2, "b1_g": 2, "b1_b": 2, "b2_g": 2,
       "b2_b": 2, "b3_g": 2, "b3_b": 2, "mlp0_b": M, "ff1_b": 2 * M}
OFFV, NV = {}, 0
for _name, _n in VEC.items():
    OFFV[_name] = NV
    NV += _n
ROWS = ["bproj", "b2", "o1_b", "o2_b", "ff2_b"]
BIAS_AFTER = {"a1": "bproj", "a3": "b2", "b1": "o1_b", "b2": "o2_b", "b3": "ff2_b"}
LN_OF = {"xa": "a1", "sa": "b1", "xb": "b2"}
PROJ = {"xa": "proj", "sa": "o1", "xb": "o2"}



COST = {"load": (0, 0, 0, 3.58), "ctxz": (0, 1.21, 0, 3.01), "ctx": (0.3, 0.42, 1.46, 2.36),
        "ctxk": (1.95, 0.36, 0.63, 6.23), "ctxr": (0, 0, 0, 0.54), "ln": (0, 1.59, 0, 3.36), "lz": (0, 1.3, 0, 1.73),
        "lt": (0.96, 0, 1.93, 2.14), "ll": (0, 1.36, 0, 1.38), "q": (1.56, 0, 0.88, 1.67), "k": (1.72, 0, 1.09, 1.78),
        "ql": (0, 1.06, 0, 4.69), "kl": (0, 1.12, 0, 4.84), "v": (1.56, 0, 1.09, 2.15), "qr": (0, 0, 0, 4.7),
        "kr": (0, 0, 0, 4.86), "ql:sa": (0, 1.17, 0, 0.09), "qr:sa:0": (0, 0, 0, 0.1), "kr:sa:0": (0, 0, 0, 0.1),
        "qr:sa:1": (0, 0, 0, 0.11), "qr:xa:0": (0, 0, 0, 1.05), "qr:xb:0": (0, 0, 0, 1.14),
        "max:sa": (0.81, 2.1, 0, 0), "max:x": (1.05, 1.28, 0, 0), "neg": (0.44, 0, 0.55, 1.47),
        "nl": (0, 0.68, 0, 3.08), "nl:sa:0": (0, 0.56, 0, 0.1), "nl:sa:1": (0, 0.62, 0, 0.1),
        "negr:sa:0": (0, 0, 0, 0.09), "negr:sa:1": (0, 0, 0, 0.12), "negr": (0, 0, 0, 2.91),
        "exp:sa": (0.88, 0, 2.12, 0), "exp:x": (0.38, 0, 1.03, 0), "val:sa": (0.96, 0, 0, 0),
        "val:x": (0.79, 0, 0, 0), "out1": (1.67, 2.35, 0, 3.57), "out2": (0.93, 0, 0.93, 1.45),
        "ol": (0, 1.22, 0, 1.2), "out3": (1.59, 1.2, 0, 2.39), "mlp0": (1.33, 0, 0.55, 0), "low0": (0, 0.57, 0.5, 0),
        "down0": (1.42, 0, 0, 0), "mlp1": (1.58, 0.6, 0.57, 0), "low1": (0, 0.65, 0.52, 0), "down1": (0.82, 0, 0, 0),
        "store0": (0, 0, 0, 4.0), "store1": (0, 0, 0, 4.3), "stats": (0, 1.96, 0, 3.13),
        "scalars": (0, 2.03, 0, 7.96), "round": (0, 0, 0, 5.69), "raw": (0, 0, 0, 9.09), "ones": (0, 0, 0, 2.1)}
BANKS = {"ctx": 1, "ctxk": 2, "lt": 2, "q": 2, "k": 2, "v": 2, "max:sa": 4, "max:x": 2, "neg": 1, "exp:sa": 4,
         "exp:x": 2, "out1": 4, "out2": 2, "out3": 2, "mlp0": 1, "mlp1": 2}
READ_IN = {"q": "ql", "k": "kl", "neg": "nl", "out2": "ol"}
SHORT = 6
SLACK = 0.72

WARM_FROM, WARM_SHARE, WARM_TIME = 0.59, 0.83, 0.2135


def cost(st):
    name, *rest = st.split(":")
    if st in COST:
        return COST[st]
    if name in ("max", "exp", "val"):
        name += ":sa" if rest[0] == "sa" else ":x"
    return COST[name]


def banks(st):
    name, *rest = st.split(":")
    if name in ("max", "exp"):
        name += ":sa" if rest[0] == "sa" else ":x"
    return BANKS.get(name, 0)


def read_in(st):
    name, *rest = st.split(":")
    return ":".join([READ_IN[name]] + rest) if name in READ_IN else None


def attention_steps(inst):
    if inst == "sa":
        out = [f"max:sa:{h}" for h in range(8)] + ["neg:sa:0", "nl:sa:0", "max:sa:8", "max:sa:9", "negr:sa:0"]
        out += [f"max:sa:{h}" for h in range(10, H)] + ["neg:sa:1", "nl:sa:1"]
        units = [f"{qd}:{kt}" for qd in range(4) for kt in range(T)]
    else:
        out = [f"max:{inst}:{t}" for t in range(T)] + [f"neg:{inst}:0", f"nl:{inst}:0", f"negr:{inst}:0"]
        units = [f"{qd}:0" for qd in range(4)]
    for i, u in enumerate(units):
        out.append(f"exp:{inst}:{u}")
        if i:
            out.append(f"val:{inst}:{units[i - 1]}")
        if inst == "sa" and i == 2:
            out.append("negr:sa:1")
    return out + [f"val:{inst}:{units[-1]}"]


def thread(par):
    out = []
    turns = [(0, par), (0, par + 2), (1, par), (1, par + 2)]
    for n, (layer, b) in enumerate(turns):
        att = ["xa"] if layer == 0 else ["sa", "xb"]
        steps = [f"load:{layer}"]
        if n == 0:
            steps += ["ctxz", "ctx:xa", "ctxk:xa", "ctxr:xa"]
        for inst in att:
            a = LN_OF[inst]
            steps += [f"ln:{a}", f"lz:{a}", f"lt:{a}", f"ll:{a}"]
            if inst == "sa":
                steps += ["q:sa", "ql:sa", "v:sa", "k:sa", "qr:sa:0", "kl:sa", "kr:sa:0", "qr:sa:1", "kr:sa:1"]
            else:
                steps += [f"q:{inst}", f"ql:{inst}", f"qr:{inst}:0", f"qr:{inst}:1"]
            steps += attention_steps(inst) + [f"out1:{inst}", f"out2:{inst}", f"ol:{inst}", f"out3:{inst}"]
        a = "a3" if layer == 0 else "b3"
        steps += [f"ln:{a}", f"lz:{a}", f"lt:{a}", f"ll:{a}"]
        ahead = {}
        if n < 3:
            nl, nb = turns[n + 1]
            x_ = "xa" if nl == 0 else "xb"
            ahead = {0: ("ctxz", nb), 2: (f"ctx:{x_}", nb), 3: (f"ctxk:{x_}", nb), 5: (f"ctxr:{x_}", nb)}
            if nl:
                del ahead[0]
        steps = [(st, b) for st in steps]
        for m in range(M):
            steps.append((f"mlp{layer}:{m}", b))
            if m:
                steps.append((f"down{layer}:{m - 1}", b))
            steps.append((f"low{layer}:{m}", b))
            if m in ahead:
                steps.append(ahead[m])
        steps += [(f"down{layer}:{M - 1}", b), (f"store{layer}", b)]
        out += steps
        if (layer, b) == (0, 3):
            out.insert(out.index(("out3:xa", 3)) + 1, ("ones", 0))
            out.append(("ones", 2))
        if (layer, b) == (0, 1):
            out.insert(out.index(("exp:xa:0:0", 1)), ("ones", 1))
    return out


QSMALL = 8
CHUNKS = [(i, a, min(4 * D, W1[w][0] * W1[w][1] - a)) for i, w in enumerate(QN)
          for a in range(0, W1[w][0] * W1[w][1], 4 * D)]
NCH = len(CHUNKS)


def order():
    quant = [("raw", 0)] + [("stats", i) for i in range(QSMALL)] + [("scalars", 0)]
    quant += [("round", i) for i in range(QSMALL)]
    quant += [("raw", 1)] + [("stats", i) for i in range(QSMALL, NCH)] + [("scalars", 1), ("round", 8), ("round", 9)]
    threads = [thread(0), thread(1), quant]
    needs = {("kr:sa", 0): ("ones", 0), ("raw", 1): (f"down0:{M - 1}", 3), ("q:sa", 0): ("round", QSMALL - 1),
             ("ctxk:xb", 0): ("round", QSMALL - 1), ("mlp1:0", 0): ("round", 9), ("ctxz", 2): ("ctxz", 1),
             ("raw", 0): ("ctxk:xa", 1)}
    def lock(st):
        take, give = [], []
        if st in ("exp:xa:0:0", "exp:sa:0:0", "exp:xb:0:0", "mlp0:0", "mlp1:0"):
            take.append("act")
        if st in ("out1:xa", "out1:sa", "out1:xb", f"down0:{M - 1}", f"down1:{M - 1}"):
            give.append("act")
        return take, give

    at, ready, held, done_, out = [0, 0, 0], [0.0, 8.1, 20.0], {}, set(), []
    pe = dve = act = 0.0
    ring, turn = [None] * SHORT, 0
    while any(at[i] < len(threads[i]) for i in range(3)):
        best = None
        for i in range(3):
            if at[i] == len(threads[i]):
                continue
            st = threads[i][at[i]]
            if needs.get(st, st) not in done_ and st in needs:
                continue
            if any(held.get(x_, i) != i for x_ in lock(st[0])[0]):
                continue
            if any(ring[(turn + k) % SHORT] for k in range(banks(st[0]))):
                continue
            c = cost(st[0])
            start = max(ready[i], pe) if c[0] else ready[i]
            if best is None or start < best[0]:
                best = (start, i, st, c)
        start, i, st, c = best
        at[i] += 1
        if c[0] and start - pe > WARM_FROM:
            out.append((f"warm:{int((start - pe) * WARM_SHARE / WARM_TIME)}", len(out)))
        out.append(st)
        done_.add(st)
        later = read_in(st[0])
        for k in range(banks(st[0])):
            ring[turn % SHORT] = (later, st[1]) if later else None
            turn += 1
        ring = [None if x_ == st else x_ for x_ in ring]
        take, give = lock(st[0])
        for x_ in take:
            held[x_] = i
        for x_ in give:
            del held[x_]
        if c[0]:
            pe = start + c[0]
        if c[1]:
            dve = max(dve, start) + c[1]
        if c[2]:
            act = max(act, start) + c[2]
        ready[i] = start + max(c[0], c[3])
        slack = 0 if c[3] else SLACK
        if c[1]:
            ready[i] = max(ready[i], dve - slack)
        if c[2]:
            ready[i] = max(ready[i], act - slack)
    return out


ORDER = order()


def heads(h):
    return h // 8 * 4 + h % 8 // 2, h % 2


def bank_uses():
    plan, count, turn = {}, [0] * 8, {"long": 0, "short": 0}

    def use(key, kind="short"):
        first, n = (0, 2) if kind == "long" else (2, SHORT)
        k = first + turn[kind] % n
        turn[kind] += 1
        plan[key] = (k, count[k])
        count[k] += 1

    for st, b in ORDER:
        name, *rest = st.split(":")
        if name == "warm":
            k = 2 + turn["short"] % SHORT
            plan[(st, b)] = (k, count[k])
        elif name == "ctx":
            use((st, b))
        elif name == "ctxk":
            use((st, b, "K"))
            use((st, b, "V"))
        elif name in ("lt", "q", "k", "out2"):
            for f in range(F):
                use((st, b, f))
        elif name in ("v", "out3"):
            for t2 in range(T // 2):
                use((st, b, t2))
        elif name == "max":
            for i in range(T if rest[0] == "sa" else 2):
                use((st, b, i))
        elif name == "neg":
            use((st, b))
        elif name == "exp":
            inst, qd, kt = rest
            if kt == "0":
                use(("pv", inst, b, int(qd)), "long")
            for j in range(4 if inst == "sa" else 2):
                use((st, b, j))
        elif name == "out1":
            for t in range(T):
                use((st, b, t))
        elif name in ("mlp0", "mlp1"):
            if rest[0] == "0":
                for t2 in range(T // 2):
                    use((name, "acc", b, t2), "long")
            if name == "mlp1":
                use((st, b, "g"))
            use((st, b, "h"))
    return plan


def prob_units():
    units, at = {}, 0
    for st, b in ORDER:
        if st.startswith("exp"):
            _, inst, qd, kt = st.split(":")
            n = 4 if inst == "sa" else 2
            units[(st, b)] = (at, n, inst != "sa" or int(kt) == T - 1)
            at += n
    return units


def program(nc, x, ctx_in, w0_in, w1_in, vec_in, rows_in, out):
    plan = bank_uses()
    units = prob_units()
    NP = 8
    tile_unit, quad_used, used = {}, {}, 0
    for u, (first, n, last) in units.items():
        for k in range(n):
            tile_unit[first + k] = u
        if not last:
            used += 1
        quad_used[u] = used

    top = [(nc.sbuf_base + 63) // 64 * 64]

    def sb(name, shape, dt, at=None):
        size = 4
        for n in shape[1:]:
            size *= n
        size = (size + 31) // 32 * 32
        if at is None:
            at = top[0]
            top[0] += size
        return nc.alloc_sbuf_tensor_at(name, shape, dt, offset=at), at + size

    def new(name, shape, dt=F32):
        return sb(name, shape, dt)[0]

    xs = [new(f"x{i}", [128, T, D]) for i in range(2)]
    rowz_at = top[0]
    rowz = [new(f"rowz{i}", [128, T, D]) for i in range(2)]
    ctx_z, ctx_hi = [], []
    for i in range(2):
        t_, at = sb(f"ctx_z{i}", [128, C], F32, rowz_at + i * T * D * 4)
        ctx_z.append(t_)
        ctx_hi.append(sb(f"ctx_hi{i}", [CK, 2, 128], F32R, at)[0])
    hiT = [new(f"hiT{i}", [128, F, R], F32R) for i in range(2)]
    full_at = top[0]
    loT = [new(f"loT{i}", [128, F, R], F32R) for i in range(2)]
    full_t = [sb(f"full_t{i}", [128, F, R], F32, full_at + i * F * R * 4)[0] for i in range(2)]
    qk_parts = new("qk_parts", [128, 2, 2, R], F32R)
    lo_at = top[0]
    ctx_lo = new("ctx_lo", [CK, 2, 128], F32R)
    ctx_full, _ = sb("ctx_full", [CK, 2, 128], F32, lo_at)
    q_stack = [new(f"q_stack{i}", [128, H // 2, R], F32R) for i in range(2)]
    o_raw = new("o_raw", [128, 4, R])
    kc_stack = [new(f"kc_stack{i}", [128, H // 2, 2 * NK], F32R) for i in range(2)]
    vc = [new(f"vc{i}", [128, VN]) for i in range(2)]
    neg_parts = new("neg_parts", [16, 2, R], F32R)
    rows = new("rows", [128, len(ROWS), D])
    vec = new("vec", [128, NV])
    ident = new("ident", [128, 128])
    ctx_rows = [new(f"ctx_rows{i}", [128, C]) for i in range(B)]
    kc_parts = new("kc_parts", [128, 2, 2 * NK], F32R)
    six = [new(f"six{i}", [128, T, 6]) for i in range(2)]
    meanvar = [new(f"meanvar{i}", [128, T, 2]) for i in range(2)]
    vareps = [new(f"vareps{i}", [128, T]) for i in range(2)]
    rstd = [new(f"rstd{i}", [128, T]) for i in range(2)]
    half = new("half", [128, T])
    negmax = [new(f"negmax{i}", [128, T, H]) for i in range(2)]
    rsum = new("rsum", [128, H])
    NQ = len(QN)
    ext = new("ext", [128, 2 * NCH])
    allext = new("allext", [128, 2 * NCH])
    ffext = new("ffext", [128, 2, NQ - QSMALL])
    qs = new("qs", [128, 8, NQ])
    qhi = new("qhi", [128, NQ], F32R)
    prods = new("prods", [128, 4])
    ffb = new("ffb", [128, M])
    arena = top[0]
    probs, end = sb("probs", [128, NP, R], F32)
    top[0] = end
    hid_hi, at = sb("hid_hi", [128, 2, R], F32R, arena)
    hid_lo, _ = sb("hid_lo", [128, 2, R], F32R, at)
    hid, at = sb("hid", [128, 2, R], F32, at)
    gate, at = sb("gate", [128, 2, R], F32, at)
    k_stack1 = new("k_stack1", [128, H // 2, R], F32R)
    raw_at = top[0]
    raw1a = new("raw1a", [128, SPLIT1])
    wn_a, _ = sb("wn_a", [128, SPLIT1], F32R, raw_at)
    vx = [new("vx0", [128, T, VN])]
    k_stack, _ = sb("k_stack0", [128, H // 2, R], F32R, top[0])
    k_stack = [k_stack, k_stack1]
    whl = {"att": [new(f"w_att_{p_}", [128, SPLIT0], F32R) for p_ in ("hi", "lo")]}
    raw1b, _ = sb("raw1b", [128, N1 - SPLIT1], F32, top[0])
    wn_b, at = sb("wn_b", [128, N1 - SPLIT1], F32R, top[0])
    vx.append(sb("vx1", [128, T, VN], F32, at)[0])
    whl["mlp"] = [new(f"w_mlp_{p_}", [128, N0 - SPLIT0], F32R) for p_ in ("hi", "lo")]
    raw0, _ = sb("raw0", [128, N0], F32, arena)

    scr = {}
    for inst in ("xa", "sa", "xb"):
        for b in range(B):
            scr["q", inst, b] = nc.dram_tensor(f"q_{inst}{b}", (D, 3, R), F32, kind="Internal").ap()
            scr["k", inst, b] = nc.dram_tensor(f"k_{inst}{b}", (D, 3, R if inst == "sa" else NK), F32,
                                               kind="Internal").ap()
            scr["n", inst, b] = nc.dram_tensor(f"n_{inst}{b}", (H, 2, R), F32, kind="Internal").ap()
    zeros = nc.dram_tensor("zeros", (2, H // 2, R), F32, kind="Internal").ap()
    mid = nc.dram_tensor("mid", (B, R, D), F32, kind="Internal").ap()

    assert top[0] <= 229376, top[0]
    with ExitStack() as stack:
        psum = stack.enter_context(nc.psum_tensor("banks", [128, 8, 512], F32))
        sems = {}

        def S(name):
            if name not in sems:
                sems[name] = stack.enter_context(nc.semaphore(name.replace(":", "_")))
            return sems[name]

        full = [S(f"bank_full{k}") for k in range(8)]
        free = [S(f"bank_free{k}") for k in range(8)]

        def bank(key):
            return psum[:, plan[key][0], :]

        def claim(pe, key):
            k, before = plan[key]
            if before:
                pe.wait_ge(free[k], before)
            return psum[:, k, :]

        def filled(eng, key):
            k, before = plan[key]
            eng.wait_ge(full[k], before + 1)
            return psum[:, k, :]

        def drained(eng, key):
            k, before = plan[key]
            eng.wait_ge(free[k], before + 1)

        def done(key):
            return full[plan[key][0]]

        def release(key):
            return free[plan[key][0]]

        def weights(name, kt, a, n, rows_=128):
            if name in W0:
                o = OFF0[name] + kt * W0[name][1] + a
                pair, o = (whl["att"], o) if o < SPLIT0 else (whl["mlp"], o - SPLIT0)
                return tuple(p_[0:rows_, o:o + n] for p_ in pair)
            o = OFF1[name] + kt * W1[name][1] + a
            t_, o = (wn_a, o) if o < SPLIT1 else (wn_b, o - SPLIT1)
            return (t_[0:rows_, o:o + n],)

        def split_to(name, part):
            o, m_ = OFF0[name], W0[name][0] * W0[name][1]
            pair, o = (whl["att"], o) if o < SPLIT0 else (whl["mlp"], o - SPLIT0)
            return pair[part][:, o:o + m_]

        def raw1_of(i):
            o, m_ = OFF1[QN[i]], W1[QN[i]][0] * W1[QN[i]][1]
            if o < SPLIT1:
                return raw1a[:, o:o + m_], wn_a[:, o:o + m_]
            return raw1b[:, o - SPLIT1:o - SPLIT1 + m_], wn_b[:, o - SPLIT1:o - SPLIT1 + m_]

        def passes(xp, wp):
            return [(xp[0], wp[0]), (xp[1], wp[0])] + ([(xp[0], wp[1])] if len(wp) == 2 else [])

        def delta(name, parts=128):
            i = QN.index(name)
            return qs[0:parts, 0, i:i + 1]

        def col(name, i, parts=128):
            o = OFFV[name] + i
            return vec[0:parts, o:o + 1]

        def stack_of(inst, b):
            return k_stack[b % 2] if inst == "sa" else kc_stack[b % 2]

        def index_of(*names):
            found = [s_ for s_ in ORDER if s_[0] in names or s_[0].split(":")[0] in names]
            return found, {s_: i for i, s_ in enumerate(found)}

        qk_list, qk_index = index_of("q", "k")
        ctx_list, ctx_index = index_of("ctx")
        z_list, z_index = index_of("ctxz")
        mlp_list, mlp_index = index_of("mlp0", "mlp1")
        neg_list, neg_index = index_of("neg")
        out_list, out_index = index_of("out1")
        ln_index = {}
        for inst in ("a1", "a3", "b1", "b2", "b3"):
            for i, s_ in enumerate(index_of(f"ln:{inst}")[0]):
                ln_index[inst, s_[1]] = i
        q_seen, q_prev, neg_total = {}, {}, {}
        for par_ in range(2):
            qs_ = [s_ for s_ in qk_list if s_[0][:2] == "q:" and s_[1] % 2 == par_]
            for i, (st, b) in enumerate(qs_):
                inst = st.split(":")[1]
                q_seen[inst, b] = i + 1
                q_prev[inst, b] = (qs_[i - 1][0].split(":")[1], qs_[i - 1][1]) if i else None
            for g in range(2):
                of_group = [s_ for s_ in neg_list if s_[1] % 2 == par_ and s_[0].endswith(f":{g}")]
                for i, (st, b) in enumerate(of_group):
                    neg_total[st.split(":")[1], b, g] = 16 * 2 * (i + 1)
        q_scaled = {"q:sa": 0, "q:xb": 1}

        def last_use(eng, inst, b):
            filled(eng, ("pv", inst, b, 3))

        def kc_user(b, inst):
            turns = [("xa", b % 2), ("xa", b % 2 + 2), ("xb", b % 2), ("xb", b % 2 + 2)]
            i = turns.index((inst, b))
            return turns[i - 1] if i else None

        def kc_count(inst, b):
            return (0 if inst == "xa" else 2) + b // 2 + 1

        block = stack.enter_context(nc.Block())

        @block.sync
        def _(sp):
            def loaded(dst, src, sem):
                sp.dma_start(dst, src).then_inc(S(sem), 16)

            loaded(raw0[:, 0:OFF0["q"]], w0_in[:, 0:OFF0["q"]], "raw0_kv_loaded")
            for b in range(B):
                for half_ in range(2):
                    loaded(ctx_rows[b][half_ * NK:half_ * NK + NK, :], ctx_in[b], f"ctx_loaded{b}")
                if b == 0:
                    loaded(vec[:], vec_in, "vectors_loaded")
                if b == 1:
                    for i in range(2):
                        loaded(xs[i][:], x[i].rearrange("(t p) d -> p t d", p=128), f"x_loaded{i}")
                    for w in ("q", "proj", "w1", "w2"):
                        o, m_ = OFF0[w], W0[w][0] * W0[w][1]
                        loaded(raw0[:, o:o + m_], w0_in[:, o:o + m_], f"raw0_{w}_loaded")
            for i in range(len(ROWS)):
                loaded(rows[:, i, :], rows_in[i:i + 1, :].broadcast_to([128, D]), "rows_loaded")

            sp.wait_ge(S("pool_set"), 4)
            sp.dma_start(zeros, q_stack[0][0:2, :, :].bitcast(F32)).then_inc(S("zeros_sent"), 16)

            def send(d, parts_, kind, sem):
                both, one = (0, 2) if kind == "q" else (1, 0)
                sp.dma_start(d[:, both:both + 2], parts_(0, 2)).then_inc(S(sem), 16)
                sp.dma_start(d[:, one:one + 1], parts_(0, 1)).then_inc(S(sem), 16)

            for st, b in ORDER:
                name, *rest = st.split(":")
                if name == "load":
                    layer = int(rest[0])
                    if (layer, b) in ((0, 0), (0, 1)):
                        continue
                    sp.wait_ge(S(f"stored{b % 2}"), 16 * (layer * 2 + b // 2))
                    loaded(xs[b % 2][:], (x if layer == 0 else mid)[b].rearrange("(t p) d -> p t d", p=128),
                           f"x_loaded{b % 2}")
                elif name == "raw":
                    if b == 0:
                        for i in range(QSMALL):
                            loaded(raw1_of(i)[0], w1_in[:, OFF1[QN[i]]:OFF1[QN[i]] + raw1_of(i)[0].shape[1]],
                                   f"raw1_{QN[i]}_loaded")
                    else:
                        filled(sp, ("mlp0", "acc", B - 1, 1))
                        for i in range(QSMALL, NQ):
                            loaded(raw1_of(i)[0], w1_in[:, OFF1[QN[i]]:OFF1[QN[i]] + raw1_of(i)[0].shape[1]],
                                   f"raw1_{QN[i]}_loaded")
                elif name == "ctxk":
                    inst = rest[0]
                    drained(sp, (st, b, "K"))
                    for m in range(F):
                        send(scr["k", inst, b][m * 128:m * 128 + 128],
                             lambda a, n: kc_parts[:, a:a + n, m * NK:m * NK + NK].bitcast(F32), "k", "kc_sent")
                elif name == "ctxr":
                    inst = rest[0]
                    sp.wait_ge(S("kc_sent"), 64 * (ctx_index[(f"ctx:{inst}", b)] + 1))
                    before = kc_user(b, inst)
                    if before:
                        last_use(sp, *before)
                    else:
                        sp.wait_ge(S("kc_set"), 4)
                    src = scr["k", inst, b].rearrange("(hp par d) s n -> par (d s) hp n", par=2, d=HD)
                    for par in range(2):
                        r = 64 * par
                        sp.dma_start(kc_stack[b % 2][r:r + 3 * HD, :, par * NK:par * NK + NK].bitcast(F32),
                                     src[par]).then_inc(S(f"kc_stacked{b % 2}"), 16)
                elif name in ("ql", "kl"):
                    name = name[0]
                    st = f"{name}:{rest[0]}"
                    for m in range(F):
                        drained(sp, (st, b, m))
                        send(scr[name, rest[0], b][m * 128:m * 128 + 128],
                             lambda a, n: qk_parts[:, m, a:a + n, :].bitcast(F32), name, f"qk_sent{m}")
                elif name in ("qr", "kr"):
                    inst, m = rest[0], int(rest[1])
                    sp.wait_ge(S(f"qk_sent{m}"), 32 * (qk_index[(f"{name[0]}:{inst}", b)] + 1))
                    src = scr[name[0], inst, b][m * 128:m * 128 + 128].rearrange(
                        "(hp par d) s n -> par (d s) hp n", par=2, d=HD)
                    if name == "qr":
                        if q_prev[inst, b]:
                            last_use(sp, *q_prev[inst, b])
                        else:
                            sp.wait_ge(S("pool_set"), 4)
                        if inst != "sa" and m == 0:
                            sp.wait_ge(S("zeros_sent"), 16)
                            for par in range(2):
                                r = 64 * par + 3 * HD
                                sp.dma_start(q_stack[b % 2][r:r + 2, :, :].bitcast(F32), zeros).then_inc(
                                    S(f"q_cleared{b % 2}"), 16)
                        dst, sem = q_stack[b % 2], f"q_stacked{b % 2}_{m}"
                    else:
                        if b >= 2:
                            last_use(sp, "sa", b - 2)
                        else:
                            sp.wait_ge(S(f"k_ones_set{b}"), 2)
                        dst, sem = k_stack[b % 2], f"k_stacked{b % 2}_{m}"
                    for par in range(2):
                        r = 64 * par
                        sp.dma_start(dst[r:r + 3 * HD, 4 * m:4 * m + 4, :].bitcast(F32), src[par]).then_inc(
                            S(sem), 16)
                elif name == "nl":
                    inst, g = rest[0], int(rest[1])
                    n = 8 if inst == "sa" else 16
                    drained(sp, (f"neg:{inst}:{g}", b))
                    sp.dma_start(scr["n", inst, b][g * 8:g * 8 + n],
                                 neg_parts[0:n, :, :].bitcast(F32)).then_inc(S("neg_sent"), 16)
                elif name == "negr":
                    inst, g = rest[0], int(rest[1])
                    n = 8 if inst == "sa" else 16
                    sp.wait_ge(S("neg_sent"), 16 * (neg_index[(f"neg:{inst}:{g}", b)] + 1))
                    src = scr["n", inst, b][g * 8:g * 8 + n].rearrange("(par hp) q n -> par q hp n", par=2)
                    for par in range(2):
                        r = 64 * par + 3 * HD
                        sp.dma_start(q_stack[b % 2][r:r + 2, g * 4:g * 4 + n // 2, :].bitcast(F32),
                                     src[par]).then_inc(S(f"neg_stacked{b % 2}_{g}"), 16)
                elif name in ("store0", "store1"):
                    for t2 in range(T // 2):
                        drained(sp, (f"mlp{name[-1]}", "acc", b, t2))
                    sp.dma_start((mid if name == "store0" else out)[b].rearrange("(t p) d -> p t d", p=128),
                                 xs[b % 2][:]).then_inc(S(f"stored{b % 2}"), 16)
            for i in range(2):
                sp.wait_ge(S(f"stored{i}"), 16 * 4)

        @block.gpsimd
        def _(pool):
            nc.gpsimd.memset(ident[:], 0.0).then_inc(S("ident_zero"), 1)
            nc.gpsimd.memset(half[:], -0.5).then_inc(S("ident_zero"), 1)
            pool.wait_ge(S("ident_zero"), 2)
            nc.gpsimd.affine_select(out=ident[:], in_=ident[:], compare_op=ALU.not_equal, fill=1.0, base=0,
                                    pattern=[[-1, 128]], channel_multiplier=1).then_inc(S("ident_ready"), 1)
            for i in range(2):
                nc.gpsimd.memset(vc[i][:], 1.0).then_inc(S("pool_set"), 1)
            nc.gpsimd.memset(vx[0][:], 1.0).then_inc(S("v_ones_set0"), 1)
            for i in range(2):
                nc.gpsimd.memset(q_stack[i][:].bitcast(F32), 0.0).then_inc(S("pool_set"), 1)

            def power(b, ready, n, var, out_, t):
                pool.wait_ge(ready, n)
                nc.gpsimd.tensor_scalar(vareps[b % 2][:, 0:t], var, EPS, 1.0, ALU.add, ALU.mult).then_inc(S("vareps"), 1)
                power.n += 1
                pool.wait_ge(S("vareps"), power.n)
                return nc.gpsimd.tensor_tensor(out_, vareps[b % 2][:, 0:t], half[:, 0:t], ALU.pow)

            power.n = 0
            step_n = chunks = 0
            latest = {}
            for st, b in ORDER:
                name, *rest = st.split(":")
                if name == "ctxz":
                    i = z_index[(st, b)]
                    power(b, S("ctx_mean"), i + 1, meanvar[b % 2][:, 0:1, 1], rstd[b % 2][:, 0:1], 1).then_inc(
                        S("ctx_rstd"), 1)
                    latest["ctx_rstd"] = i + 1
                elif name == "ln":
                    inst = rest[0]
                    i = ln_index[inst, b]
                    power(b, S(f"{inst}_mean"), T * (i + 1), meanvar[b % 2][:, :, 1], rstd[b % 2][:],
                          T).then_inc(S(f"{inst}_rstd"), 1)
                    latest[f"{inst}_rstd"] = i + 1
                elif name == "lz":
                    inst = rest[0]
                    i = ln_index[inst, b]
                    if i == 0 and inst == "a1":
                        pool.wait_ge(S("rows_loaded"), 16 * len(ROWS))
                    pool.wait_ge(S(f"{inst}_rowz"), T * (i + 1))
                    r = ROWS.index(BIAS_AFTER[inst])
                    for t in range(T):
                        nc.gpsimd.tensor_tensor(xs[b % 2][:, t, :], xs[b % 2][:, t, :], rows[:, r, :],
                                                ALU.add).then_inc(S(f"{inst}_biased"), 1)
                    latest[f"{inst}_biased"] = T * (i + 1)
                elif name == "scalars":
                    pool.wait_ge(S("extremes"), 2 * (QSMALL if b == 0 else NCH))
                    if b:
                        pool.wait_ge(S("quant_scalars"), 1)
                    nc.gpsimd.partition_all_reduce(allext[:], ext[:], 128,
                                                   bass.bass_isa.ReduceOp.max).then_inc(S("extremes_all"), 1)
                    latest["extremes_all"] = b + 1
                elif name == "round":
                    raw, ints = raw1_of(b)
                    pool.wait_ge(S("quant_scalars"), 1 if b < QSMALL else 2)
                    for a in range(0, raw.shape[1], 2 * R):
                        n = min(2 * R, raw.shape[1] - a)
                        v = raw[:, a:a + n]
                        nc.gpsimd.tensor_scalar(v, v, qs[:, 1, b:b + 1], MAGIC, ALU.mult, ALU.add).then_inc(
                            S("round_step"), 1)
                        pool.wait_ge(S("round_step"), step_n + 1)
                        nc.gpsimd.tensor_scalar(v, v, qs[:, 3, b:b + 1], qs[:, 4, b:b + 1], ALU.max,
                                                ALU.min).then_inc(S("round_step"), 1)
                        step_n += 2
                        chunks += 1
                        pool.wait_ge(S("round_step"), step_n)
                        nc.gpsimd.tensor_scalar(ints[:, a:a + n], v, -MAGIC, None, ALU.add).then_inc(
                            S("integers"), 1)
                    latest["integers"] = chunks
                elif name == "ones":
                    if b == 0:
                        filled(pool, ("out3:xa", B - 1, 1))
                    elif b == 1:
                        pool.wait_ge(S("w0_split"), len(W0))
                    else:
                        filled(pool, ("mlp0", "acc", B - 1, 1))
                        nc.gpsimd.memset(vx[1][:], 1.0).then_inc(S("v_ones_set1"), 1)
                        continue
                    for own, count in latest.items():
                        pool.wait_ge(S(own), count)
                    for par in range(2):
                        nc.gpsimd.memset(k_stack[b][64 * par + 32:64 * par + 64, :, :].bitcast(F32), 1.0).then_inc(
                            S(f"k_ones_set{b}"), 1)
                        pool.wait_ge(S(f"k_ones_set{b}"), 1 + par)

        @block.tensor
        def _(pe):
            def product(out_, pairs, lhs_is_w):
                for i, (xp, wp) in enumerate(pairs):
                    lhs, rhs = (wp, xp) if lhs_is_w else (xp, wp)
                    last = nc.tensor.matmul(out_, lhs, rhs, start=(i == 0), stop=(i == len(pairs) - 1))
                return last

            def parts(b, kt, a, n):
                return (hiT[b % 2][:, kt, a:a + n], loT[b % 2][:, kt, a:a + n])

            def wait_weights(name):
                if name in W0:
                    pe.wait_ge(S("w0_split"), list(W0).index(name) + 1)
                else:
                    pe.wait_ge(S("integers"), sum(-(-W1[w][0] * W1[w][1] // (2 * R))
                                                  for w in QN[:QN.index(name) + 1]))

            pe.wait_ge(S("ident_ready"), 1)
            for st, b in ORDER:
                name, *rest = st.split(":")
                if name == "warm":
                    o = claim(pe, (st, b))
                    for _i in range(int(rest[0])):
                        nc.tensor.matmul(o[:, 0:128], ident[:], ident[:], start=True, stop=True)
                elif name == "ctx":
                    o = claim(pe, (st, b))
                    if rest[0] == "xa":
                        pe.wait_ge(S("ctx_z"), z_index[("ctxz", b)] + 1)
                        src = ctx_z[b % 2]
                    else:
                        pe.wait_ge(S(f"ctx_loaded{b}"), 32)
                        src = ctx_rows[b]
                    for kt in range(2):
                        mm = nc.tensor.transpose(o[0:CK, kt * 128:kt * 128 + 128], src[:, kt * CK:kt * CK + CK],
                                                 ident[:])
                    mm.then_inc(done((st, b)), 1)
                elif name == "ctxk":
                    wk, wv, va = ("kv", "kv", D) if rest[0] == "xa" else ("k2", "v2", 0)
                    o = claim(pe, (st, b, "K"))
                    pe.wait_ge(S("ctx_lo"), ctx_index[(f"ctx:{rest[0]}", b)] + 1)
                    wait_weights(wk)
                    for m in range(2):
                        pairs = []
                        for kt in range(2):
                            xp = (ctx_hi[b % 2][:, kt, 0:NK], ctx_lo[:, kt, 0:NK])
                            pairs += passes(xp, weights(wk, kt, m * 128, 128, CK))
                        mm = product(o[:, m * NK:m * NK + NK], pairs, True)
                    mm.then_inc(done((st, b, "K")), 1)
                    o = claim(pe, (st, b, "V"))
                    wait_weights(wv)
                    pairs = []
                    for kt in range(2):
                        pairs += passes((ctx_hi[b % 2][:, kt, :], ctx_lo[:, kt, :]), weights(wv, kt, va, D, CK))
                    product(o[:, 0:D], pairs, False).then_inc(done((st, b, "V")), 1)
                elif name == "lt":
                    inst = rest[0]
                    pe.wait_ge(S(f"{inst}_rowz"), T * (ln_index[inst, b] + 1))
                    for f in range(F):
                        o = claim(pe, (st, b, f))
                        for t in range(T):
                            mm = nc.tensor.transpose(o[:, t * 128:t * 128 + 128],
                                                     rowz[b % 2][:, t, f * 128:f * 128 + 128], ident[:])
                        mm.then_inc(done((st, b, f)), 1)
                elif name in ("q", "k"):
                    w = {"q:xa": "q", "q:sa": "q1", "k:sa": "k1", "q:xb": "q2"}[st]
                    wait_weights(w)
                    inst = LN_OF[rest[0]]
                    pe.wait_ge(S(f"{inst}_loT"), F * (ln_index[inst, b] + 1))
                    for m in range(F):
                        o = claim(pe, (st, b, m))
                        pairs = []
                        for kt in range(F):
                            pairs += passes(parts(b, kt, 0, R), weights(w, kt, m * 128, 128))
                        product(o, pairs, True).then_inc(done((st, b, m)), 1)
                elif name == "v":
                    wait_weights("v1")
                    for t2 in range(T // 2):
                        o = claim(pe, (st, b, t2))
                        for i in range(2):
                            pairs = []
                            for kt in range(F):
                                pairs += passes(parts(b, kt, (2 * t2 + i) * 128, 128), weights("v1", kt, 0, D))
                            mm = product(o[:, i * D:i * D + D], pairs, False)
                        mm.then_inc(done((st, b, t2)), 1)
                elif name == "max":
                    inst, i = rest[0], int(rest[1])
                    for m in (i // 8,) if inst == "sa" else range(F):
                        pe.wait_ge(S(f"q_stacked{b % 2}_{m}"), 32 * q_seen[inst, b])
                    ks = stack_of(inst, b)
                    if inst == "sa":
                        pe.wait_ge(S(f"k_stacked{b % 2}_{i // 8}"), 32 * (b // 2 + 1))
                        hp, par = heads(i)
                        r = 64 * par
                        for t in range(T):
                            o = claim(pe, (st, b, t))
                            nc.tensor.matmul(o, q_stack[b % 2][r:r + 3 * HD, hp, t * 128:t * 128 + 128],
                                             ks[r:r + 3 * HD, hp, :], start=True, stop=True,
                                             tile_position=(r, 0)).then_inc(done((st, b, t)), 1)
                    else:
                        pe.wait_ge(S(f"kc_stacked{b % 2}"), 32 * kc_count(inst, b))
                        pe.wait_ge(S(f"q_cleared{b % 2}"), 32 * kc_count(inst, b))
                        for g in range(2):
                            o = claim(pe, (st, b, g))
                            for slot, first, n in ((3, 2, 2), (0, 0, 2), (1, 1, 2), (2, 2, 1)):
                                mm = nc.tensor.matmul(o[:, first * 2 * NK:(first + n) * 2 * NK],
                                                      q_stack[b % 2][:, 4 * g + slot, i * 128:i * 128 + 128],
                                                      ks[:, 4 * g + first:4 * g + first + n, :],
                                                      start=True, stop=True)
                            mm.then_inc(done((st, b, g)), 1)
                elif name == "neg":
                    inst, g = rest[0], int(rest[1])
                    n = 8 if inst == "sa" else 16
                    o = claim(pe, (st, b))
                    drained(pe, (f"max:sa:{g * 8 + 7}", b, T - 1) if inst == "sa" else (f"max:{inst}:{T - 1}", b, 1))
                    for t in range(T):
                        mm = nc.tensor.transpose(o[0:n, t * 128:t * 128 + 128], negmax[b % 2][:, t, g * 8:g * 8 + n],
                                                 ident[:])
                    mm.then_inc(done((st, b)), 1)
                elif name == "exp":
                    inst, qd, kt = rest[0], int(rest[1]), int(rest[2])
                    ks = stack_of(inst, b)
                    g = qd // 2 if inst == "sa" else 0
                    pe.wait_ge(S(f"neg_stacked{b % 2}_{g}"), neg_total[inst, b, g])
                    for j in range(4 if inst == "sa" else 2):
                        o = claim(pe, (st, b, j))
                        if inst == "sa":
                            hp, r = 2 * qd + j // 2, 64 * (j % 2)
                            nc.tensor.matmul(o, ks[r:r + 3 * HD + 2, hp, kt * 128:kt * 128 + 128],
                                             q_stack[b % 2][r:r + 3 * HD + 2, hp, :], start=True, stop=True,
                                             tile_position=(r, 0)).then_inc(done((st, b, j)), 1)
                        else:
                            nc.tensor.matmul(o, ks[:, 2 * qd + j, :], q_stack[b % 2][:, 2 * qd + j, :],
                                             start=True, stop=True).then_inc(done((st, b, j)), 1)
                elif name == "val":
                    inst, qd, kt = rest[0], int(rest[1]), int(rest[2])
                    unit = (f"exp:{inst}:{qd}:{kt}", b)
                    first, n, last = units[unit]
                    pv = ("pv", inst, b, qd)
                    if kt == 0:
                        claim(pe, pv)
                        if qd == 0:
                            pe.wait_ge(S("pool_set"), 4)
                            if inst == "sa":
                                pe.wait_ge(S(f"v_ones_set{b % 2}"), 1)
                            for key in ([("v:sa", b, t2) for t2 in range(T // 2)] if inst == "sa" else
                                        [(f"ctxk:{inst}", b, "V")]):
                                drained(pe, key)
                    drained(pe, (*unit, n - 1))
                    for j in range(4):
                        h = 4 * qd + j
                        if inst == "sa":
                            r, lhs, rhs = 0, vx[b % 2][:, kt, h * VS:h * VS + VW], probs[:, (first + j) % NP, :]
                        else:
                            r = NK * (j % 2)
                            lhs = vc[b % 2][r:r + NK, h * VS:h * VS + VW]
                            rhs = probs[r:r + NK, (first + j // 2) % NP, :]
                        mm = nc.tensor.matmul(bank(pv)[VW * j:VW * j + VW, :], lhs, rhs, start=(kt == 0), stop=last,
                                              tile_position=(r, VW * j))
                    mm.then_inc(done(pv) if last else S("probs_used"), 1)
                elif name == "out1":
                    inst = rest[0]
                    for t in range(T):
                        o = claim(pe, (st, b, t))
                        for qd in range(4):
                            drained(pe, ("pv", inst, b, qd))
                            mm = nc.tensor.transpose(o[:, qd * 128:qd * 128 + 128],
                                                     o_raw[:, qd, t * 128:t * 128 + 128], ident[:])
                        mm.then_inc(done((st, b, t)), 1)
                elif name == "out2":
                    inst = rest[0]
                    for t in range(T):
                        drained(pe, (f"out1:{inst}", b, t))
                    for f in range(F):
                        o = claim(pe, (st, b, f))
                        for t in range(T):
                            mm = nc.tensor.transpose(o[:, t * 128:t * 128 + 128],
                                                     rowz[b % 2][:, t, f * 128:f * 128 + 128], ident[:])
                        mm.then_inc(done((st, b, f)), 1)
                elif name == "out3":
                    inst = rest[0]
                    w = PROJ[inst]
                    wait_weights(w)
                    for f in range(F):
                        drained(pe, (f"out2:{inst}", b, f))
                    for t2 in range(T // 2):
                        o = claim(pe, (st, b, t2))
                        for i in range(2):
                            pairs = []
                            for kt in range(F):
                                pairs += passes(parts(b, kt, (2 * t2 + i) * 128, 128), weights(w, kt, 0, D))
                            mm = product(o[:, i * D:i * D + D], pairs, False)
                        mm.then_inc(done((st, b, t2)), 1)
                elif name in ("mlp0", "mlp1"):
                    m = int(rest[0])
                    wu, ln = ("w1", "a3") if name == "mlp0" else ("ff1", "b3")
                    wait_weights(wu)
                    pe.wait_ge(S(f"{ln}_loT"), F * (ln_index[ln, b] + 1))
                    for kind in ("h",) if name == "mlp0" else ("g", "h"):
                        a = m * 128 + (HID if kind == "g" else 0)
                        o = claim(pe, (st, b, kind))
                        pairs = []
                        for kt in range(F):
                            pairs += passes(parts(b, kt, 0, R), weights(wu, kt, a, 128))
                        product(o, pairs, True).then_inc(done((st, b, kind)), 1)
                elif name in ("down0", "down1"):
                    m = int(rest[0])
                    mlp, wd = (("mlp0", "w2"), ("mlp1", "ff2"))[int(name[-1])]
                    if m == 0:
                        for t2 in range(T // 2):
                            claim(pe, (mlp, "acc", b, t2))
                        wait_weights(wd)
                    u = mlp_index[(f"{mlp}:{m}", b)]
                    pe.wait_ge(S("hid_lo"), u + 1)
                    hp_ = (hid_hi[:, u % 2, :], hid_lo[:, u % 2, :])
                    for t in range(T):
                        o = bank((mlp, "acc", b, t // 2))[:, (t % 2) * D:(t % 2) * D + D]
                        ps_ = passes(tuple(p_[:, t * 128:t * 128 + 128] for p_ in hp_), weights(wd, m, 0, D))
                        for i, (a_, w_) in enumerate(ps_):
                            mm = nc.tensor.matmul(o, a_, w_, start=(m == 0 and i == 0 and t % 2 == 0),
                                                  stop=(m == M - 1 and i == len(ps_) - 1), skip_group_check=True)
                        if m == M - 1 and t % 2 == 1:
                            mm.then_inc(done((mlp, "acc", b, t // 2)), 1)

        @block.scalar
        def _(act):
            def split0(i):
                w = list(W0)[i]
                o, m_ = OFF0[w], W0[w][0] * W0[w][1]
                act.wait_ge(S(f"raw0_{w}_loaded"), 16)
                nc.scalar.copy(split_to(w, 0), raw0[:, o:o + m_]).then_inc(S("w0_hi"), 1)

            split0(0)
            act.wait_ge(S("vectors_loaded"), 16)
            for st, b in ORDER:
                name, *rest = st.split(":")
                if name == "ctx":
                    n = ctx_index[(st, b)]
                    o = filled(act, (st, b))
                    if n:
                        pst, pb = ctx_list[n - 1]
                        filled(act, (pst.replace("ctx", "ctxk"), pb, "V"))
                    for kt in range(2):
                        src = o[0:CK, kt * 128:kt * 128 + 128]
                        if rest[0] == "xa":
                            ins = nc.scalar.activation(ctx_full[:, kt, :], src, ACT.Identity,
                                                       bias=col("a2_b", kt, CK), scale=col("a2_g", kt, CK))
                        else:
                            ins = nc.scalar.copy(ctx_full[:, kt, :], src)
                    ins.then_inc(release((st, b)), 1)
                    drained(act, (st, b))
                    nc.scalar.copy(ctx_hi[b % 2][:], ctx_full[:]).then_inc(S("ctx_hi"), 1)
                elif name == "ctxk":
                    inst = rest[0]
                    n = ctx_index[(f"ctx:{inst}", b)]
                    o = filled(act, (st, b, "K"))
                    if n:
                        act.wait_ge(S("kc_sent"), 64 * n)
                    nc.scalar.copy(kc_parts[:, 0, :], o[:, 0:2 * NK]).then_inc(S("kc_hi"), 1)
                    o = filled(act, (st, b, "V"))
                    before = kc_user(b, inst)
                    if before:
                        last_use(act, *before)
                    else:
                        act.wait_ge(S("pool_set"), 2)
                    v_ = vc[b % 2][:, 0:H * VS].rearrange("p (h e) -> p h e", e=VS)[:, :, 0:HD]
                    src = o[:, 0:D].rearrange("p (h d) -> p h d", d=HD)
                    if inst == "xa":
                        nc.scalar.copy(v_, src).then_inc(release((st, b, "V")), 1)
                    else:
                        nc.scalar.mul(v_, src, delta("v2")).then_inc(release((st, b, "V")), 1)
                    if (inst, b) in (("xa", 0), ("xa", 1)):
                        for i in ((1, 2), (3, 4))[b]:
                            split0(i)
                elif name == "lt":
                    inst = rest[0]
                    for f in range(F):
                        o = filled(act, (st, b, f))
                        nc.scalar.activation(full_t[b % 2][:, f, :], o, ACT.Identity, bias=col(f"{inst}_b", f),
                                             scale=col(f"{inst}_g", f)).then_inc(release((st, b, f)), 1)
                        drained(act, (st, b, f))
                        nc.scalar.copy(hiT[b % 2][:, f, :], full_t[b % 2][:, f, :]).then_inc(S(f"{inst}_hiT"), 1)
                elif name in ("q", "k"):
                    i = qk_index[(st, b)]
                    for m in range(F):
                        o = filled(act, (st, b, m))
                        if i:
                            act.wait_ge(S(f"qk_sent{m}"), 32 * i)
                        if st in q_scaled:
                            nc.scalar.mul(qk_parts[:, m, 0, :], o, prods[:, q_scaled[st]:q_scaled[st] + 1]).then_inc(
                                S("qk_hi"), 1)
                        else:
                            nc.scalar.copy(qk_parts[:, m, 0, :], o).then_inc(S("qk_hi"), 1)
                elif name == "v":
                    if b >= 2:
                        last_use(act, "sa", b - 2)
                    else:
                        act.wait_ge(S(f"v_ones_set{b}"), 1)
                    for t2 in range(T // 2):
                        o = filled(act, (st, b, t2))
                        nc.scalar.mul(vx[b % 2][:, 2 * t2:2 * t2 + 2, 0:H * VS].rearrange(
                                          "p t (h e) -> p t h e", e=VS)[:, :, :, 0:HD],
                                      o.rearrange("p (t h d) -> p t h d", t=2, d=HD),
                                      delta("v1")).then_inc(release((st, b, t2)), 1)
                elif name == "neg":
                    n = 8 if rest[0] == "sa" else 16
                    i = neg_index[(st, b)]
                    o = filled(act, (st, b))
                    if i:
                        act.wait_ge(S("neg_sent"), 16 * i)
                    nc.scalar.copy(neg_parts[0:n, 0, :], o[0:n, :]).then_inc(S("neg_hi"), 1)
                elif name == "exp":
                    first, n, _last = units[(st, b)]
                    if first == 0:
                        act.wait_ge(S("w0_split"), len(W0))
                    for j in range(n):
                        tile = first + j
                        o = filled(act, (st, b, j))
                        if tile >= NP:
                            u = tile_unit[tile - NP]
                            if units[u][2]:
                                last_of = u[0].split(":")
                                filled(act, ("pv", last_of[1], u[1], int(last_of[2])))
                            else:
                                act.wait_ge(S("probs_used"), quad_used[u])
                        nc.scalar.activation(probs[:, tile % NP, :], o, ACT.Exp, scale=SCALE).then_inc(
                            release((st, b, j)), 1)
                elif name == "val":
                    inst, qd, kt = rest[0], int(rest[1]), int(rest[2])
                    if units[(f"exp:{inst}:{qd}:{kt}", b)][2]:
                        o = filled(act, ("pv", inst, b, qd))
                        nc.scalar.copy(o_raw[:, qd, :], o).then_inc(release(("pv", inst, b, qd)), 1)
                elif name == "out2":
                    for f in range(F):
                        o = filled(act, (st, b, f))
                        nc.scalar.copy(hiT[b % 2][:, f, :], o).then_inc(S("o_hiT"), 1)
                elif name in ("mlp0", "mlp1"):
                    m = int(rest[0])
                    u = mlp_index[(st, b)]
                    s_ = u % 2
                    if name == "mlp0":
                        o = filled(act, (st, b, "h"))
                        nc.scalar.activation(hid[:, s_, :], o, ACT.Gelu, bias=col("mlp0_b", m)).then_inc(
                            release((st, b, "h")), 1)
                    else:
                        o = filled(act, (st, b, "g"))
                        if m >= 2:
                            drained(act, (*mlp_list[u - 2], "h"))
                        nc.scalar.activation(gate[:, s_, :], o, ACT.Gelu_apprx_tanh,
                                             bias=col("ff1_b", M + m), scale=delta("ff1")).then_inc(
                            release((st, b, "g")), 1)
                elif name in ("low0", "low1"):
                    key = (f"mlp{name[-1]}:{rest[0]}", b)
                    s_ = mlp_index[key] % 2
                    drained(act, (*key, "h"))
                    nc.scalar.copy(hid_hi[:, s_, :], hid[:, s_, :]).then_inc(S("hid_hi"), 1)

        @block.vector
        def _(dve):
            def split0(i):
                w = list(W0)[i]
                o, m_ = OFF0[w], W0[w][0] * W0[w][1]
                dve.wait_ge(S("w0_hi"), i + 1)
                nc.vector.tensor_tensor(split_to(w, 1), raw0[:, o:o + m_], split_to(w, 0),
                                        ALU.subtract).then_inc(S("w0_split"), 1)

            for i in range(2):
                nc.vector.memset(kc_stack[i][:].bitcast(F32), 0.0).then_inc(S("kc_zero"), 1)
                dve.wait_ge(S("kc_zero"), i + 1)
                for par in range(2):
                    nc.vector.memset(kc_stack[i][64 * par + 32:64 * par + 64, :, par * NK:par * NK + NK].bitcast(F32),
                                     1.0).then_inc(S("kc_set"), 1)
            steps = [0]
            nc.vector.memset(ext[:], -3.0e38).then_inc(S("ext_set"), 1)
            split0(0)
            for st, b in ORDER:
                name, *rest = st.split(":")
                if name == "ctxz":
                    i = z_index[(st, b)]
                    cr = ctx_rows[b]
                    dve.wait_ge(S(f"ctx_loaded{b}"), 32)
                    nc.vector.bn_stats(six[b % 2][:, 0, :], cr[:]).then_inc(S("ctx_six"), 1)
                    dve.wait_ge(S("ctx_six"), i + 1)
                    nc.vector.bn_aggr(meanvar[b % 2][:, 0, :], six[b % 2][:, 0, :]).then_inc(S("ctx_mean"), 1)
                    dve.wait_ge(S("ctx_rstd"), i + 1)
                    nc.vector.tensor_scalar(ctx_z[b % 2][:], cr[:], meanvar[b % 2][:, 0, 0:1], rstd[b % 2][:, 0:1],
                                            ALU.subtract, ALU.mult).then_inc(S("ctx_z"), 1)
                elif name == "ctx":
                    dve.wait_ge(S("ctx_hi"), ctx_index[(st, b)] + 1)
                    nc.vector.tensor_tensor(ctx_lo[:], ctx_full[:], ctx_hi[b % 2][:], ALU.subtract).then_inc(S("ctx_lo"), 1)
                elif name == "ctxk":
                    dve.wait_ge(S("kc_hi"), ctx_index[(f"ctx:{rest[0]}", b)] + 1)
                    o = filled(dve, (st, b, "K"))
                    nc.vector.tensor_tensor(kc_parts[:, 1, :], o[:, 0:2 * NK], kc_parts[:, 0, :],
                                            ALU.subtract).then_inc(release((st, b, "K")), 1)
                    filled(dve, (st, b, "V"))
                    if (rest[0], b) in (("xa", 0), ("xa", 1)):
                        for i in ((1, 2), (3, 4))[b]:
                            split0(i)
                elif name == "ln":
                    inst = rest[0]
                    i = ln_index[inst, b]
                    xb = xs[b % 2]
                    if inst in ("a1", "b1"):
                        dve.wait_ge(S(f"x_loaded{b % 2}"), 16 * ((0 if inst == "a1" else 2) + b // 2 + 1))
                    else:
                        att = {"a3": "xa", "b2": "sa", "b3": "xb"}[inst]
                        for t2 in range(T // 2):
                            drained(dve, (f"out3:{att}", b, t2))
                    for t in range(T):
                        nc.vector.bn_stats(six[b % 2][:, t, :], xb[:, t, :]).then_inc(S(f"{inst}_six"), 1)
                    for t in range(T):
                        dve.wait_ge(S(f"{inst}_six"), T * i + t + 1)
                        nc.vector.bn_aggr(meanvar[b % 2][:, t, :], six[b % 2][:, t, :]).then_inc(
                            S(f"{inst}_mean"), 1)
                elif name == "lz":
                    inst = rest[0]
                    i = ln_index[inst, b]
                    xb = xs[b % 2]
                    dve.wait_ge(S(f"{inst}_rstd"), i + 1)
                    for t in range(T):
                        nc.vector.tensor_scalar(rowz[b % 2][:, t, :], xb[:, t, :], meanvar[b % 2][:, t, 0:1],
                                                rstd[b % 2][:, t:t + 1], ALU.subtract, ALU.mult).then_inc(
                            S(f"{inst}_rowz"), 1)
                elif name == "ll":
                    inst = rest[0]
                    for f in range(F):
                        dve.wait_ge(S(f"{inst}_hiT"), F * ln_index[inst, b] + f + 1)
                        nc.vector.tensor_tensor(loT[b % 2][:, f, :], full_t[b % 2][:, f, :], hiT[b % 2][:, f, :],
                                                ALU.subtract).then_inc(S(f"{inst}_loT"), 1)
                elif name in ("ql", "kl"):
                    st = f"{name[0]}:{rest[0]}"
                    i = qk_index[(st, b)]
                    for m in range(F):
                        dve.wait_ge(S("qk_hi"), F * i + m + 1)
                        o = filled(dve, (st, b, m))
                        hi_ = qk_parts[:, m, 0, :]
                        if st in q_scaled:
                            ins = nc.vector.scalar_tensor_tensor(
                                out=qk_parts[:, m, 1, :], in0=o, scalar=prods[:, q_scaled[st]:q_scaled[st] + 1],
                                in1=hi_, op0=ALU.mult, op1=ALU.subtract)
                        else:
                            ins = nc.vector.tensor_tensor(qk_parts[:, m, 1, :], o, hi_, ALU.subtract)
                        ins.then_inc(release((st, b, m)), 1)
                elif name == "max":
                    i = int(rest[1])
                    nm = negmax[b % 2]
                    if rest[0] == "sa":
                        hp, par = heads(i)
                        c = hp // 4 * 8 + par * 4 + hp % 4
                        for t in range(T):
                            o = filled(dve, (st, b, t))
                            nc.vector.tensor_reduce(nm[:, t, c:c + 1], o, AX.X, ALU.max, negate=True).then_inc(
                                release((st, b, t)), 1)
                    else:
                        by_slot = nm[:, i, :].rearrange("p (par hp) -> p hp par", par=2)
                        for g in range(2):
                            o = filled(dve, (st, b, g))
                            nc.vector.tensor_reduce(by_slot[:, 4 * g:4 * g + 4, :],
                                                    o.rearrange("p (hp par k) -> p hp par k", par=2, k=NK), AX.X,
                                                    ALU.max, negate=True).then_inc(release((st, b, g)), 1)
                elif name == "nl":
                    st = f"neg:{rest[0]}:{rest[1]}"
                    n = 8 if rest[0] == "sa" else 16
                    dve.wait_ge(S("neg_hi"), neg_index[(st, b)] + 1)
                    o = filled(dve, (st, b))
                    nc.vector.tensor_tensor(neg_parts[0:n, 1, :], o[0:n, :], neg_parts[0:n, 0, :],
                                            ALU.subtract).then_inc(release((st, b)), 1)
                elif name == "out1":
                    for t in range(T):
                        o = filled(dve, (st, b, t)).rearrange("p (h e) -> p h e", e=VW)
                        n = out_index[(st, b)] * T + t
                        if n:
                            pst, pb = (st, b) if t else out_list[out_index[(st, b)] - 1]
                            drained(dve, (pst, pb, (t - 1) % T))
                        nc.vector.reciprocal(rsum[:], o[:, :, HD]).then_inc(S("rsum"), 1)
                        dve.wait_ge(S("rsum"), n + 1)
                        nc.vector.tensor_tensor(rowz[b % 2][:, t, :].rearrange("p (h d) -> p h d", d=HD),
                                                o[:, :, 0:HD], rsum[:].unsqueeze(2).broadcast_to([128, H, HD]),
                                                ALU.mult).then_inc(release((st, b, t)), 1)
                elif name == "ol":
                    st = f"out2:{rest[0]}"
                    n = out_index[(st.replace("out2", "out1"), b)]
                    for f in range(F):
                        dve.wait_ge(S("o_hiT"), F * n + f + 1)
                        o = filled(dve, (st, b, f))
                        nc.vector.tensor_tensor(loT[b % 2][:, f, :], o, hiT[b % 2][:, f, :], ALU.subtract).then_inc(
                            release((st, b, f)), 1)
                elif name == "out3":
                    inst = rest[0]
                    ln = LN_OF[inst]
                    dve.wait_ge(S(f"{ln}_biased"), T * (ln_index[ln, b] + 1))
                    for t2 in range(T // 2):
                        o = filled(dve, (st, b, t2)).rearrange("p (t d) -> p t d", t=2)
                        x2 = xs[b % 2][:, 2 * t2:2 * t2 + 2, :]
                        if inst == "xa":
                            ins = nc.vector.tensor_tensor(x2, o, x2, ALU.add)
                        else:
                            ins = nc.vector.scalar_tensor_tensor(out=x2, in0=o, scalar=delta(PROJ[inst]), in1=x2,
                                                                 op0=ALU.mult, op1=ALU.add)
                        ins.then_inc(release((st, b, t2)), 1)
                elif name == "mlp1":
                    m = int(rest[0])
                    s_ = mlp_index[(st, b)] % 2
                    o = filled(dve, (st, b, "h"))
                    drained(dve, (st, b, "g"))
                    nc.vector.scalar_tensor_tensor(out=hid[:, s_, :], in0=o, scalar=ffb[:, m:m + 1],
                                                   in1=gate[:, s_, :], op0=ALU.add, op1=ALU.mult).then_inc(
                        release((st, b, "h")), 1)
                elif name in ("low0", "low1"):
                    u = mlp_index[(f"mlp{name[-1]}:{rest[0]}", b)]
                    s_ = u % 2
                    dve.wait_ge(S("hid_hi"), u + 1)
                    nc.vector.tensor_tensor(hid_lo[:, s_, :], hid[:, s_, :], hid_hi[:, s_, :],
                                            ALU.subtract).then_inc(S("hid_lo"), 1)
                elif name in ("down0", "down1") and int(rest[0]) == M - 1:
                    mlp, ln = (("mlp0", "a3"), ("mlp1", "b3"))[int(name[-1])]
                    dve.wait_ge(S(f"{ln}_biased"), T * (ln_index[ln, b] + 1))
                    for t2 in range(T // 2):
                        o = filled(dve, (mlp, "acc", b, t2)).rearrange("p (t d) -> p t d", t=2)
                        x2 = xs[b % 2][:, 2 * t2:2 * t2 + 2, :]
                        if mlp == "mlp0":
                            ins = nc.vector.tensor_tensor(x2, o, x2, ALU.add)
                        else:
                            ins = nc.vector.scalar_tensor_tensor(out=x2, in0=o, scalar=prods[:, 2:3], in1=x2,
                                                                 op0=ALU.mult, op1=ALU.add)
                        ins.then_inc(release((mlp, "acc", b, t2)), 1)
                elif name == "stats":
                    i, a, n = CHUNKS[b]
                    p_ = CK if QN[i] in ("k2", "v2") else 128
                    raw = raw1_of(i)[0][0:p_, a:a + n]
                    dve.wait_ge(S(f"raw1_{QN[i]}_loaded"), 16)
                    nc.vector.tensor_reduce(ext[0:p_, b:b + 1], raw, AX.X, ALU.max).then_inc(S("extremes"), 1)
                    nc.vector.tensor_reduce(ext[0:p_, NCH + b:NCH + b + 1], raw, AX.X, ALU.min,
                                            negate=True).then_inc(S("extremes"), 1)
                elif name == "scalars":
                    dve.wait_ge(S("extremes_all"), b + 1)
                    lo_, hi_ = ((0, QSMALL), (QSMALL, NQ))[b]
                    def step(ins):
                        ins.then_inc(S("scalar_step"), 1)
                        steps[0] += 1
                        dve.wait_ge(S("scalar_step"), steps[0])

                    mx, nmn = allext[:, 0:QSMALL], allext[:, NCH:NCH + QSMALL]
                    if b:
                        at_ = QSMALL
                        for i in range(QSMALL, NQ):
                            n = sum(c_[0] == i for c_ in CHUNKS)
                            src = allext[:].rearrange("p (k c) -> p k c", k=2)[:, :, at_:at_ + n]
                            step(nc.vector.tensor_reduce(ffext[:, :, i - QSMALL], src, AX.X, ALU.max))
                            at_ += n
                        mx, nmn = ffext[:, 0, :], ffext[:, 1, :]
                    dl, inv, span, low, high, t0, t1, zp = (qs[:, i, lo_:hi_] for i in range(8))
                    qh = qhi[:, lo_:hi_]
                    step(nc.vector.tensor_tensor(span, mx, nmn, ALU.add))
                    step(nc.vector.tensor_scalar(t0, span, 1.0 / LEVELS, None, ALU.mult))
                    step(nc.vector.tensor_copy(qh, t0))
                    step(nc.vector.tensor_tensor(t1, t0, qh, ALU.subtract))
                    step(nc.vector.scalar_tensor_tensor(out=zp, in0=qh, scalar=-LEVELS, in1=span, op0=ALU.mult,
                                                        op1=ALU.add))
                    step(nc.vector.scalar_tensor_tensor(out=low, in0=t1, scalar=-LEVELS, in1=zp, op0=ALU.mult,
                                                        op1=ALU.add))
                    step(nc.vector.scalar_tensor_tensor(out=dl, in0=low, scalar=1.0 / LEVELS, in1=t0, op0=ALU.mult,
                                                        op1=ALU.add))
                    step(nc.vector.reciprocal(inv, dl))
                    step(nc.vector.tensor_tensor(t0, nmn, inv, ALU.mult))
                    step(nc.vector.tensor_scalar(t1, t0, MAGIC, None, ALU.add))
                    step(nc.vector.tensor_scalar(zp, t1, -MAGIC, None, ALU.add))
                    step(nc.vector.tensor_scalar(low, zp, -1.0, MAGIC, ALU.mult, ALU.add))
                    step(nc.vector.tensor_scalar(high, low, LEVELS, None, ALU.add))
                    for i, (a_, c_) in enumerate((("q1", "k1"), ("q2", "k2"), ("ff1", "ff2"))):
                        if (i == 2) == (b == 1):
                            step(nc.vector.tensor_tensor(prods[:, i:i + 1], delta(a_), delta(c_), ALU.mult))
                    if b == 0:
                        nc.vector.tensor_copy(ffb[:], vec[:, OFFV["ff1_b"]:OFFV["ff1_b"] + M]).then_inc(
                            S("quant_scalars"), 1)
                    else:
                        i = QN.index("ff1")
                        dve.wait_ge(S("quant_scalars"), 1)
                        nc.vector.tensor_scalar(ffb[:], vec[:, OFFV["ff1_b"]:OFFV["ff1_b"] + M], qs[:, 1, i:i + 1],
                                                None, ALU.mult).then_inc(S("quant_scalars"), 1)


_VECTORS = {"a1_g": "L0_xattn_ln1_w", "a1_b": "L0_xattn_ln1_b", "a2_g": "L0_xattn_ln2_w", "a2_b": "L0_xattn_ln2_b",
            "a3_g": "L0_xattn_ln3_w", "a3_b": "L0_xattn_ln3_b", "b1_g": "L1_xattn_ln1_g", "b1_b": "L1_xattn_ln1_b",
            "b2_g": "L1_xattn_ln2_g", "b2_b": "L1_xattn_ln2_b", "b3_g": "L1_xattn_ln3_g", "b3_b": "L1_xattn_ln3_b",
            "mlp0_b": "L0_xattn_b1", "ff1_b": "L1_xattn_ff1_b"}


def kernel(**inputs):
    import numpy as _np
    import concourse.bacc as _bacc
    from concourse import mybir as _mybir
    from concourse.bass_utils import run_bass_kernel_spmd as _run

    a = {k: _np.asarray(v) for k, v in inputs.items()}

    def pack(weights, widths):
        cols = []
        for name, w in weights.items():
            tiles, n = widths[name]
            rows_ = w.shape[0] // tiles
            tile = _np.zeros((128, tiles, n), w.dtype)
            tile[:rows_] = w.reshape(tiles, rows_, n).transpose(1, 0, 2)
            cols.append(tile.reshape(128, tiles * n))
        return _np.ascontiguousarray(_np.concatenate(cols, axis=1))

    w0 = pack({"kv": a["L0_xattn_Wkv"], "q": a["L0_xattn_Wq"], "proj": a["L0_xattn_Wproj"], "w1": a["L0_xattn_W1"],
               "w2": a["L0_xattn_W2"]}, W0)
    w1 = pack({n: a[f"L1_xattn_{n}_w"].T for n in W1}, W1)
    vec = _np.zeros((128, NV), w0.dtype)
    for name, n in VEC.items():
        v = a[_VECTORS[name]].reshape(n, -1).T
        vec[:v.shape[0], OFFV[name]:OFFV[name] + n] = v
    rows = _np.stack([a["L0_xattn_bproj"], a["L0_xattn_b2"], a["L1_xattn_o1_b"], a["L1_xattn_o2_b"],
                      a["L1_xattn_ff2_b"]])
    arrays = {"x": a["x"], "ctx": a["ctx_768"], "w0": w0, "w1": w1, "vec": vec, "rows": rows}
    arrays = {f"in_{k}_dram": _np.ascontiguousarray(v) for k, v in arrays.items()}

    nc = _bacc.Bacc("TRN2", target_bir_lowering=False, num_devices=1)
    args = [nc.dram_tensor(k, v.shape, _mybir.dt.from_np(v.dtype), kind="ExternalInput").ap()
            for k, v in arrays.items()]
    o = nc.dram_tensor("out_0_dram", (B, R, D), _mybir.dt.float32, kind="ExternalOutput").ap()
    program(nc, *args, o)
    r = _run(nc, [arrays], core_ids=[0])
    return r.results[0]["out_0_dram"]
```
